# Optimizing a Trainium2 kernel written in Bass

```python
import numpy as np
import jax
import jax.numpy as jnp

def _softmax(x, axis=-1):
    return jax.nn.softmax(x, axis=axis)

def _gelu(x):
    return jax.nn.gelu(x, approximate=True)

def _silu(x):
    return jax.nn.silu(x)

def _sigmoid(x):
    return jax.nn.sigmoid(x)

def _layernorm(x, axis=-1, eps=1e-05):
    m = jnp.mean(x, axis=axis, keepdims=True)
    v = jnp.var(x, axis=axis, keepdims=True)
    return (x - m) / jnp.sqrt(v + eps)

def _scatter_add(tgt, idx, src, axis=0):
    return tgt.at[idx].add(src)

def _segment_sum(src, seg, n):
    return jax.ops.segment_sum(src, seg, n)
kernel_name = 'mk_xattn_seq_d4_seqx_r4_9c9aa0'

def setup_inputs(seed: int=0):
    np.random.seed(seed)
    _w = jnp.asarray

    def _rec_inputs():
        import jax
        import jax.numpy as jnp
        _rk = jax.random.key(seed)
        x = -0.0005146 + 1 * jax.random.normal(jax.random.fold_in(_rk, 1), (8, 100, 512), jnp.float32)
        _lenS = 100 - jax.random.randint(jax.random.fold_in(_rk, 7), (8,), 0, max(1, 100 // 4) + 1, jnp.int32)
        _lenS2 = 361 - jax.random.randint(jax.random.fold_in(_rk, 8), (8,), 0, max(1, 361 // 4) + 1, jnp.int32)
        _ctx_2048P = jax.random.normal(jax.random.fold_in(_rk, 11), (8, 16, 512), jnp.float32)
        _ctx_2048c = jax.random.dirichlet(jax.random.fold_in(_rk, 511), 0.3 * jnp.ones((16,), jnp.float32), (8, 361))
        _ctx_2048t = jnp.einsum('bsk,bkd->bsd', _ctx_2048c, _ctx_2048P)
        _ctx_2048t = _ctx_2048t * jax.lax.rsqrt(jnp.mean(jnp.square(_ctx_2048t)) + 1e-12) * 0.953939
        ctx_2048 = -0.000392918 + 0.999932 * (_ctx_2048t + 0.3 * jax.random.normal(jax.random.fold_in(_rk, 611), (8, 361, 512), jnp.float32))
        _validS = jnp.arange(100)[None, :] < _lenS[:, None]
        _validS2 = jnp.arange(361)[None, :] < _lenS2[:, None]
        _causal = jnp.tril(jnp.ones((100, 100), dtype=bool))
        mask_BxS2_ik0 = jnp.where(jnp.broadcast_to(_validS2[:, :], (8, 361)), 0, 1).astype(jnp.int32)
        mask_Bx1xSxS2_ff0 = jnp.where(jnp.ones((8, 1, 100, 361), dtype=bool), 0.0, -1000000000.0).astype(jnp.float32)
        return (x, ctx_2048, mask_BxS2_ik0, mask_Bx1xSxS2_ff0)
    x, ctx_2048, mask_BxS2_ik0, mask_Bx1xSxS2_ff0 = _rec_inputs()

    def _L0_xattn_setup():
        import jax, jax.numpy as jnp
        import numpy as np
        B, P, K, H, NH = (4, 512, 64, 512, 16)
        DH = H // NH
        EPS = 1e-06

        def rmsnorm(x, w):
            var = jnp.mean(jnp.square(x), axis=-1, keepdims=True)
            return x * jax.lax.rsqrt(var + EPS) * w
        key = jax.random.key(seed)
        ks = jax.random.split(key, 12)
        s = 0.02
        return {'x': jax.random.normal(ks[0], (B, P, H), jnp.float32), 'latents': jax.random.normal(ks[1], (B, K, H), jnp.float32), 'attention_mask': jax.random.randint(ks[2], (B, P), 0, 2, jnp.int32), 'q_w': s * jax.random.normal(ks[3], (H, H), jnp.float32), 'q_b': jnp.zeros((H,), jnp.float32), 'kv_w': s * jax.random.normal(ks[4], (H, 2 * H), jnp.float32), 'kv_b': jnp.zeros((2 * H,), jnp.float32), 'out_w': s * jax.random.normal(ks[5], (H, H), jnp.float32), 'out_b': jnp.zeros((H,), jnp.float32), 'postnorm_w': jnp.ones((H,), jnp.float32), 'mlp_w1': s * jax.random.normal(ks[6], (H, 4 * H), jnp.float32), 'mlp_b1': jnp.zeros((4 * H,), jnp.float32), 'mlp_w2': s * jax.random.normal(ks[7], (4 * H, H), jnp.float32), 'mlp_b2': jnp.zeros((H,), jnp.float32)}
    _L0_xattn_all = _L0_xattn_setup()
    _L0_xattn_in = {k: v for k, v in _L0_xattn_all.items() if k in ('q_w', 'q_b', 'kv_w', 'kv_b', 'out_w', 'out_b', 'postnorm_w', 'mlp_w1', 'mlp_b1', 'mlp_w2', 'mlp_b2')}
    del _L0_xattn_all

    def _L1_xattn_setup():
        import jax, jax.numpy as jnp
        import numpy as np
        N_HEAD = 32
        EPS = 1e-05

        def _ln(x, w, b):
            m = jnp.mean(x, axis=-1, keepdims=True)
            v = jnp.mean((x - m) ** 2, axis=-1, keepdims=True)
            return (x - m) * jax.lax.rsqrt(v + EPS) * w + b

        def _forward(x, state, i, ln1_w, ln1_b, ln2_w, ln2_b, maa_x, maa_w, maa_k, maa_v, maa_r, maa_g, maa_w1, maa_w2, time_decay, decay_w1, decay_w2, faaaa, Wr, Wk, Wv, Wg, Wo, gn_w, gn_b, fmaa_k, fmaa_r, fWk, fWr, fWv):
            B, L, C = x.shape
            H = N_HEAD
            S = C // H
            i0 = (2 + S) * i
            xa = _ln(x, ln1_w, ln1_b)
            sx = jnp.concatenate([state[:, i0 + 1][:, None], xa[:, :-1]], axis=1) - xa
            xxx = xa + sx * maa_x
            t = jnp.tanh(xxx @ maa_w1).reshape(B, L, 5, -1)
            m = jnp.einsum('blfd,fdc->blfc', t, maa_w2)
            mw, mk, mv, mr, mg = (m[:, :, j] for j in range(5))
            xw = xa + sx * (maa_w + mw)
            xk = xa + sx * (maa_k + mk)
            xv = xa + sx * (maa_v + mv)
            xr = xa + sx * (maa_r + mr)
            xg = xa + sx * (maa_g + mg)
            w = time_decay + jnp.tanh(xw @ decay_w1) @ decay_w2
            w = jnp.exp(-jnp.exp(w)).reshape(B, L, H, S)
            r = (xr @ Wr.T).reshape(B, L, H, S)
            k = (xk @ Wk.T).reshape(B, L, H, S)
            v = (xv @ Wv.T).reshape(B, L, H, S)
            g = jax.nn.silu(xg @ Wg.T)
            s0 = state[:, i0 + 2:i0 + 2 + S].reshape(B, H, S, S)

            def step(s, inp):
                k_l, v_l, w_l, r_l = inp
                a = k_l[..., :, None] * v_l[..., None, :]
                out = jnp.einsum('bhs,bhst->bht', r_l, faaaa * a + s)
                s_new = a + w_l[..., None] * s
                return (s_new, out)
            seq = tuple((z.transpose(1, 0, 2, 3) for z in (k, v, w, r)))
            _, outs = jax.lax.scan(step, s0, seq)
            y = outs.transpose(1, 0, 2, 3)
            gm = jnp.mean(y, axis=-1, keepdims=True)
            gv = jnp.mean((y - gm) ** 2, axis=-1, keepdims=True)
            y = ((y - gm) * jax.lax.rsqrt(gv + EPS)).reshape(B, L, C) * gn_w + gn_b
            x = x + y * g @ Wo.T
            xc = _ln(x, ln2_w, ln2_b)
            sxc = jnp.concatenate([state[:, i0][:, None], xc[:, :-1]], axis=1) - xc
            xk2 = xc + sxc * fmaa_k
            xr2 = xc + sxc * fmaa_r
            rr = jax.nn.sigmoid(xr2 @ fWr.T)
            kk = jnp.square(jax.nn.relu(xk2 @ fWk.T))
            x = x + rr * (kk @ fWv.T)
            return x
        key = jax.random.key(seed)
        B, L, C, H = (8, 128, 512, N_HEAD)
        S = C // H
        DM, DD = (32, 64)
        ks = jax.random.split(key, 32)
        n = lambda k, shp, s=1.0: jax.random.normal(k, shp, dtype=jnp.float32) * s
        u = lambda k, shp: jax.random.uniform(k, shp, dtype=jnp.float32)
        inp = {'x': n(ks[0], (B, L, C)), 'state': n(ks[1], (B, 2 + S, C), 0.1), 'i': 0, 'ln1_w': jnp.ones((C,), jnp.float32), 'ln1_b': jnp.zeros((C,), jnp.float32), 'ln2_w': jnp.ones((C,), jnp.float32), 'ln2_b': jnp.zeros((C,), jnp.float32), 'maa_x': u(ks[2], (C,)), 'maa_w': u(ks[3], (C,)), 'maa_k': u(ks[4], (C,)), 'maa_v': u(ks[5], (C,)), 'maa_r': u(ks[6], (C,)), 'maa_g': u(ks[7], (C,)), 'maa_w1': n(ks[8], (C, 5 * DM), 0.02), 'maa_w2': n(ks[9], (5, DM, C), 0.02), 'time_decay': n(ks[10], (C,), 0.5), 'decay_w1': n(ks[11], (C, DD), 0.02), 'decay_w2': n(ks[12], (DD, C), 0.02), 'faaaa': n(ks[13], (H, S, 1), 0.1), 'Wr': n(ks[14], (C, C), 0.02), 'Wk': n(ks[15], (C, C), 0.02), 'Wv': n(ks[16], (C, C), 0.02), 'Wg': n(ks[17], (C, C), 0.02), 'Wo': n(ks[18], (C, C), 0.02), 'gn_w': jnp.ones((C,), jnp.float32), 'gn_b': jnp.zeros((C,), jnp.float32), 'fmaa_k': u(ks[19], (C,)), 'fmaa_r': u(ks[20], (C,)), 'fWk': n(ks[21], (C, C), 0.02), 'fWr': n(ks[22], (C, C), 0.02), 'fWv': n(ks[23], (C, C), 0.02)}
        return inp
    _L1_xattn_all = _L1_xattn_setup()
    _L1_xattn_in = {k: v for k, v in _L1_xattn_all.items() if k in ('ln1_w', 'ln1_b', 'ln2_w', 'ln2_b', 'maa_x', 'maa_w', 'maa_k', 'maa_v', 'maa_r', 'maa_g', 'maa_w1', 'maa_w2', 'time_decay', 'decay_w1', 'decay_w2', 'faaaa', 'Wr', 'Wk', 'Wv', 'Wg', 'Wo', 'gn_w', 'gn_b', 'fmaa_k', 'fmaa_r', 'fWk', 'fWr', 'fWv')}
    del _L1_xattn_all

    def _L2_xattn_setup():
        import jax, jax.numpy as jnp
        import numpy as np
        B, Q, S1, S2 = (4, 64, 512, 512)
        D, H, K, F = (512, 16, 128, 2048)
        LN_EPS = 1e-05

        def _layer_norm(x, scale, offset):
            mu = jnp.mean(x, axis=-1, keepdims=True)
            var = jnp.var(x, axis=-1, keepdims=True)
            return (x - mu) * jax.lax.rsqrt(var + LN_EPS) * scale + offset

        def _cross_attention(q_in, kv_in, wq, bq, wk, bk, wv, bv, wo, bo, bias_k, bias_v):
            b, q_len, _ = q_in.shape
            t = kv_in.shape[1]
            qh = (q_in @ wq + bq).reshape(b, q_len, H, K)
            kh = (kv_in @ wk + bk).reshape(b, t, H, K)
            vh = (kv_in @ wv + bv).reshape(b, t, H, K)
            kh = jnp.concatenate([kh, jnp.broadcast_to(bias_k, (b, 1, H, K))], axis=1)
            vh = jnp.concatenate([vh, jnp.broadcast_to(bias_v, (b, 1, H, K))], axis=1)
            scale = jnp.sqrt(jnp.asarray(K, q_in.dtype))
            logits = jnp.einsum('bqhk,bthk->bhqt', qh, kh) / scale
            weights = jax.nn.softmax(logits, axis=-1)
            ctx = jnp.einsum('bhqt,bthk->bqhk', weights, vh).reshape(b, q_len, H * K)
            return ctx @ wo + bo

        def _forward(x, xf_1, xf_2, ln1_scale, ln1_offset, wq1, bq1, wk1, bk1, wv1, bv1, wo1, bo1, bias_k1, bias_v1, ln2_scale, ln2_offset, wq2, bq2, wk2, bk2, wv2, bv2, wo2, bo2, bias_k2, bias_v2, ln_mlp_scale, ln_mlp_offset, w_fc1, b_fc1, w_fc2, b_fc2):
            res = x
            h = _layer_norm(x, ln1_scale, ln1_offset)
            x = res + _cross_attention(h, xf_1, wq1, bq1, wk1, bk1, wv1, bv1, wo1, bo1, bias_k1, bias_v1)
            res = x
            h = _layer_norm(x, ln2_scale, ln2_offset)
            x = res + _cross_attention(h, xf_2, wq2, bq2, wk2, bk2, wv2, bv2, wo2, bo2, bias_k2, bias_v2)
            h = _layer_norm(x, ln_mlp_scale, ln_mlp_offset)
            h = jax.nn.gelu(h @ w_fc1 + b_fc1, approximate=False) @ w_fc2 + b_fc2
            return x + h
        key = jax.random.key(seed)
        ks = iter(jax.random.split(key, 64))

        def rn(shape, s=0.02):
            return jax.random.normal(next(ks), shape, jnp.float32) * s
        inp = {'x': rn((B, Q, D), 1.0), 'xf_1': rn((B, S1, D), 1.0), 'xf_2': rn((B, S2, D), 1.0)}
        for i in (1, 2):
            inp[f'ln{i}_scale'] = jnp.ones((D,), jnp.float32)
            inp[f'ln{i}_offset'] = jnp.zeros((D,), jnp.float32)
            inp[f'wq{i}'] = rn((D, H * K))
            inp[f'bq{i}'] = jnp.zeros((H * K,), jnp.float32)
            inp[f'wk{i}'] = rn((D, H * K))
            inp[f'bk{i}'] = jnp.zeros((H * K,), jnp.float32)
            inp[f'wv{i}'] = rn((D, H * K))
            inp[f'bv{i}'] = jnp.zeros((H * K,), jnp.float32)
            inp[f'wo{i}'] = rn((H * K, D))
            inp[f'bo{i}'] = jnp.zeros((D,), jnp.float32)
            inp[f'bias_k{i}'] = rn((1, 1, H, K))
            inp[f'bias_v{i}'] = rn((1, 1, H, K))
        inp['ln_mlp_scale'] = jnp.ones((D,), jnp.float32)
        inp['ln_mlp_offset'] = jnp.zeros((D,), jnp.float32)
        inp['w_fc1'] = rn((D, F))
        inp['b_fc1'] = jnp.zeros((F,), jnp.float32)
        inp['w_fc2'] = rn((F, D))
        inp['b_fc2'] = jnp.zeros((D,), jnp.float32)
        return inp
    _L2_xattn_all = _L2_xattn_setup()
    _L2_xattn_in = {k: v for k, v in _L2_xattn_all.items() if k in ('ln1_scale', 'ln1_offset', 'wq1', 'bq1', 'wk1', 'bk1', 'wv1', 'bv1', 'wo1', 'bo1', 'bias_k1', 'bias_v1', 'ln2_scale', 'ln2_offset', 'wq2', 'bq2', 'wk2', 'bk2', 'wv2', 'bv2', 'wo2', 'bo2', 'bias_k2', 'bias_v2', 'ln_mlp_scale', 'ln_mlp_offset', 'w_fc1', 'b_fc1', 'w_fc2', 'b_fc2')}
    del _L2_xattn_all

    def _L3_xattn_setup():
        import jax, jax.numpy as jnp
        import numpy as np
        H = 512
        NH = 32
        KVH = 8
        HD = H // NH
        GROUPS = NH // KVH
        EPS = 1e-06
        B, L, S = (4, 256, 256)

        def _gqa_forward(hidden_state, encoder_hidden_state, encoder_attention_mask, Wq, bq, Wk, bk, Wv, bv, Wo, bo, gamma, beta):
            b, l, _ = hidden_state.shape
            s = encoder_hidden_state.shape[1]
            q = hidden_state @ Wq + bq
            k = encoder_hidden_state @ Wk + bk
            v = encoder_hidden_state @ Wv + bv
            q = q.reshape(b, l, KVH, GROUPS, HD).transpose(0, 2, 3, 1, 4)
            k = k.reshape(b, s, KVH, HD).transpose(0, 2, 1, 3)
            v = v.reshape(b, s, KVH, HD).transpose(0, 2, 1, 3)
            scale = 1.0 / jnp.sqrt(jnp.asarray(HD, q.dtype))
            scores = jnp.einsum('bkgld,bksd->bkgls', q, k) * scale
            scores = scores + encoder_attention_mask[:, :, None, :, :]
            attn = jax.nn.softmax(scores, axis=-1)
            out = jnp.einsum('bkgls,bksd->bkgld', attn, v)
            out = out.transpose(0, 3, 1, 2, 4).reshape(b, l, H)
            out = out @ Wo + bo
            x = out + hidden_state
            mu = jnp.mean(x, axis=-1, keepdims=True)
            var = jnp.var(x, axis=-1, keepdims=True)
            return (x - mu) * jax.lax.rsqrt(var + EPS) * gamma + beta
        key = jax.random.key(seed)
        ks = jax.random.split(key, 12)
        sd = 0.02
        return {'hidden_state': jax.random.normal(ks[0], (B, L, H), jnp.float32), 'encoder_hidden_state': jax.random.normal(ks[1], (B, S, H), jnp.float32), 'encoder_attention_mask': jnp.zeros((B, 1, L, S), jnp.float32), 'Wq': jax.random.normal(ks[2], (H, H), jnp.float32) * sd, 'bq': jnp.zeros((H,), jnp.float32), 'Wk': jax.random.normal(ks[3], (H, KVH * HD), jnp.float32) * sd, 'bk': jnp.zeros((KVH * HD,), jnp.float32), 'Wv': jax.random.normal(ks[4], (H, KVH * HD), jnp.float32) * sd, 'bv': jnp.zeros((KVH * HD,), jnp.float32), 'Wo': jax.random.normal(ks[5], (H, H), jnp.float32) * sd, 'bo': jnp.zeros((H,), jnp.float32), 'gamma': jnp.ones((H,), jnp.float32), 'beta': jnp.zeros((H,), jnp.float32)}
    _L3_xattn_all = _L3_xattn_setup()
    _L3_xattn_in = {k: v for k, v in _L3_xattn_all.items() if k in ('Wq', 'bq', 'Wk', 'bk', 'Wv', 'bv', 'Wo', 'bo', 'gamma', 'beta')}
    del _L3_xattn_all
    return {'x': x, 'ctx_2048': ctx_2048, 'mask_BxS2_ik0': mask_BxS2_ik0, 'mask_Bx1xSxS2_ff0': mask_Bx1xSxS2_ff0, 'L0_xattn_q_w': _L0_xattn_in['q_w'], 'L0_xattn_q_b': _L0_xattn_in['q_b'], 'L0_xattn_kv_w': _L0_xattn_in['kv_w'], 'L0_xattn_kv_b': _L0_xattn_in['kv_b'], 'L0_xattn_out_w': _L0_xattn_in['out_w'], 'L0_xattn_out_b': _L0_xattn_in['out_b'], 'L0_xattn_postnorm_w': _L0_xattn_in['postnorm_w'], 'L0_xattn_mlp_w1': _L0_xattn_in['mlp_w1'], 'L0_xattn_mlp_b1': _L0_xattn_in['mlp_b1'], 'L0_xattn_mlp_w2': _L0_xattn_in['mlp_w2'], 'L0_xattn_mlp_b2': _L0_xattn_in['mlp_b2'], 'L1_xattn_ln1_w': _L1_xattn_in['ln1_w'], 'L1_xattn_ln1_b': _L1_xattn_in['ln1_b'], 'L1_xattn_ln2_w': _L1_xattn_in['ln2_w'], 'L1_xattn_ln2_b': _L1_xattn_in['ln2_b'], 'L1_xattn_maa_x': _L1_xattn_in['maa_x'], 'L1_xattn_maa_w': _L1_xattn_in['maa_w'], 'L1_xattn_maa_k': _L1_xattn_in['maa_k'], 'L1_xattn_maa_v': _L1_xattn_in['maa_v'], 'L1_xattn_maa_r': _L1_xattn_in['maa_r'], 'L1_xattn_maa_g': _L1_xattn_in['maa_g'], 'L1_xattn_maa_w1': _L1_xattn_in['maa_w1'], 'L1_xattn_maa_w2': _L1_xattn_in['maa_w2'], 'L1_xattn_time_decay': _L1_xattn_in['time_decay'], 'L1_xattn_decay_w1': _L1_xattn_in['decay_w1'], 'L1_xattn_decay_w2': _L1_xattn_in['decay_w2'], 'L1_xattn_faaaa': _L1_xattn_in['faaaa'], 'L1_xattn_Wr': _L1_xattn_in['Wr'], 'L1_xattn_Wk': _L1_xattn_in['Wk'], 'L1_xattn_Wv': _L1_xattn_in['Wv'], 'L1_xattn_Wg': _L1_xattn_in['Wg'], 'L1_xattn_Wo': _L1_xattn_in['Wo'], 'L1_xattn_gn_w': _L1_xattn_in['gn_w'], 'L1_xattn_gn_b': _L1_xattn_in['gn_b'], 'L1_xattn_fmaa_k': _L1_xattn_in['fmaa_k'], 'L1_xattn_fmaa_r': _L1_xattn_in['fmaa_r'], 'L1_xattn_fWk': _L1_xattn_in['fWk'], 'L1_xattn_fWr': _L1_xattn_in['fWr'], 'L1_xattn_fWv': _L1_xattn_in['fWv'], 'L2_xattn_ln1_scale': _L2_xattn_in['ln1_scale'], 'L2_xattn_ln1_offset': _L2_xattn_in['ln1_offset'], 'L2_xattn_wq1': _L2_xattn_in['wq1'], 'L2_xattn_bq1': _L2_xattn_in['bq1'], 'L2_xattn_wk1': _L2_xattn_in['wk1'], 'L2_xattn_bk1': _L2_xattn_in['bk1'], 'L2_xattn_wv1': _L2_xattn_in['wv1'], 'L2_xattn_bv1': _L2_xattn_in['bv1'], 'L2_xattn_wo1': _L2_xattn_in['wo1'], 'L2_xattn_bo1': _L2_xattn_in['bo1'], 'L2_xattn_bias_k1': _L2_xattn_in['bias_k1'], 'L2_xattn_bias_v1': _L2_xattn_in['bias_v1'], 'L2_xattn_ln2_scale': _L2_xattn_in['ln2_scale'], 'L2_xattn_ln2_offset': _L2_xattn_in['ln2_offset'], 'L2_xattn_wq2': _L2_xattn_in['wq2'], 'L2_xattn_bq2': _L2_xattn_in['bq2'], 'L2_xattn_wk2': _L2_xattn_in['wk2'], 'L2_xattn_bk2': _L2_xattn_in['bk2'], 'L2_xattn_wv2': _L2_xattn_in['wv2'], 'L2_xattn_bv2': _L2_xattn_in['bv2'], 'L2_xattn_wo2': _L2_xattn_in['wo2'], 'L2_xattn_bo2': _L2_xattn_in['bo2'], 'L2_xattn_bias_k2': _L2_xattn_in['bias_k2'], 'L2_xattn_bias_v2': _L2_xattn_in['bias_v2'], 'L2_xattn_ln_mlp_scale': _L2_xattn_in['ln_mlp_scale'], 'L2_xattn_ln_mlp_offset': _L2_xattn_in['ln_mlp_offset'], 'L2_xattn_w_fc1': _L2_xattn_in['w_fc1'], 'L2_xattn_b_fc1': _L2_xattn_in['b_fc1'], 'L2_xattn_w_fc2': _L2_xattn_in['w_fc2'], 'L2_xattn_b_fc2': _L2_xattn_in['b_fc2'], 'L3_xattn_Wq': _L3_xattn_in['Wq'], 'L3_xattn_bq': _L3_xattn_in['bq'], 'L3_xattn_Wk': _L3_xattn_in['Wk'], 'L3_xattn_bk': _L3_xattn_in['bk'], 'L3_xattn_Wv': _L3_xattn_in['Wv'], 'L3_xattn_bv': _L3_xattn_in['bv'], 'L3_xattn_Wo': _L3_xattn_in['Wo'], 'L3_xattn_bo': _L3_xattn_in['bo'], 'L3_xattn_gamma': _L3_xattn_in['gamma'], 'L3_xattn_beta': _L3_xattn_in['beta']}

def reference(x, ctx_2048, mask_BxS2_ik0, mask_Bx1xSxS2_ff0, L0_xattn_q_w, L0_xattn_q_b, L0_xattn_kv_w, L0_xattn_kv_b, L0_xattn_out_w, L0_xattn_out_b, L0_xattn_postnorm_w, L0_xattn_mlp_w1, L0_xattn_mlp_b1, L0_xattn_mlp_w2, L0_xattn_mlp_b2, L1_xattn_ln1_w, L1_xattn_ln1_b, L1_xattn_ln2_w, L1_xattn_ln2_b, L1_xattn_maa_x, L1_xattn_maa_w, L1_xattn_maa_k, L1_xattn_maa_v, L1_xattn_maa_r, L1_xattn_maa_g, L1_xattn_maa_w1, L1_xattn_maa_w2, L1_xattn_time_decay, L1_xattn_decay_w1, L1_xattn_decay_w2, L1_xattn_faaaa, L1_xattn_Wr, L1_xattn_Wk, L1_xattn_Wv, L1_xattn_Wg, L1_xattn_Wo, L1_xattn_gn_w, L1_xattn_gn_b, L1_xattn_fmaa_k, L1_xattn_fmaa_r, L1_xattn_fWk, L1_xattn_fWr, L1_xattn_fWv, L2_xattn_ln1_scale, L2_xattn_ln1_offset, L2_xattn_wq1, L2_xattn_bq1, L2_xattn_wk1, L2_xattn_bk1, L2_xattn_wv1, L2_xattn_bv1, L2_xattn_wo1, L2_xattn_bo1, L2_xattn_bias_k1, L2_xattn_bias_v1, L2_xattn_ln2_scale, L2_xattn_ln2_offset, L2_xattn_wq2, L2_xattn_bq2, L2_xattn_wk2, L2_xattn_bk2, L2_xattn_wv2, L2_xattn_bv2, L2_xattn_wo2, L2_xattn_bo2, L2_xattn_bias_k2, L2_xattn_bias_v2, L2_xattn_ln_mlp_scale, L2_xattn_ln_mlp_offset, L2_xattn_w_fc1, L2_xattn_b_fc1, L2_xattn_w_fc2, L2_xattn_b_fc2, L3_xattn_Wq, L3_xattn_bq, L3_xattn_Wk, L3_xattn_bk, L3_xattn_Wv, L3_xattn_bv, L3_xattn_Wo, L3_xattn_bo, L3_xattn_gamma, L3_xattn_beta):
    import jax
    import jax.numpy as jnp

    def _L0_xattn_ref(x, latents, attention_mask, q_w, q_b, kv_w, kv_b, out_w, out_b, postnorm_w, mlp_w1, mlp_b1, mlp_w2, mlp_b2):
        import jax, jax.numpy as jnp
        import numpy as np
        B, P, K, H, NH = (4, 512, 64, 512, 16)
        DH = H // NH
        EPS = 1e-06

        def rmsnorm(x, w):
            var = jnp.mean(jnp.square(x), axis=-1, keepdims=True)
            return x * jax.lax.rsqrt(var + EPS) * w
        b, p, _ = x.shape
        k_len = latents.shape[1]
        residual = latents
        h = jnp.concatenate([x, latents], axis=1)
        q = (latents @ q_w + q_b).reshape(b, k_len, NH, DH)
        kv = (h @ kv_w + kv_b).reshape(b, p + k_len, NH, DH, 2)
        kmat, v = (kv[..., 0], kv[..., 1])
        attn = jnp.einsum('bkhd,bnhd->bhkn', q, kmat) / DH
        full_mask = jnp.concatenate([attention_mask.astype(bool), jnp.ones((b, k_len), bool)], axis=-1)
        attn = jnp.where(full_mask[:, None, None, :], attn, -jnp.inf)
        attn = jax.nn.softmax(attn.astype(jnp.float32), axis=-1).astype(q.dtype)
        attn_out = jnp.einsum('bhkn,bnhd->bkhd', attn, v).reshape(b, k_len, H)
        attn_out = attn_out @ out_w + out_b + residual
        out = rmsnorm(attn_out, postnorm_w)
        out = jax.nn.gelu(out @ mlp_w1 + mlp_b1) @ mlp_w2 + mlp_b2
        return out + residual

    def _L1_xattn_ref(x, state, i, ln1_w, ln1_b, ln2_w, ln2_b, maa_x, maa_w, maa_k, maa_v, maa_r, maa_g, maa_w1, maa_w2, time_decay, decay_w1, decay_w2, faaaa, Wr, Wk, Wv, Wg, Wo, gn_w, gn_b, fmaa_k, fmaa_r, fWk, fWr, fWv):
        import jax, jax.numpy as jnp
        import numpy as np
        N_HEAD = 32
        EPS = 1e-05

        def _ln(x, w, b):
            m = jnp.mean(x, axis=-1, keepdims=True)
            v = jnp.mean((x - m) ** 2, axis=-1, keepdims=True)
            return (x - m) * jax.lax.rsqrt(v + EPS) * w + b

        def _forward(x, state, i, ln1_w, ln1_b, ln2_w, ln2_b, maa_x, maa_w, maa_k, maa_v, maa_r, maa_g, maa_w1, maa_w2, time_decay, decay_w1, decay_w2, faaaa, Wr, Wk, Wv, Wg, Wo, gn_w, gn_b, fmaa_k, fmaa_r, fWk, fWr, fWv):
            B, L, C = x.shape
            H = N_HEAD
            S = C // H
            i0 = (2 + S) * i
            xa = _ln(x, ln1_w, ln1_b)
            sx = jnp.concatenate([state[:, i0 + 1][:, None], xa[:, :-1]], axis=1) - xa
            xxx = xa + sx * maa_x
            t = jnp.tanh(xxx @ maa_w1).reshape(B, L, 5, -1)
            m = jnp.einsum('blfd,fdc->blfc', t, maa_w2)
            mw, mk, mv, mr, mg = (m[:, :, j] for j in range(5))
            xw = xa + sx * (maa_w + mw)
            xk = xa + sx * (maa_k + mk)
            xv = xa + sx * (maa_v + mv)
            xr = xa + sx * (maa_r + mr)
            xg = xa + sx * (maa_g + mg)
            w = time_decay + jnp.tanh(xw @ decay_w1) @ decay_w2
            w = jnp.exp(-jnp.exp(w)).reshape(B, L, H, S)
            r = (xr @ Wr.T).reshape(B, L, H, S)
            k = (xk @ Wk.T).reshape(B, L, H, S)
            v = (xv @ Wv.T).reshape(B, L, H, S)
            g = jax.nn.silu(xg @ Wg.T)
            s0 = state[:, i0 + 2:i0 + 2 + S].reshape(B, H, S, S)

            def step(s, inp):
                k_l, v_l, w_l, r_l = inp
                a = k_l[..., :, None] * v_l[..., None, :]
                out = jnp.einsum('bhs,bhst->bht', r_l, faaaa * a + s)
                s_new = a + w_l[..., None] * s
                return (s_new, out)
            seq = tuple((z.transpose(1, 0, 2, 3) for z in (k, v, w, r)))
            _, outs = jax.lax.scan(step, s0, seq)
            y = outs.transpose(1, 0, 2, 3)
            gm = jnp.mean(y, axis=-1, keepdims=True)
            gv = jnp.mean((y - gm) ** 2, axis=-1, keepdims=True)
            y = ((y - gm) * jax.lax.rsqrt(gv + EPS)).reshape(B, L, C) * gn_w + gn_b
            x = x + y * g @ Wo.T
            xc = _ln(x, ln2_w, ln2_b)
            sxc = jnp.concatenate([state[:, i0][:, None], xc[:, :-1]], axis=1) - xc
            xk2 = xc + sxc * fmaa_k
            xr2 = xc + sxc * fmaa_r
            rr = jax.nn.sigmoid(xr2 @ fWr.T)
            kk = jnp.square(jax.nn.relu(xk2 @ fWk.T))
            x = x + rr * (kk @ fWv.T)
            return x
        return _forward(x, state, i, ln1_w, ln1_b, ln2_w, ln2_b, maa_x, maa_w, maa_k, maa_v, maa_r, maa_g, maa_w1, maa_w2, time_decay, decay_w1, decay_w2, faaaa, Wr, Wk, Wv, Wg, Wo, gn_w, gn_b, fmaa_k, fmaa_r, fWk, fWr, fWv)

    def _L2_xattn_ref(x, xf_1, xf_2, ln1_scale, ln1_offset, wq1, bq1, wk1, bk1, wv1, bv1, wo1, bo1, bias_k1, bias_v1, ln2_scale, ln2_offset, wq2, bq2, wk2, bk2, wv2, bv2, wo2, bo2, bias_k2, bias_v2, ln_mlp_scale, ln_mlp_offset, w_fc1, b_fc1, w_fc2, b_fc2):
        import jax, jax.numpy as jnp
        import numpy as np
        B, Q, S1, S2 = (4, 64, 512, 512)
        D, H, K, F = (512, 16, 128, 2048)
        LN_EPS = 1e-05

        def _layer_norm(x, scale, offset):
            mu = jnp.mean(x, axis=-1, keepdims=True)
            var = jnp.var(x, axis=-1, keepdims=True)
            return (x - mu) * jax.lax.rsqrt(var + LN_EPS) * scale + offset

        def _cross_attention(q_in, kv_in, wq, bq, wk, bk, wv, bv, wo, bo, bias_k, bias_v):
            b, q_len, _ = q_in.shape
            t = kv_in.shape[1]
            qh = (q_in @ wq + bq).reshape(b, q_len, H, K)
            kh = (kv_in @ wk + bk).reshape(b, t, H, K)
            vh = (kv_in @ wv + bv).reshape(b, t, H, K)
            kh = jnp.concatenate([kh, jnp.broadcast_to(bias_k, (b, 1, H, K))], axis=1)
            vh = jnp.concatenate([vh, jnp.broadcast_to(bias_v, (b, 1, H, K))], axis=1)
            scale = jnp.sqrt(jnp.asarray(K, q_in.dtype))
            logits = jnp.einsum('bqhk,bthk->bhqt', qh, kh) / scale
            weights = jax.nn.softmax(logits, axis=-1)
            ctx = jnp.einsum('bhqt,bthk->bqhk', weights, vh).reshape(b, q_len, H * K)
            return ctx @ wo + bo

        def _forward(x, xf_1, xf_2, ln1_scale, ln1_offset, wq1, bq1, wk1, bk1, wv1, bv1, wo1, bo1, bias_k1, bias_v1, ln2_scale, ln2_offset, wq2, bq2, wk2, bk2, wv2, bv2, wo2, bo2, bias_k2, bias_v2, ln_mlp_scale, ln_mlp_offset, w_fc1, b_fc1, w_fc2, b_fc2):
            res = x
            h = _layer_norm(x, ln1_scale, ln1_offset)
            x = res + _cross_attention(h, xf_1, wq1, bq1, wk1, bk1, wv1, bv1, wo1, bo1, bias_k1, bias_v1)
            res = x
            h = _layer_norm(x, ln2_scale, ln2_offset)
            x = res + _cross_attention(h, xf_2, wq2, bq2, wk2, bk2, wv2, bv2, wo2, bo2, bias_k2, bias_v2)
            h = _layer_norm(x, ln_mlp_scale, ln_mlp_offset)
            h = jax.nn.gelu(h @ w_fc1 + b_fc1, approximate=False) @ w_fc2 + b_fc2
            return x + h
        return _forward(x, xf_1, xf_2, ln1_scale, ln1_offset, wq1, bq1, wk1, bk1, wv1, bv1, wo1, bo1, bias_k1, bias_v1, ln2_scale, ln2_offset, wq2, bq2, wk2, bk2, wv2, bv2, wo2, bo2, bias_k2, bias_v2, ln_mlp_scale, ln_mlp_offset, w_fc1, b_fc1, w_fc2, b_fc2)

    def _L3_xattn_ref(hidden_state, encoder_hidden_state, encoder_attention_mask, Wq, bq, Wk, bk, Wv, bv, Wo, bo, gamma, beta):
        import jax, jax.numpy as jnp
        import numpy as np
        H = 512
        NH = 32
        KVH = 8
        HD = H // NH
        GROUPS = NH // KVH
        EPS = 1e-06
        B, L, S = (4, 256, 256)

        def _gqa_forward(hidden_state, encoder_hidden_state, encoder_attention_mask, Wq, bq, Wk, bk, Wv, bv, Wo, bo, gamma, beta):
            b, l, _ = hidden_state.shape
            s = encoder_hidden_state.shape[1]
            q = hidden_state @ Wq + bq
            k = encoder_hidden_state @ Wk + bk
            v = encoder_hidden_state @ Wv + bv
            q = q.reshape(b, l, KVH, GROUPS, HD).transpose(0, 2, 3, 1, 4)
            k = k.reshape(b, s, KVH, HD).transpose(0, 2, 1, 3)
            v = v.reshape(b, s, KVH, HD).transpose(0, 2, 1, 3)
            scale = 1.0 / jnp.sqrt(jnp.asarray(HD, q.dtype))
            scores = jnp.einsum('bkgld,bksd->bkgls', q, k) * scale
            scores = scores + encoder_attention_mask[:, :, None, :, :]
            attn = jax.nn.softmax(scores, axis=-1)
            out = jnp.einsum('bkgls,bksd->bkgld', attn, v)
            out = out.transpose(0, 3, 1, 2, 4).reshape(b, l, H)
            out = out @ Wo + bo
            x = out + hidden_state
            mu = jnp.mean(x, axis=-1, keepdims=True)
            var = jnp.var(x, axis=-1, keepdims=True)
            return (x - mu) * jax.lax.rsqrt(var + EPS) * gamma + beta
        return _gqa_forward(hidden_state, encoder_hidden_state, encoder_attention_mask, Wq, bq, Wk, bk, Wv, bv, Wo, bo, gamma, beta)
    x = _L0_xattn_ref(ctx_2048, x, mask_BxS2_ik0, L0_xattn_q_w, L0_xattn_q_b, L0_xattn_kv_w, L0_xattn_kv_b, L0_xattn_out_w, L0_xattn_out_b, L0_xattn_postnorm_w, L0_xattn_mlp_w1, L0_xattn_mlp_b1, L0_xattn_mlp_w2, L0_xattn_mlp_b2)
    x = _L1_xattn_ref(x, ctx_2048, 0, L1_xattn_ln1_w, L1_xattn_ln1_b, L1_xattn_ln2_w, L1_xattn_ln2_b, L1_xattn_maa_x, L1_xattn_maa_w, L1_xattn_maa_k, L1_xattn_maa_v, L1_xattn_maa_r, L1_xattn_maa_g, L1_xattn_maa_w1, L1_xattn_maa_w2, L1_xattn_time_decay, L1_xattn_decay_w1, L1_xattn_decay_w2, L1_xattn_faaaa, L1_xattn_Wr, L1_xattn_Wk, L1_xattn_Wv, L1_xattn_Wg, L1_xattn_Wo, L1_xattn_gn_w, L1_xattn_gn_b, L1_xattn_fmaa_k, L1_xattn_fmaa_r, L1_xattn_fWk, L1_xattn_fWr, L1_xattn_fWv)
    x = _L2_xattn_ref(x, ctx_2048, ctx_2048, L2_xattn_ln1_scale, L2_xattn_ln1_offset, L2_xattn_wq1, L2_xattn_bq1, L2_xattn_wk1, L2_xattn_bk1, L2_xattn_wv1, L2_xattn_bv1, L2_xattn_wo1, L2_xattn_bo1, L2_xattn_bias_k1, L2_xattn_bias_v1, L2_xattn_ln2_scale, L2_xattn_ln2_offset, L2_xattn_wq2, L2_xattn_bq2, L2_xattn_wk2, L2_xattn_bk2, L2_xattn_wv2, L2_xattn_bv2, L2_xattn_wo2, L2_xattn_bo2, L2_xattn_bias_k2, L2_xattn_bias_v2, L2_xattn_ln_mlp_scale, L2_xattn_ln_mlp_offset, L2_xattn_w_fc1, L2_xattn_b_fc1, L2_xattn_w_fc2, L2_xattn_b_fc2)
    x = _L3_xattn_ref(x, ctx_2048, mask_Bx1xSxS2_ff0, L3_xattn_Wq, L3_xattn_bq, L3_xattn_Wk, L3_xattn_bk, L3_xattn_Wv, L3_xattn_bv, L3_xattn_Wo, L3_xattn_bo, L3_xattn_gamma, L3_xattn_beta)
    return x

_drawn_inputs = setup_inputs


def setup_inputs(seed=0):
    import zlib

    import numpy as np

    out = dict(_drawn_inputs(seed))
    spreads = {'L0_xattn_q_b': (0.0, 0.8),
     'L0_xattn_kv_b': (0.0, 0.771),
     'L0_xattn_out_b': (0.0, 0.339),
     'L0_xattn_postnorm_w': (1.0, 0.2),
     'L0_xattn_mlp_b1': (0.0, 0.1),
     'L0_xattn_mlp_b2': (0.0, 0.1),
     'L1_xattn_ln1_w': (1.0, 0.2),
     'L1_xattn_ln1_b': (0.0, 0.318),
     'L1_xattn_ln2_w': (1.0, 0.6),
     'L1_xattn_ln2_b': (0.0, 0.8),
     'L1_xattn_gn_w': (1.0, 0.6),
     'L1_xattn_gn_b': (0.0, 0.8),
     'L2_xattn_ln1_scale': (1.0, 0.6),
     'L2_xattn_ln1_offset': (0.0, 0.8),
     'L2_xattn_bq1': (0.0, 0.8),
     'L2_xattn_bk1': (0.0, 2.0),
     'L2_xattn_bv1': (0.0, 0.1),
     'L2_xattn_bo1': (0.0, 0.1),
     'L2_xattn_ln2_scale': (1.0, 0.6),
     'L2_xattn_ln2_offset': (0.0, 0.8),
     'L2_xattn_bq2': (0.0, 0.8),
     'L2_xattn_bk2': (0.0, 2.0),
     'L2_xattn_bv2': (0.0, 0.1),
     'L2_xattn_bo2': (0.0, 0.1),
     'L2_xattn_ln_mlp_scale': (1.0, 0.2),
     'L2_xattn_ln_mlp_offset': (0.0, 0.39),
     'L2_xattn_b_fc1': (0.0, 0.1),
     'L2_xattn_b_fc2': (0.0, 0.1),
     'L3_xattn_bq': (0.0, 0.8),
     'L3_xattn_bk': (0.0, 2.0),
     'L3_xattn_bv': (0.0, 0.273),
     'L3_xattn_bo': (0.0, 0.1),
     'L3_xattn_gamma': (1.0, 0.2),
     'L3_xattn_beta': (0.0, 0.1)}
    factors = {'L0_xattn_q_w': 8.0,
     'L0_xattn_kv_w': 6.027,
     'L0_xattn_out_w': 4.161,
     'L1_xattn_maa_x': 7.444,
     'L1_xattn_maa_w': 8.0,
     'L1_xattn_maa_w1': 3.81,
     'L1_xattn_maa_w2': 3.893,
     'L1_xattn_decay_w1': 8.0,
     'L1_xattn_decay_w2': 8.0,
     'L1_xattn_faaaa': 4.199,
     'L1_xattn_fmaa_k': 2.933,
     'L1_xattn_fmaa_r': 8.0,
     'L1_xattn_fWr': 8.0,
     'L2_xattn_wq1': 4.03,
     'L2_xattn_wk1': 3.956,
     'L2_xattn_bias_k1': 64.0,
     'L2_xattn_bias_v1': 64.0,
     'L2_xattn_wq2': 3.953,
     'L2_xattn_wk2': 3.842,
     'L2_xattn_bias_k2': 64.0,
     'L2_xattn_bias_v2': 64.0,
     'L3_xattn_Wq': 7.521,
     'L3_xattn_Wk': 7.375}
    for name, (base, spread) in spreads.items():
        noise = np.random.default_rng([zlib.crc32(name.encode()), seed]).standard_normal(out[name].shape)
        drawn = base * np.exp(spread * noise) if base else spread * noise
        out[name] = jnp.asarray(drawn.astype(out[name].dtype))
    for name, factor in factors.items():
        out[name] = (out[name] * factor).astype(out[name].dtype)
    return out
```

```python
from contextlib import ExitStack

import concourse.bass as bass
from concourse import mybir

F32 = mybir.dt.float32
I32 = mybir.dt.int32
ALU = mybir.AluOpType
ACT = mybir.ActivationFunctionType
AX = mybir.AxisListType

P = 128
B, L, D = 8, 100, 512
S = 361
KT = D // P
HALF = 4 * L
HALVES = B * L // HALF
MASKED = -1e30

H0, DH0 = 16, 32
T0 = 116
NT0 = 4
N0 = T0 * NT0
F_MLP = 2048
FT = F_MLP // P


def at(batch, events, event, back=0):
    return events * (batch + 2 - back) + event + 1


class Semaphores:

    def __init__(self, nc):
        self.nc, self.taken, self.ended = nc, [], []

    def take(self, name):
        self.taken.append(self.nc.alloc_semaphore(name))
        return self.taken[-1]

    def clear_ended(self, pool):
        for s in self.ended:
            pool.sem_clear(s)

    def end_phase(self):
        for s in self.ended:
            self.nc.release_semaphore(s)
        self.ended, self.taken = self.taken, []


class Shared:
    pass


PARAM_TILES = [
    [("L0_xattn_q_b", 4), ("L0_xattn_postnorm_w", 4), ("L0_xattn_mlp_b1", 16), ("kv_b_keys", 4),
     ("L1_xattn_ln1_w", 4), ("L1_xattn_ln1_b", 4), ("L1_xattn_ln2_w", 4), ("L1_xattn_ln2_b", 4),
     ("L1_xattn_maa_x", 4), ("L1_xattn_maa_w", 4), ("L1_xattn_maa_k", 4), ("L1_xattn_maa_v", 4),
     ("L1_xattn_maa_r", 4), ("L1_xattn_maa_g", 4), ("L1_xattn_time_decay", 4), ("L1_xattn_faaaa", 4),
     ("L1_xattn_gn_w", 4), ("L1_xattn_gn_b", 4), ("L1_xattn_fmaa_k", 4), ("L1_xattn_fmaa_r", 4)],
    [("L2_xattn_ln1_scale", 4), ("L2_xattn_ln1_offset", 4), ("L2_xattn_ln2_scale", 4),
     ("L2_xattn_ln2_offset", 4), ("L2_xattn_ln_mlp_scale", 4), ("L2_xattn_ln_mlp_offset", 4),
     ("L2_xattn_bq1", 16), ("L2_xattn_bq2", 16), ("L2_xattn_bv1", 16), ("L2_xattn_bv2", 16),
     ("L2_xattn_b_fc1", 16)],
    [("L2_xattn_bk1", 16), ("L2_xattn_bk2", 16), ("L2_xattn_bias_k1", 16), ("L2_xattn_bias_k2", 16),
     ("L3_xattn_bq", 4), ("L3_xattn_bk", 1)],
]
PARAM_AT = {}
for _tile, _rows in enumerate(PARAM_TILES):
    _at = 0
    for _name, _n in _rows:
        PARAM_AT[_name] = (_tile, _at, _n)
        _at += _n


def column(k, name, j=0, n=1, rows=slice(0, P)):
    tile, first, _ = PARAM_AT[name]
    return k.params[rows, tile, first + j:first + j + n]


def setup(nc, k, ins, ctx):
    k.ident = ctx.enter_context(nc.sbuf_tensor("ident", [P, P], F32))
    k.params = ctx.enter_context(nc.sbuf_tensor("params", [P, len(PARAM_TILES), P], F32))
    k.minus_half = ctx.enter_context(nc.sbuf_tensor("minus_half", [P, 4], F32))
    k.eps5 = ctx.enter_context(nc.sbuf_tensor("eps5", [P, 1], F32))
    k.head_of = ctx.enter_context(nc.sbuf_tensor("head_of", [P, P // N1], F32))
    k.X = ctx.enter_context(nc.sbuf_tensor("X", [L, B, D], F32))
    with ExitStack() as own:
        own.callback(k.sems.end_phase)
        rows = own.enter_context(nc.sbuf_tensor("param_rows", [P, len(PARAM_TILES), P], F32))
        ps = own.enter_context(nc.psum_tensor("ps_setup", [P, len(PARAM_TILES), P], F32))
        zeroed = k.sems.take("rows_zeroed")
        blank = k.sems.take("ident_blank")
        ready = k.sems.take("ident_ready")
        loaded = k.sems.take("params_loaded")
        k.x_loaded = k.sems.take("x_loaded")
        turned = k.sems.take("params_turned")
        copied = k.sems.take("params_copied")
        block = own.enter_context(nc.Block())

        n_loads = sum(len(t) for t in PARAM_TILES)

        @block.vector
        def _(dve):
            dve.memset(rows[:], 0.0).then_inc(zeroed, 1)
            dve.wait_ge(k.x_loaded, 16)
            dve.wait_ge(turned, 1)
            dve.tensor_copy(k.params[:], ps[:]).then_inc(copied, 1)

        @block.gpsimd
        def _(pool):
            k.sems.clear_ended(pool)
            pool.memset(k.minus_half[:], -0.5)
            pool.memset(k.eps5[:], 1e-5)
            pool.memset(k.ident[:], 0.0).then_inc(blank, 1)
            pool.wait_ge(blank, 1)
            pool.affine_select(out=k.ident[:], in_=k.ident[:], pattern=[[1, P]], compare_op=ALU.not_equal,
                               fill=1.0, base=0, channel_multiplier=-1).then_inc(ready, 1)

        @block.sync
        def _(sp):
            sp.dma_start(k.X[:], ins["x"].rearrange("b l d -> l b d")).then_inc(k.x_loaded, 16)
            sp.wait_ge(zeroed, 1)
            for name, (tile, first, n) in PARAM_AT.items():
                dst = rows[first:first + n, tile, :]
                if name == "kv_b_keys":
                    src = ins["L0_xattn_kv_b"].rearrange("(m p two) -> m p two", m=n, two=2)[:, :, 0]
                    with nc.allow_non_contiguous_dma("512 biases"):
                        sp.dma_start(dst, src).then_inc(loaded, 16)
                    continue
                if name == "L3_xattn_bq":
                    src = ins[name].rearrange("(v g d) -> g v d", v=8, g=4)
                    dst = dst.rearrange("g (v d) -> g v d", v=8)
                    sp.dma_start(dst, src).then_inc(loaded, 16)
                    continue
                src = ins[name]
                if len(src.shape) == 3:
                    src = src.rearrange("a b c -> (a b c)")
                elif len(src.shape) == 4:
                    src = src.rearrange("a b c d -> (a b c d)")
                sp.dma_start(dst, src.rearrange("(n p) -> n p", p=P)).then_inc(loaded, 16)

        @block.tensor
        def _(pe):
            pe.wait_ge(ready, 1)
            pe.wait_ge(loaded, 16 * n_loads)
            for t in range(len(PARAM_TILES)):
                last = pe.transpose(ps[:, t, :], rows[:, t, :], k.ident[:])
            last.then_inc(turned, 1)


def layer0_attention(nc, k, ins, ctx):
    x, context, mask = ins["x"], ins["ctx_2048"], ins["mask_BxS2_ik0"]
    k.ctxT = nc.dram_tensor("ctxT", [B, P, KT, S], F32, kind="Internal").ap()

    def sem(name):
        return k.sems.take(name)

    with ExitStack() as own:
        own.callback(k.sems.end_phase)
        def sb(name, shape, dt=F32):
            return own.enter_context(nc.sbuf_tensor(name, shape, dt))

        q_w = sb("q_w", [P, KT, D])
        kv_w = sb("kv_w", [P, KT, 2 * D])
        v_bias = sb("v_bias", [P, 2 * D])
        mask_i = sb("mask_i", [L, B, S], I32)
        mask_add = [sb(f"mask_add{s}", [L, N0]) for s in range(2)]
        hcat = [sb(f"hcat{s}", [T0, NT0, D]) for s in range(2)]
        hT = [sb(f"hT{s}", [P, KT, N0]) for s in range(2)]
        keysT = sb("keysT", [P, KT, N0])
        keys_bias = sb("keys_bias", [P, KT])
        values = sb("values", [T0, NT0, D])
        q_heads = sb("q_heads", [P, H0, L])
        probs = [sb(f"probs{s}", [L, N0]) for s in range(4)]
        probsT = [sb(f"probsT{s}", [T0, NT0, L]) for s in range(2)]
        neg_max = sb("neg_max", [L, H0])
        sums = [sb(f"sums{s}", [L, H0]) for s in range(2)]
        rsum = sb("rsum", [L, H0])

        work = [own.enter_context(nc.psum_tensor(f"work{i}", [P, 512], F32)) for i in range(3)]
        ps_scores = [own.enter_context(nc.psum_tensor(f"scores{i}", [P, 512], F32)) for i in range(2)]
        ps_probsT = [own.enter_context(nc.psum_tensor(f"turned{i}", [P, 512], F32)) for i in range(2)]
        ps_att = own.enter_context(nc.psum_tensor("ps_att", [P, H0, DH0], F32))

        weights_loaded = sem("l0_weights_loaded")
        consts_done = sem("l0_consts_done")
        tokens_loaded = [sem(f"l0_tokens_loaded{s}") for s in range(2)]
        ctxT_stored = [sem(f"l0_ctxT_stored{s}") for s in range(2)]
        tile_done = sem("l0_tile_done")
        act_copied = sem("l0_act_copied")
        dve_copied = sem("l0_dve_copied")
        scored = sem("l0_scored")
        shifted = sem("l0_shifted")
        maxed = sem("l0_maxed")
        exped = sem("l0_exped")
        turned = sem("l0_turned")
        probsT_copied = sem("l0_probsT_copied")
        attended = sem("l0_attended")
        masked = sem("l0_masked")
        inverted = sem("l0_inverted")
        att_copied = sem("l0_att_copied")

        TILES = 3 * KT + 1
        ACT_OF = {**{j: j for j in range(KT)}, **{KT + 1 + m: KT + m for m in range(KT)}}
        DVE_OF = {KT: 0, **{2 * KT + 1 + j: 1 + j for j in range(NT0)}}

        def wait_copied(eng, b, tile):
            if tile < 0:
                b, tile = b - 1, {-3: TILES - 3, -2: TILES - 2, -1: TILES - 1}[tile]
            if tile in ACT_OF:
                eng.wait_ge(act_copied, at(b, len(ACT_OF), ACT_OF[tile]))
            else:
                eng.wait_ge(dve_copied, at(b, len(DVE_OF), DVE_OF[tile]))

        def bank_of(tile):
            return tile % 3

        def bank_before(tile):
            if tile >= 3:
                return tile - 3
            return {TILES - 1 - j: -1 - j for j in range(3)}[
                next(t for t in range(TILES - 1, TILES - 4, -1) if bank_of(t) == tile)]

        block = own.enter_context(nc.Block())

        @block.sync
        def _(sp):
            sp.dma_start(kv_w[:], ins["L0_xattn_kv_w"].rearrange("(k p) n -> p k n", p=P)).then_inc(weights_loaded, 16)
            sp.dma_start(q_w[:], ins["L0_xattn_q_w"].rearrange("(k p) n -> p k n", p=P)).then_inc(weights_loaded, 16)
            sp.dma_start(v_bias[:], ins["L0_xattn_kv_b"].partition_broadcast(P)).then_inc(weights_loaded, 16)
            sp.dma_start(mask_i[:], mask.partition_broadcast(L)).then_inc(weights_loaded, 16)
            sp.wait_ge(consts_done, 2)
            for s in range(2):
                sp.sem_inc(ctxT_stored[s], 16)
            whole = 3 * T0
            rest = S - whole
            with sp.Fori(0, B // 2) as i:
                for s in range(2):
                    b = 2 * i + s
                    sp.wait_ge(tile_done, at(b, TILES, KT - 1, back=2))
                    sp.dma_start(hcat[s][:, 0:3, :], context[b, 0:whole, :].rearrange("(t p) d -> p t d", p=T0)
                                 ).then_inc(tokens_loaded[s], 16)
                    sp.dma_start(hcat[s][0:rest, 3, :], context[b, whole:S, :]).then_inc(tokens_loaded[s], 16)
                    sp.dma_start(hcat[s][rest:rest + L, 3, :], x[b]).then_inc(tokens_loaded[s], 16)
                    wait_copied(sp, b, KT - 1)
                    sp.dma_start(k.ctxT[b], hT[s][:, :, 0:S]).then_inc(ctxT_stored[s], 16)
            for s in range(2):
                sp.wait_ge(ctxT_stored[s], 16 * (B // 2 + 1))

        @block.gpsimd
        def _(pool):
            k.sems.clear_ended(pool)
            for s in range(2):
                last = pool.memset(hcat[s][:, 3, :], 0.0)
            last.then_inc(consts_done, 1)
            pool.memset(q_heads[:], 0.0).then_inc(consts_done, 1)

        @block.tensor
        def _(pe):
            for done, per in ((tile_done, TILES), (scored, H0), (turned, H0), (attended, H0)):
                pe.sem_inc(done, 2 * per)
            pe.wait_ge(weights_loaded, 64)
            with pe.Fori(0, B // 2) as i:
                for s in range(2):
                    b = 2 * i + s
                    pe.wait_ge(tokens_loaded[s], 48 * (i + 1))
                    for t in range(KT):
                        wait_copied(pe, b, bank_before(t))
                        for j in range(NT0):
                            mm = pe.transpose(work[bank_of(t)][:, j * T0:(j + 1) * T0],
                                              hcat[s][:, j, t * P:(t + 1) * P], k.ident[0:T0, 0:T0])
                        mm.then_inc(tile_done, 1)
                    wait_copied(pe, b, bank_before(KT))
                    wait_copied(pe, b, KT - 1)
                    for m in range(KT):
                        for t in range(KT):
                            mm = pe.matmul(work[bank_of(KT)][:, m * L:(m + 1) * L], q_w[:, t, m * P:(m + 1) * P],
                                           hT[s][:, t, S:S + L], start=(t == 0), stop=(t == KT - 1))
                    mm.then_inc(tile_done, 1)
                    for m in range(KT):
                        tile = KT + 1 + m
                        wait_copied(pe, b, bank_before(tile))
                        for t in range(KT):
                            mm = pe.matmul(work[bank_of(tile)][:, 0:N0],
                                           kv_w[:, t, 2 * m * P:2 * (m + 1) * P:2], hT[s][:, t, :],
                                           start=(t == 0), stop=(t == KT - 1))
                        mm.then_inc(tile_done, 1)
                    for j in range(NT0):
                        tile = 2 * KT + 1 + j
                        wait_copied(pe, b, bank_before(tile))
                        for t in range(KT):
                            mm = pe.matmul(work[bank_of(tile)][0:T0, :], hT[s][:, t, j * T0:(j + 1) * T0],
                                           kv_w[:, t, 1:2 * D:2], start=(t == 0), stop=(t == KT - 1))
                        mm.then_inc(tile_done, 1)

                    def scores(h):
                        if h == 0:
                            wait_copied(pe, b, KT)
                        if h % 4 == 0:
                            wait_copied(pe, b, KT + 1 + h // 4)
                        pe.wait_ge(shifted, at(b, H0, h - 2))
                        pe.matmul(ps_scores[h % 2][0:L, 0:N0], q_heads[:, h, :], keysT[:, h // 4, :],
                                  start=True, stop=True).then_inc(scored, 1)

                    def turn(h):
                        pe.wait_ge(exped, at(b, H0, h))
                        pe.wait_ge(probsT_copied, at(b, H0, h - 2))
                        for j in range(NT0):
                            mm = pe.transpose(ps_probsT[h % 2][0:T0, j * L:(j + 1) * L],
                                              probs[h % 4][:, j * T0:(j + 1) * T0], k.ident[0:L, 0:L])
                        mm.then_inc(turned, 1)

                    def attend(h):
                        if h == 0:
                            wait_copied(pe, b, TILES - 1)
                            pe.wait_ge(att_copied, at(b, 1, 0, back=1))
                        pe.wait_ge(probsT_copied, at(b, H0, h))
                        for j in range(NT0):
                            mm = pe.matmul(ps_att[0:L, h, :], probsT[h % 2][:, j, :],
                                           values[:, j, h * DH0:(h + 1) * DH0], start=(j == 0), stop=(j == NT0 - 1))
                        mm.then_inc(attended, 1)

                    for step in range(H0 + 3):
                        if step < H0:
                            scores(step)
                        if 0 <= step - 2 < H0:
                            turn(step - 2)
                        if 0 <= step - 3 < H0:
                            attend(step - 3)

        @block.scalar
        def _(act):
            act.sem_inc(act_copied, 2 * len(ACT_OF))
            act.sem_inc(exped, 2 * H0)
            act.sem_inc(probsT_copied, 2 * H0)
            act.wait_ge(consts_done, 3)
            with act.Fori(0, B // 2) as i:
                for s in range(2):
                    b = 2 * i + s
                    act.wait_ge(ctxT_stored[s], 16 * (i + 1))
                    for t in range(KT):
                        act.wait_ge(tile_done, at(b, TILES, t))
                        act.activation(hT[s][:, t, :], work[bank_of(t)][:, 0:N0], ACT.Copy).then_inc(act_copied, 1)
                    for m in range(KT):
                        tile = KT + 1 + m
                        act.wait_ge(tile_done, at(b, TILES, tile))
                        act.activation(keysT[:, m, :], work[bank_of(tile)][:, 0:N0], ACT.Identity,
                                       scale=1.0 / DH0, bias=keys_bias[:, m:m + 1]).then_inc(act_copied, 1)

                    def copy_probsT(h):
                        act.wait_ge(turned, at(b, H0, h))
                        act.wait_ge(attended, at(b, H0, h - 2))
                        act.activation(probsT[h % 2][:].rearrange("p j l -> p (j l)"),
                                       ps_probsT[h % 2][0:T0, 0:NT0 * L], ACT.Copy).then_inc(probsT_copied, 1)

                    for h in range(H0):
                        act.wait_ge(maxed, at(b, H0, h))
                        act.activation(probs[h % 4][:], probs[h % 4][:], ACT.Exp, bias=neg_max[:, h:h + 1],
                                       accum_out=sums[s][:, h:h + 1]).then_inc(exped, 1)
                        if h >= 1:
                            copy_probsT(h - 1)
                    copy_probsT(H0 - 1)

        @block.vector
        def _(dve):
            dve.sem_inc(dve_copied, 2 * len(DVE_OF))
            dve.sem_inc(shifted, 2 * H0)
            dve.sem_inc(maxed, 2 * H0)
            dve.sem_inc(inverted, 2)
            dve.sem_inc(att_copied, 2)
            dve.wait_ge(weights_loaded, 64)
            dve.wait_ge(consts_done, 2)
            dve.sem_inc(masked, 2)
            dve.tensor_scalar(keys_bias[:], column(k, "kv_b_keys", 0, KT), 1.0 / DH0, None, ALU.mult)
            for s in range(2):
                dve.memset(mask_add[s][:, S:S + L], 0.0)
                last = dve.memset(mask_add[s][:, S + L:N0], MASKED)
            last.then_inc(consts_done, 1)
            with dve.Fori(0, B // 2) as i:
                for s in range(2):
                    b = 2 * i + s
                    dve.wait_ge(tile_done, at(b, TILES, KT))
                    for j in range(4):
                        r = slice(DH0 * j, DH0 * (j + 1))
                        last = dve.tensor_tensor(
                            q_heads[r, j:H0:4, :], work[bank_of(KT)][r, 0:HALF].rearrange("p (m l) -> p m l", m=KT),
                            column(k, "L0_xattn_q_b", 0, KT, rows=r).unsqueeze(2).broadcast_to([DH0, KT, L]), ALU.add)
                    last.then_inc(dve_copied, 1)
                    for j in range(NT0):
                        tile = 2 * KT + 1 + j
                        dve.wait_ge(tile_done, at(b, TILES, tile))
                        dve.tensor_tensor(values[:, j, :], work[bank_of(tile)][0:T0, :], v_bias[0:T0, 1:2 * D:2],
                                          ALU.add).then_inc(dve_copied, 1)
                    dve.tensor_scalar(mask_add[s][:, 0:S], mask_i[:, bass.ds(b, 1), :].squeeze(1), 0, MASKED,
                                      ALU.is_equal, ALU.mult).then_inc(masked, 1)
                    dve.wait_ge(masked, at(b, 1, 0))
                    for h in range(H0):
                        dve.wait_ge(scored, at(b, H0, h))
                        dve.wait_ge(turned, at(b, H0, h - 4))
                        dve.tensor_tensor(probs[h % 4][:], ps_scores[h % 2][0:L, 0:N0], mask_add[s][:], ALU.add
                                          ).then_inc(shifted, 1)
                        dve.wait_ge(shifted, at(b, H0, h))
                        dve.tensor_reduce(neg_max[:, h:h + 1], probs[h % 4][:], AX.X, ALU.max, negate=True
                                          ).then_inc(maxed, 1)
                    dve.wait_ge(exped, at(b, H0, H0 - 1))
                    dve.reciprocal(rsum[:], sums[s][:]).then_inc(inverted, 1)
                    dve.wait_ge(inverted, at(b, 1, 0))
                    dve.wait_ge(attended, at(b, H0, H0 - 1))
                    dve.tensor_tensor(
                        k.ATT[:, bass.ds(b, 1), :].squeeze(1).rearrange("l (h d) -> l h d", h=H0), ps_att[0:L, :, :],
                        rsum[:].unsqueeze(2).broadcast_to([L, H0, DH0]), ALU.mult).then_inc(att_copied, 1)



class Tiles:

    def __init__(self, k, name, banks, stages):
        self.filled = k.sems.take(f"{name}_filled")
        self.emptied = {"a": k.sems.take(f"{name}_act_emptied"),
                        "d": k.sems.take(f"{name}_dve_emptied")}
        self.banks = banks
        self.first, self.size, self.by = {}, {}, []
        counts = {"a": 0, "d": 0}
        for stage, n, engines in stages:
            self.first[stage], self.size[stage] = len(self.by), n
            for j in range(n):
                e = engines[j % len(engines)]
                counts[e] += 1
                self.by.append((e, counts[e]))

    def bank(self, stage, j):
        return self.banks[(self.first[stage] + j) % len(self.banks)]

    def wait_free(self, pe, stage, j):
        before = self.first[stage] + j - len(self.banks)
        if before >= 0:
            e, n = self.by[before]
            pe.wait_ge(self.emptied[e], n)

    def wait_filled(self, eng, stage, j):
        eng.wait_ge(self.filled, self.first[stage] + j + 1)

    def wait_out(self, eng, stage, tiles=None):
        last = {}
        for j in (range(self.size[stage]) if tiles is None else tiles):
            e, n = self.by[self.first[stage] + j]
            last[e] = max(last.get(e, 0), n)
        for e, n in last.items():
            eng.wait_ge(self.emptied[e], n)

    def mine(self, engine, stage):
        return [j for j in range(self.size[stage]) if self.by[self.first[stage] + j][0] == engine]


def psum_banks(nc, ctx, name, n):
    return [ctx.enter_context(nc.psum_tensor(f"{name}{i}", [P, 512], F32)) for i in range(n)]


def half_tokens(t, tile, half):
    return t[:, tile, half * HALF:(half + 1) * HALF]


def turn_tokens(pe, k, tiles, stage, src, ready):
    for half in range(HALVES):
        for t in range(KT):
            j = half * KT + t
            tiles.wait_free(pe, stage, j)
            for c in range(4):
                b = 4 * half + c
                if t == 0:
                    ready(b)
                mm = pe.transpose(tiles.bank(stage, j)[:, c * L:(c + 1) * L],
                                  src[:, b, t * P:(t + 1) * P], k.ident[0:L, 0:L])
            mm.then_inc(tiles.filled, 1)


def project_tokens(pe, tiles, stage, lhs, weights, n_k, ready=None):
    for b in range(B):
        tiles.wait_free(pe, stage, b)
        if ready is not None:
            ready(b)
        for t in range(n_k):
            mm = pe.matmul(tiles.bank(stage, b)[0:L, :], lhs[:, t, b * L:(b + 1) * L], weights[:, t, :],
                           start=(t == 0), stop=(t == n_k - 1))
        mm.then_inc(tiles.filled, 1)


def statistics_semaphores(nc, k, ctx):
    k.stat_sem = {n: ctx.enter_context(nc.semaphore(f"norm_{n}")) for n in
                  ("summed", "aggregated", "shifted", "inverted", "normed")}
    k.norms = 0


def norm_half_dve(dve, k, src, dst, stats, eps, half, n):
    sem = k.stat_sem
    for c in range(4):
        b = 4 * half + c
        last = dve.bn_stats(stats.six[:, b, :], src[:, b, :])
    last.then_inc(sem["summed"], 1)
    dve.wait_ge(sem["summed"], n + 1)
    for c in range(4):
        b = 4 * half + c
        last = dve.bn_aggr(stats.mean_var[:, b, :], stats.six[:, b, :])
    last.then_inc(sem["aggregated"], 1)
    dve.wait_ge(sem["aggregated"], n + 1)
    r = slice(4 * half, 4 * half + 4)
    dve.tensor_scalar(stats.shifted[:, r], stats.mean_var[:, r, 1], eps, None, ALU.add).then_inc(sem["shifted"], 1)
    dve.wait_ge(sem["inverted"], n + 1)
    for c in range(4):
        b = 4 * half + c
        dve.tensor_scalar(dst[:, b, :], src[:, b, :], stats.mean_var[:, b, 0:1], stats.inverse[:, b:b + 1],
                          ALU.subtract, ALU.mult).then_inc(sem["normed"], 1)


def invert_half_pool(pool, k, stats, half, n):
    r = slice(4 * half, 4 * half + 4)
    pool.wait_ge(k.stat_sem["shifted"], n + 1)
    pool.tensor_tensor(stats.inverse[:, r], stats.shifted[:, r], k.minus_half[0:L, 0:4], ALU.pow
                       ).then_inc(k.stat_sem["inverted"], 1)


def norm_stats(nc, ctx, name):
    def sb(what, shape):
        return ctx.enter_context(nc.sbuf_tensor(f"{name}_{what}", shape, F32))
    stats = Shared()
    stats.six = sb("six", [L, B, 6])
    stats.mean_var = sb("mean_var", [L, B, 2])
    stats.shifted = sb("shifted", [L, B])
    stats.inverse = sb("inverse", [L, B])
    return stats


def norm_features(nc, k, ctx, name, dst, scale, offset, eps, loads=(), add_row=None):
    with ExitStack() as own:
        own.callback(k.sems.end_phase)
        stats = norm_stats(nc, own, name)
        N = own.enter_context(nc.sbuf_tensor(f"{name}_N", [L, B, D], F32))
        tiles = Tiles(k, name, psum_banks(nc, own, f"{name}_ps", 8), [("T", 2 * KT, "ad")])
        n0 = k.norms
        k.norms += HALVES
        loaded = k.sems.take(f"{name}_loaded")
        row = own.enter_context(nc.sbuf_tensor(f"{name}_row", [L, D], F32)) if add_row is not None else None
        n_loads = len(loads) + (row is not None)
        block = own.enter_context(nc.Block())

        @block.sync
        def _(sp):
            if row is not None:
                sp.dma_start(row[:], add_row.partition_broadcast(L)).then_inc(loaded, 16)
            for out, in_ in loads:
                with nc.allow_non_contiguous_dma("a column"):
                    sp.dma_start(out, in_).then_inc(loaded, 16)
            if n_loads:
                sp.wait_ge(loaded, 16 * n_loads)

        @block.gpsimd
        def _(pool):
            k.sems.clear_ended(pool)
            for half in range(HALVES):
                invert_half_pool(pool, k, stats, half, n0 + half)
            if row is not None:
                pool.wait_ge(loaded, 16 * n_loads)
                for b in range(B):
                    pool.wait_ge(k.stat_sem["normed"], 4 * n0 + b + 1)
                    pool.tensor_tensor(k.X[:, b, :], k.X[:, b, :], row[:], ALU.add)

        @block.tensor
        def _(pe):
            turn_tokens(pe, k, tiles, "T", N, lambda b: pe.wait_ge(k.stat_sem["normed"], 4 * n0 + b + 1))

        def batches(ap):
            return ap.rearrange("p (b l) -> p b l", b=4)

        @block.scalar
        def _(act):
            for j in tiles.mine("a", "T"):
                half, t = divmod(j, KT)
                tiles.wait_filled(act, "T", j)
                act.activation(dst(t, half), batches(tiles.bank("T", j)[:, 0:HALF]), ACT.Identity,
                               bias=column(k, offset, t), scale=column(k, scale, t)).then_inc(tiles.emptied["a"], 1)

        @block.vector
        def _(dve):
            for half in range(HALVES):
                norm_half_dve(dve, k, k.X, N, stats, eps, half, n0 + half)
            for j in tiles.mine("d", "T"):
                half, t = divmod(j, KT)
                tiles.wait_filled(dve, "T", j)
                dve.tensor_scalar(dst(t, half), batches(tiles.bank("T", j)[:, 0:HALF]), column(k, scale, t),
                                  column(k, offset, t), ALU.mult, ALU.add).then_inc(tiles.emptied["d"], 1)


def load_features(sp, dst, src, sem):
    sp.dma_start(dst[:], src.rearrange("(k p) n -> p k n", p=P)).then_inc(sem, 16)


def mlp(nc, k, ctx, name, hT, w1, w2, bias1, func):
    with ExitStack() as own:
        own.callback(k.sems.end_phase)
        w1_sb = own.enter_context(nc.sbuf_tensor(f"{name}_w1", [P, KT, F_MLP], F32))
        w2_sb = own.enter_context(nc.sbuf_tensor(f"{name}_w2", [P, FT, D], F32))
        gT = own.enter_context(nc.sbuf_tensor(f"{name}_gT", [P, FT, B * L], F32))
        tiles = Tiles(k, name, psum_banks(nc, own, f"{name}_ps", 8),
                      [("up", HALVES * FT, "a"), ("down", B, "d")])
        loaded1 = [k.sems.take(f"{name}_loaded1_{t}") for t in range(KT)]
        loaded2 = k.sems.take(f"{name}_loaded2")
        block = own.enter_context(nc.Block())

        @block.sync
        def _(sp):
            for t in range(KT):
                sp.dma_start(w1_sb[:, t, :], w1[t * P:(t + 1) * P, :]).then_inc(loaded1[t], 16)
            load_features(sp, w2_sb, w2, loaded2)

        @block.gpsimd
        def _(pool):
            k.sems.clear_ended(pool)

        @block.tensor
        def _(pe):
            for half in range(HALVES):
                for f in range(FT):
                    j = half * FT + f
                    tiles.wait_free(pe, "up", j)
                    for t in range(KT):
                        if j == 0:
                            pe.wait_ge(loaded1[t], 16)
                        mm = pe.matmul(tiles.bank("up", j)[:, 0:HALF], w1_sb[:, t, f * P:(f + 1) * P],
                                       half_tokens(hT, t, half), start=(t == 0), stop=(t == KT - 1))
                    mm.then_inc(tiles.filled, 1)
            pe.wait_ge(loaded2, 16)
            project_tokens(pe, tiles, "down", gT, w2_sb, FT,
                           lambda b: tiles.wait_out(pe, "up", range((b // 4) * FT, (b // 4 + 1) * FT)))

        @block.scalar
        def _(act):
            for half in range(HALVES):
                for f in range(FT):
                    j = half * FT + f
                    tiles.wait_filled(act, "up", j)
                    act.activation(half_tokens(gT, f, half), tiles.bank("up", j)[:, 0:HALF], func,
                                   bias=column(k, bias1, f)).then_inc(tiles.emptied["a"], 1)

        @block.vector
        def _(dve):
            for b in range(B):
                tiles.wait_filled(dve, "down", b)
                dve.tensor_tensor(k.X[:, b, :], k.X[:, b, :], tiles.bank("down", b)[0:L, :], ALU.add
                                  ).then_inc(tiles.emptied["d"], 1)


def layer0_output(nc, k, ins, ctx, hT):
    with ExitStack() as own:
        own.callback(k.sems.end_phase)
        def sb(name, shape):
            return own.enter_context(nc.sbuf_tensor(name, shape, F32))

        out_w = sb("out_w", [P, KT, D])
        out_b = sb("out_b", [L, D])
        mlp_b2 = sb("mlp_b2", [L, D])
        attT = sb("attT", [P, KT, B * L])
        Y = sb("Y", [L, B, D])
        square = sb("square", [L, D])
        sum_squares = sb("sum_squares", [L, B])
        mean_square = sb("mean_square", [L, B])
        inverse = sb("inverse", [L, B])
        tiles = Tiles(k, "l0o", psum_banks(nc, own, "l0o_ps", 8),
                      [("attT", 2 * KT, "ad"), ("out", B, "d"), ("hT", 2 * KT, "ad")])
        loaded = k.sems.take("l0o_loaded")
        residual = k.sems.take("l0o_residual")
        squared = k.sems.take("l0o_squared")
        meaned = k.sems.take("l0o_meaned")
        inverted = k.sems.take("l0o_inverted")
        normed = k.sems.take("l0o_normed")
        block = own.enter_context(nc.Block())

        @block.sync
        def _(sp):
            load_features(sp, out_w, ins["L0_xattn_out_w"], loaded)
            sp.dma_start(out_b[:], ins["L0_xattn_out_b"].partition_broadcast(L)).then_inc(loaded, 16)
            sp.dma_start(mlp_b2[:], ins["L0_xattn_mlp_b2"].partition_broadcast(L)).then_inc(loaded, 16)

        @block.tensor
        def _(pe):
            turn_tokens(pe, k, tiles, "attT", k.ATT, lambda b: None)
            pe.wait_ge(loaded, 48)
            project_tokens(pe, tiles, "out", attT, out_w, KT,
                           lambda b: tiles.wait_out(pe, "attT", range((b // 4) * KT, (b // 4 + 1) * KT)))
            turn_tokens(pe, k, tiles, "hT", Y, lambda b: pe.wait_ge(normed, b + 1))

        @block.gpsimd
        def _(pool):
            k.sems.clear_ended(pool)
            pool.wait_ge(loaded, 48)
            for b in range(B):
                pool.tensor_tensor(Y[:, b, :], k.X[:, b, :], out_b[:], ALU.add).then_inc(residual, 1)
            for half in range(HALVES):
                r = slice(4 * half, 4 * half + 4)
                pool.wait_ge(meaned, half + 1)
                pool.tensor_tensor(inverse[:, r], mean_square[:, r], k.minus_half[0:L, 0:4], ALU.pow
                                   ).then_inc(inverted, 1)
            for b in range(B):
                pool.wait_ge(residual, b + 1)
                pool.tensor_tensor(k.X[:, b, :], k.X[:, b, :], mlp_b2[:], ALU.add)

        @block.scalar
        def _(act):
            for j in tiles.mine("a", "attT"):
                tiles.wait_filled(act, "attT", j)
                act.activation(half_tokens(attT, j % KT, j // KT), tiles.bank("attT", j)[:, 0:HALF], ACT.Copy
                               ).then_inc(tiles.emptied["a"], 1)
            for b in range(B):
                tiles.wait_out(act, "out", [b])
                if b:
                    act.wait_ge(squared, b)
                act.activation(square[:], Y[:, b, :], ACT.Square, accum_out=sum_squares[:, b:b + 1]
                               ).then_inc(squared, 1)
            for j in tiles.mine("a", "hT"):
                tiles.wait_filled(act, "hT", j)
                act.activation(half_tokens(hT, j % KT, j // KT), tiles.bank("hT", j)[:, 0:HALF], ACT.Copy,
                               scale=column(k, "L0_xattn_postnorm_w", j % KT)).then_inc(tiles.emptied["a"], 1)

        @block.vector
        def _(dve):
            for j in tiles.mine("d", "attT"):
                tiles.wait_filled(dve, "attT", j)
                dve.tensor_copy(half_tokens(attT, j % KT, j // KT), tiles.bank("attT", j)[:, 0:HALF]
                                ).then_inc(tiles.emptied["d"], 1)
            for half in range(HALVES):
                for c in range(4):
                    b = 4 * half + c
                    tiles.wait_filled(dve, "out", b)
                    dve.wait_ge(residual, b + 1)
                    dve.tensor_tensor(Y[:, b, :], Y[:, b, :], tiles.bank("out", b)[0:L, :], ALU.add
                                      ).then_inc(tiles.emptied["d"], 1)
                r = slice(4 * half, 4 * half + 4)
                dve.wait_ge(squared, 4 * half + 4)
                dve.tensor_scalar(mean_square[:, r], sum_squares[:, r], 1.0 / D, 1e-6, ALU.mult, ALU.add
                                  ).then_inc(meaned, 1)
                dve.wait_ge(inverted, half + 1)
                for c in range(4):
                    b = 4 * half + c
                    dve.tensor_scalar(Y[:, b, :], Y[:, b, :], inverse[:, b:b + 1], None, ALU.mult
                                      ).then_inc(normed, 1)
            for j in tiles.mine("d", "hT"):
                tiles.wait_filled(dve, "hT", j)
                dve.tensor_scalar(half_tokens(hT, j % KT, j // KT), tiles.bank("hT", j)[:, 0:HALF],
                                  column(k, "L0_xattn_postnorm_w", j % KT), None, ALU.mult
                                  ).then_inc(tiles.emptied["d"], 1)


H1, N1 = 32, 16
F_MIX = 32
BRANCHES = ("w", "k", "v", "r", "g")
L_DECAY = 64
PREV = L + 1


def prev_tokens(t, tile, half, first):
    return t[:, tile, 4 * half:4 * half + 4, first:first + L]


def by_batch(ap):
    return ap.rearrange("p (b l) -> p b l", l=L)


def turn_weight(pe, k, tiles, stage, src, ready):
    for t in range(KT):
        tiles.wait_free(pe, stage, t)
        if t == 0:
            ready()
        for m in range(KT):
            mm = pe.transpose(tiles.bank(stage, t)[:, m * P:(m + 1) * P], src[:, m, t * P:(t + 1) * P], k.ident[:])
        mm.then_inc(tiles.filled, 1)


def copy_weight(tiles, engine, eng, stage, dst):
    for t in tiles.mine(engine, stage):
        tiles.wait_filled(eng, stage, t)
        if engine == "a":
            eng.activation(dst[:, t, :], tiles.bank(stage, t)[:], ACT.Copy).then_inc(tiles.emptied["a"], 1)
        else:
            eng.tensor_copy(dst[:, t, :], tiles.bank(stage, t)[:]).then_inc(tiles.emptied["d"], 1)


def project_features(pe, tiles, stage, weights, src, n_k, ready=None, rows=None):
    for m in range(KT):
        for half in range(HALVES):
            j = m * HALVES + half
            tiles.wait_free(pe, stage, j)
            if ready is not None:
                ready(j)
            for t in range(n_k):
                mm = pe.matmul(tiles.bank(stage, j)[:, 0:HALF], weights(t, m), src(t, half),
                               start=(t == 0), stop=(t == n_k - 1))
            mm.then_inc(tiles.filled, 1)


def layer1_mixing(nc, k, ins, ctx, xa, T):
    with ExitStack() as own:
        own.callback(k.sems.end_phase)
        def sb(name, shape):
            return own.enter_context(nc.sbuf_tensor(name, shape, F32))

        def sem(name):
            return k.sems.take(name)

        sx = sb("sx", [P, KT, B * L])
        mixed = [sb(f"mixed{i}", [P, KT, B * L]) for i in range(2)]
        w1 = sb("maa_w1", [P, KT, 5 * F_MIX])
        w2 = sb("maa_w2", [P, 4, D])
        w2_last = sb("maa_w2_last", [F_MIX, D])
        t_four = sb("t_four", [P, B * L])
        t_last = sb("t_last", [F_MIX, B * L])
        dw1 = sb("decay_w1", [P, KT, L_DECAY])
        dw2 = sb("decay_w2", [L_DECAY, D])
        t_decay = sb("t_decay", [L_DECAY, B * L])
        natural = [sb(f"W_natural{i}", [P, KT, D]) for i in range(2)]
        turned = [sb(f"W_turned{i}", [P, KT, D]) for i in range(2)]
        stages = [("t", 4, "a")]
        for n, f in enumerate(BRANCHES):
            if f != "w":
                stages.append((f"W{f}", KT, "ad"))
            stages.append((f"mix_{f}", 2 * KT, "d"))
            if f == "w":
                stages += [("decay1", HALVES, "a"), ("decay2", 2 * KT, "a")]
            else:
                stages.append((f"out_{f}", 2 * KT, "a"))
        tiles = Tiles(k, "l1m", psum_banks(nc, own, "l1m_ps", 8), stages)
        zeroed = sem("l1m_zeroed")
        small = sem("l1m_small_loaded")
        W_loaded = {f: sem(f"l1m_W{f}_loaded") for f in BRANCHES[1:]}
        differed = sem("l1m_differed")
        first_mixed = sem("l1m_first_mixed")
        completed = sem("l1m_completed")
        exped = sem("l1m_exped")
        block = own.enter_context(nc.Block())

        @block.sync
        def _(sp):
            load_features(sp, w1, ins["L1_xattn_maa_w1"], small)
            sp.wait_ge(zeroed, 1)
            for f in range(4):
                sp.dma_start(w2[F_MIX * f:F_MIX * (f + 1), f, :], ins["L1_xattn_maa_w2"][f]).then_inc(small, 16)
            sp.dma_start(w2_last[:], ins["L1_xattn_maa_w2"][4]).then_inc(small, 16)
            load_features(sp, dw1, ins["L1_xattn_decay_w1"], small)
            sp.dma_start(dw2[:], ins["L1_xattn_decay_w2"]).then_inc(small, 16)
            for n, f in enumerate(BRANCHES[1:]):
                if n >= 2:
                    tiles.wait_out(sp, f"W{BRANCHES[n - 1]}")
                sp.dma_start(natural[n % 2][:], ins[f"L1_xattn_W{f}"].rearrange("(m p) i -> p m i", p=P)
                             ).then_inc(W_loaded[f], 16)

        @block.tensor
        def _(pe):
            pe.wait_ge(small, 16 * 8)
            for half in range(HALVES):
                for part in range(2):
                    j = 2 * half + part
                    tiles.wait_free(pe, "t", j)
                    for t in range(KT):
                        if j == 0:
                            pe.wait_ge(first_mixed, t + 1)
                        rows = slice(0, P) if part == 0 else slice(P, P + F_MIX)
                        n = rows.stop - rows.start
                        mm = pe.matmul(tiles.bank("t", j)[0:n, 0:HALF], w1[:, t, rows],
                                       half_tokens(mixed[0], t, half), start=(t == 0), stop=(t == KT - 1))
                    mm.then_inc(tiles.filled, 1)
            for n, f in enumerate(BRANCHES):
                W = n - 1
                if f != "w":
                    turn_weight(pe, k, tiles, f"W{f}", natural[W % 2], lambda: pe.wait_ge(W_loaded[f], 16))
                if n == 0:
                    tiles.wait_out(pe, "t")
                if n < 4:
                    project_features(pe, tiles, f"mix_{f}", lambda t, m: w2[:, n, m * P:(m + 1) * P],
                                     lambda t, half: t_four[:, half * HALF:(half + 1) * HALF], 1)
                else:
                    project_features(pe, tiles, f"mix_{f}", lambda t, m: w2_last[:, m * P:(m + 1) * P],
                                     lambda t, half: t_last[:, half * HALF:(half + 1) * HALF], 1)
                m_in = mixed[(n + 1) % 2]
                if f == "w":
                    for half in range(HALVES):
                        tiles.wait_free(pe, "decay1", half)
                        pe.wait_ge(completed, 2 * KT * (n + 1))
                        for t in range(KT):
                            mm = pe.matmul(tiles.bank("decay1", half)[0:L_DECAY, 0:HALF], dw1[:, t, :],
                                           half_tokens(m_in, t, half), start=(t == 0), stop=(t == KT - 1))
                        mm.then_inc(tiles.filled, 1)
                    tiles.wait_out(pe, "decay1")
                    project_features(pe, tiles, "decay2", lambda t, m: dw2[:, m * P:(m + 1) * P],
                                     lambda t, half: t_decay[:, half * HALF:(half + 1) * HALF], 1)
                else:
                    pe.wait_ge(completed, 2 * KT * (n + 1))
                    tiles.wait_out(pe, f"W{f}")
                    project_features(pe, tiles, f"out_{f}", lambda t, m: turned[W % 2][:, t, m * P:(m + 1) * P],
                                     lambda t, half: half_tokens(m_in, t, half), KT)

        @block.scalar
        def _(act):
            for half in range(HALVES):
                for part in range(2):
                    j = 2 * half + part
                    tiles.wait_filled(act, "t", j)
                    dst = t_four if part == 0 else t_last
                    n = P if part == 0 else F_MIX
                    act.activation(dst[:, half * HALF:(half + 1) * HALF], tiles.bank("t", j)[0:n, 0:HALF], ACT.Tanh
                                   ).then_inc(tiles.emptied["a"], 1)
            for n, f in enumerate(BRANCHES):
                if f == "w":
                    for half in range(HALVES):
                        tiles.wait_filled(act, "decay1", half)
                        act.activation(t_decay[:, half * HALF:(half + 1) * HALF],
                                       tiles.bank("decay1", half)[0:L_DECAY, 0:HALF], ACT.Tanh
                                       ).then_inc(tiles.emptied["a"], 1)
                    for j in range(2 * KT):
                        m, half = divmod(j, HALVES)
                        tiles.wait_filled(act, "decay2", j)
                        w = prev_tokens(T["w"], m, half, 1)
                        act.activation(w, by_batch(tiles.bank("decay2", j)[:, 0:HALF]), ACT.Exp,
                                       bias=column(k, "L1_xattn_time_decay", m)).then_inc(tiles.emptied["a"], 1)
                        tiles.wait_out(act, "decay2", [j])
                        act.activation(w, w, ACT.Exp, scale=-1.0)
                else:
                    copy_weight(tiles, "a", act, f"W{f}", turned[(n - 1) % 2])
                    for j in range(2 * KT):
                        m, half = divmod(j, HALVES)
                        tiles.wait_filled(act, f"out_{f}", j)
                        act.activation(half_tokens(T[f], m, half), tiles.bank(f"out_{f}", j)[:, 0:HALF],
                                       ACT.Silu if f == "g" else ACT.Copy).then_inc(tiles.emptied["a"], 1)

        @block.vector
        def _(dve):
            dve.memset(w2[:], 0.0).then_inc(zeroed, 1)
            dve.memset(T["w"][:, :, :, 0], 0.0)
            for t in range(KT):
                dve.tensor_tensor(by_batch(sx[:, t, :]), xa[:, t, :, 0:L], xa[:, t, :, 1:PREV], ALU.subtract
                                  ).then_inc(differed, 1)
            for t in range(KT):
                dve.wait_ge(differed, t + 1)
                dve.scalar_tensor_tensor(by_batch(mixed[0][:, t, :]), by_batch(sx[:, t, :]),
                                         column(k, "L1_xattn_maa_x", t), xa[:, t, :, 1:PREV], ALU.mult, ALU.add
                                         ).then_inc(first_mixed, 1)
            for n, f in enumerate(BRANCHES):
                if f != "w":
                    copy_weight(tiles, "d", dve, f"W{f}", turned[(n - 1) % 2])
                if n == 1:
                    tiles.wait_out(dve, "t")
                for j in range(2 * KT):
                    m, half = divmod(j, HALVES)
                    tiles.wait_filled(dve, f"mix_{f}", j)
                    if n >= 2 and j == 0:
                        back = BRANCHES[n - 2]
                        tiles.wait_filled(dve, "decay1" if back == "w" else f"out_{back}",
                                          (HALVES if back == "w" else 2 * KT) - 1)
                    dve.scalar_tensor_tensor(half_tokens(mixed[(n + 1) % 2], m, half),
                                             tiles.bank(f"mix_{f}", j)[:, 0:HALF], column(k, f"L1_xattn_maa_{f}", m),
                                             half_tokens(sx, m, half), ALU.add, ALU.mult
                                             ).then_inc(tiles.emptied["d"], 1)

        @block.gpsimd
        def _(pool):
            k.sems.clear_ended(pool)
            for n, f in enumerate(BRANCHES):
                for j in range(2 * KT):
                    m, half = divmod(j, HALVES)
                    tiles.wait_out(pool, f"mix_{f}", [j])
                    dst = by_batch(half_tokens(mixed[(n + 1) % 2], m, half))
                    pool.tensor_tensor(dst, dst, prev_tokens(xa, m, half, 1), ALU.add).then_inc(completed, 1)


def layer1_scan(nc, k, ins, ctx, T, yT):
    context = ins["ctx_2048"]
    with ExitStack() as own:
        own.callback(k.sems.end_phase)
        def sb(name, shape):
            return own.enter_context(nc.sbuf_tensor(name, shape, F32))

        def sem(name):
            return k.sems.take(name)

        start = sb("start_state", [P, KT, B, N1])
        spread = sb("spread", [P, N1, P])
        gather = sb("gather", [P, N1, P])
        rows = sb("row_in_head", [P, N1])
        kv = [sb(f"kv{i}", [P, B, PREV]) for i in range(2)]
        state = [sb(f"state{i}", [P, B, PREV]) for i in range(2)]
        rs = [sb(f"rs{i}", [P, B, L]) for i in range(2)]
        r_tile = sb("r_tile", [P, B * L])
        ps_v = [own.enter_context(nc.psum_tensor(f"ps_v{i}", [P, HALVES, 512], F32)) for i in range(2)]
        ps_y = [own.enter_context(nc.psum_tensor(f"ps_y{i}", [P, HALVES, 512], F32)) for i in range(2)]

        loaded = sem("l1s_loaded")
        built = sem("l1s_built")
        spreaded = sem("l1s_spread")
        started = sem("l1s_started")
        keyed = sem("l1s_keyed")
        scanned = sem("l1s_scanned")
        received = sem("l1s_received")
        gathered = sem("l1s_gathered")
        y_copied = sem("l1s_y_copied")
        r_copied = sem("l1s_r_copied")
        block = own.enter_context(nc.Block())

        @block.sync
        def _(sp):
            for b in range(B):
                src = context[b, 2:2 + N1, :].rearrange("r d -> (r d)").rearrange("(k p t) -> p k t", p=P, t=N1)
                with nc.allow_non_contiguous_dma("64-byte rows of the starting state"):
                    sp.dma_start(start[:, :, b, :], src).then_inc(loaded, 16)

        @block.gpsimd
        def _(pool):
            k.sems.clear_ended(pool)
            pool.sem_inc(received, 2 * N1)
            with pool.Fori(0, KT) as m:
                for t in range(N1):
                    if t == 0:
                        pool.wait_ge(r_copied, at(m, 1, 0))
                    pool.wait_ge(scanned, at(m, N1, t))
                    pool.wait_ge(gathered, at(m, N1, t - 2))
                    pool.tensor_tensor(rs[t % 2][:], by_batch(r_tile[:]),
                                       state[t % 2][:, :, 0:L], ALU.mult).then_inc(received, 1)

        @block.vector
        def _(dve):
            dve.sem_inc(keyed, 2 * N1)
            dve.sem_inc(scanned, 2 * N1)
            ident = k.ident[:].rearrange("p (h t) -> p h t", t=N1)
            dve.tensor_reduce(rows[:], k.ident[:].rearrange("p (h t) -> p t h", t=N1), AX.X, ALU.add)
            dve.tensor_reduce(k.head_of[:], ident, AX.X, ALU.add)
            dve.memset(gather[:], 0.0).then_inc(built, 1)
            dve.wait_ge(built, 1)
            dve.tensor_copy(k.same_head[:].rearrange("p (h t) -> p h t", t=N1),
                            k.head_of[:].unsqueeze(2).broadcast_to([P, P // N1, N1])).then_inc(built, 1)
            dve.wait_ge(built, 2)
            for t in range(N1):
                dve.tensor_scalar(spread[:, t, :], k.same_head[:], rows[:, t:t + 1], None, ALU.mult)
                last = dve.tensor_copy(gather[:, t, t:P:N1], k.same_head[:, t:P:N1])
            last.then_inc(built, 1)
            with dve.Fori(0, KT) as m:
                for t in range(N1 + 1):
                    if t < N1:
                        dve.wait_ge(spreaded, at(m, N1, t))
                        dve.wait_ge(scanned, at(m, N1, t - 2))
                        dve.tensor_tensor(
                            kv[t % 2][:, :, 1:PREV].rearrange("p (h b) l -> p h b l", h=HALVES),
                            ps_v[t % 2][:, :, 0:HALF].rearrange("p h (b l) -> p h b l", l=L),
                            T["k"][:, bass.ds(m, 1), :].squeeze(1).rearrange("p (h b l) -> p h b l", h=HALVES, l=L),
                            ALU.mult).then_inc(keyed, 1)
                    if t > 0:
                        u = t - 1
                        dve.wait_ge(keyed, at(m, N1, u))
                        dve.wait_ge(started, at(m, N1, u))
                        dve.wait_ge(received, at(m, N1, u - 2))
                        dve.tensor_tensor_scan(
                            state[u % 2][:].rearrange("p b l -> p (b l)"),
                            T["w"][:, bass.ds(m, 1), :, :].squeeze(1).rearrange("p b l -> p (b l)"),
                            kv[u % 2][:].rearrange("p b l -> p (b l)"), 0.0, ALU.mult, ALU.add).then_inc(scanned, 1)

        @block.scalar
        def _(act):
            act.sem_inc(started, 2 * N1)
            act.sem_inc(y_copied, 2)
            act.sem_inc(r_copied, 2)
            act.wait_ge(loaded, 16 * B)
            with act.Fori(0, KT) as m:
                act.wait_ge(received, at(m, N1, -1))
                act.activation(r_tile[:], T["r"][:, bass.ds(m, 1), :].squeeze(1), ACT.Copy).then_inc(r_copied, 1)
                for t in range(N1):
                    act.wait_ge(scanned, at(m, N1, t - 2))
                    act.activation(kv[t % 2][:, :, 0], start[:, bass.ds(m, 1), :, t].squeeze(1), ACT.Copy
                                   ).then_inc(started, 1)
                act.wait_ge(gathered, at(m, N1, N1 - 1))
                act.activation(yT[:, bass.ds(m, 1), :].squeeze(1).rearrange("p (h n) -> p h n", h=HALVES),
                               ps_y[0][:, :, 0:HALF], ACT.Copy).then_inc(y_copied, 1)

        @block.tensor
        def _(pe):
            pe.sem_inc(spreaded, 2 * N1)
            pe.sem_inc(gathered, 2 * N1)
            pe.wait_ge(built, 3)
            with pe.Fori(0, KT) as m:
                for t in range(N1 + 2):
                    if t < N1:
                        pe.wait_ge(keyed, at(m, N1, t - 2))
                        for half in range(HALVES):
                            mm = pe.matmul(ps_v[t % 2][:, half, 0:HALF], spread[:, t, :],
                                           T["v"][:, bass.ds(m, 1), half * HALF:(half + 1) * HALF].squeeze(1),
                                           start=True, stop=True)
                        mm.then_inc(spreaded, 1)
                    if t >= 2:
                        u = t - 2
                        pe.wait_ge(received, at(m, N1, u))
                        if u == 0:
                            pe.wait_ge(y_copied, at(m, 1, -1))
                        for half in range(HALVES):
                            mm = pe.matmul(ps_y[0][:, half, 0:HALF], gather[:, u, :],
                                           rs[u % 2][:].rearrange("p b l -> p (b l)")[:, half * HALF:(half + 1) * HALF],
                                           start=(u == 0), stop=(u == N1 - 1))
                        mm.then_inc(gathered, 1)


def layer1_output(nc, k, ins, ctx, T, yT):
    with ExitStack() as own:
        own.callback(k.sems.end_phase)
        def sb(name, shape):
            return own.enter_context(nc.sbuf_tensor(name, shape, F32))

        def sem(name):
            return k.sems.take(name)

        natural = sb("Wo_natural", [P, KT, D])
        turned = sb("Wo_turned", [P, KT, D])
        head_mean = sb("head_mean", [P, P])
        own_key = sb("own_key", [P, KT, B * L])
        square = sb("y_square", [P, KT, B * L])
        tiles = Tiles(k, "l1o", psum_banks(nc, own, "l1o_ps", 8),
                      [("Wo", KT, "a"), ("own", 2 * KT, "d"), ("mean", 2 * KT, "d"), ("var", 2 * KT, "a"),
                       ("out", B, "d")])
        loaded = sem("l1o_loaded")
        built = sem("l1o_built")
        keyed = sem("l1o_keyed")
        added = sem("l1o_added")
        squared = sem("l1o_squared")
        inverted = sem("l1o_inverted")
        scaled = sem("l1o_scaled")
        block = own.enter_context(nc.Block())

        def tile_of(t, j):
            return half_tokens(t, j // HALVES, j % HALVES)

        @block.sync
        def _(sp):
            sp.dma_start(natural[:], ins["L1_xattn_Wo"].rearrange("(m p) i -> p m i", p=P)).then_inc(loaded, 16)

        @block.tensor
        def _(pe):
            turn_weight(pe, k, tiles, "Wo", natural, lambda: pe.wait_ge(loaded, 16))
            for stage, weights, src, ready in (
                    ("own", k.same_head, own_key, lambda j: pe.wait_ge(keyed, KT + j // HALVES + 1)),
                    ("mean", head_mean, yT, lambda j: pe.wait_ge(added, j + 1)),
                    ("var", head_mean, square, lambda j: pe.wait_ge(squared, j + 1))):
                for j in range(2 * KT):
                    tiles.wait_free(pe, stage, j)
                    ready(j)
                    pe.matmul(tiles.bank(stage, j)[:, 0:HALF], weights[:], tile_of(src, j), start=True, stop=True
                              ).then_inc(tiles.filled, 1)
            pe.wait_ge(scaled, 3 * 2 * KT)
            tiles.wait_out(pe, "Wo")
            project_tokens(pe, tiles, "out", yT, turned, KT)

        @block.scalar
        def _(act):
            copy_weight(tiles, "a", act, "Wo", turned)
            for j in range(2 * KT):
                tiles.wait_out(act, "mean", [j])
                act.activation(tile_of(square, j), tile_of(yT, j), ACT.Square).then_inc(squared, 1)
            for j in range(2 * KT):
                tiles.wait_filled(act, "var", j)
                act.activation(tile_of(own_key, j), tiles.bank("var", j)[:, 0:HALF], ACT.Sqrt, bias=k.eps5[:]
                               ).then_inc(tiles.emptied["a"], 1)

        @block.gpsimd
        def _(pool):
            k.sems.clear_ended(pool)
            for j in range(2 * KT):
                tiles.wait_out(pool, "own", [j])
                pool.tensor_tensor(tile_of(yT, j), tile_of(yT, j), tile_of(square, j), ALU.add).then_inc(added, 1)

        @block.vector
        def _(dve):
            dve.tensor_scalar(head_mean[:], k.same_head[:], 1.0 / N1, None, ALU.mult).then_inc(built, 1)
            for t in range(KT):
                dve.scalar_tensor_tensor(own_key[:, t, :], T["r"][:, t, :], column(k, "L1_xattn_faaaa", t),
                                         T["k"][:, t, :], ALU.mult, ALU.mult).then_inc(keyed, 1)
            dve.wait_ge(keyed, KT)
            dve.wait_ge(built, 1)
            dve.sem_inc(keyed, KT)
            for j in range(2 * KT):
                tiles.wait_filled(dve, "own", j)
                dve.tensor_tensor(tile_of(square, j), tiles.bank("own", j)[:, 0:HALF], tile_of(T["v"], j), ALU.mult
                                  ).then_inc(tiles.emptied["d"], 1)
            for j in range(2 * KT):
                tiles.wait_filled(dve, "mean", j)
                dve.tensor_tensor(tile_of(yT, j), tile_of(yT, j), tiles.bank("mean", j)[:, 0:HALF], ALU.subtract
                                  ).then_inc(tiles.emptied["d"], 1)
            for j in range(2 * KT):
                tiles.wait_out(dve, "var", [j])
                dve.reciprocal(tile_of(square, j), tile_of(own_key, j)).then_inc(inverted, 1)
                dve.wait_ge(inverted, j + 1)
                dve.tensor_tensor(tile_of(yT, j), tile_of(yT, j), tile_of(square, j), ALU.mult).then_inc(scaled, 1)
                dve.wait_ge(scaled, 3 * j + 1)
                m = j // HALVES
                dve.tensor_scalar(tile_of(yT, j), tile_of(yT, j), column(k, "L1_xattn_gn_w", m),
                                  column(k, "L1_xattn_gn_b", m), ALU.mult, ALU.add).then_inc(scaled, 1)
                dve.wait_ge(scaled, 3 * j + 2)
                dve.tensor_tensor(tile_of(yT, j), tile_of(yT, j), tile_of(T["g"], j), ALU.mult).then_inc(scaled, 1)
            for b in range(B):
                tiles.wait_filled(dve, "out", b)
                dve.tensor_tensor(k.X[:, b, :], k.X[:, b, :], tiles.bank("out", b)[0:L, :], ALU.add
                                  ).then_inc(tiles.emptied["d"], 1)


def layer1_channel_mix(nc, k, ins, ctx, xc):
    with ExitStack() as own:
        own.callback(k.sems.end_phase)
        def sb(name, shape):
            return own.enter_context(nc.sbuf_tensor(name, shape, F32))

        def sem(name):
            return k.sems.take(name)

        names = ("fWk", "fWr", "fWv")
        natural = {n: sb(f"{n}_natural", [P, KT, D]) for n in names}
        turned = {n: sb(f"{n}_turned", [P, KT, D]) for n in names}
        sx = sb("sxc", [P, KT, B * L])
        xk = sb("xk", [P, KT, B * L])
        xr = sb("xr", [P, KT, B * L])
        kk = sb("kk", [P, KT, B * L])
        rr = sb("rr", [L, B, D])
        tiles = Tiles(k, "l1c", psum_banks(nc, own, "l1c_ps", 8),
                      [(n, KT, "ad") for n in names] + [("kk", 2 * KT, "a"), ("rr", B, "a"), ("out", B, "d")])
        loaded = {n: sem(f"l1c_{n}_loaded") for n in names}
        differed = sem("l1c_differed")
        mixed = sem("l1c_mixed")
        squared = sem("l1c_squared")
        block = own.enter_context(nc.Block())

        @block.sync
        def _(sp):
            for n in names:
                sp.dma_start(natural[n][:], ins[f"L1_xattn_{n}"].rearrange("(m p) i -> p m i", p=P)
                             ).then_inc(loaded[n], 16)

        @block.tensor
        def _(pe):
            for n in names:
                turn_weight(pe, k, tiles, n, natural[n], lambda: pe.wait_ge(loaded[n], 16))
            tiles.wait_out(pe, "fWk")
            pe.wait_ge(mixed, KT)
            project_features(pe, tiles, "kk", lambda t, m: turned["fWk"][:, t, m * P:(m + 1) * P],
                             lambda t, half: half_tokens(xk, t, half), KT)
            tiles.wait_out(pe, "fWr")
            tiles.wait_out(pe, "fWv")
            pe.wait_ge(mixed, 2 * KT)
            project_tokens(pe, tiles, "rr", xr, turned["fWr"], KT)
            pe.wait_ge(squared, 2 * KT)
            project_tokens(pe, tiles, "out", kk, turned["fWv"], KT)

        @block.scalar
        def _(act):
            for n in names:
                copy_weight(tiles, "a", act, n, turned[n])
            for j in range(2 * KT):
                tiles.wait_filled(act, "kk", j)
                act.activation(half_tokens(kk, j // HALVES, j % HALVES), tiles.bank("kk", j)[:, 0:HALF], ACT.Relu
                               ).then_inc(tiles.emptied["a"], 1)
            for b in range(B):
                tiles.wait_filled(act, "rr", b)
                act.activation(rr[:, b, :], tiles.bank("rr", b)[0:L, :], ACT.Sigmoid).then_inc(tiles.emptied["a"], 1)

        @block.gpsimd
        def _(pool):
            k.sems.clear_ended(pool)
            for j in range(2 * KT):
                tiles.wait_out(pool, "kk", [j])
                t = half_tokens(kk, j // HALVES, j % HALVES)
                pool.tensor_tensor(t, t, t, ALU.mult).then_inc(squared, 1)
            for b in range(B):
                tiles.wait_out(pool, "out", [b])
                pool.tensor_tensor(k.X[:, b, :], k.X[:, b, :], rr[:, b, :], ALU.add)

        @block.vector
        def _(dve):
            copy = lambda n: copy_weight(tiles, "d", dve, n, turned[n])
            for t in range(KT):
                dve.tensor_tensor(by_batch(sx[:, t, :]), xc[:, t, :, 0:L], xc[:, t, :, 1:PREV], ALU.subtract
                                  ).then_inc(differed, 1)
            copy("fWk")
            dve.wait_ge(differed, KT)
            for dst, mix in ((xk, "L1_xattn_fmaa_k"), (xr, "L1_xattn_fmaa_r")):
                for t in range(KT):
                    dve.scalar_tensor_tensor(by_batch(dst[:, t, :]), by_batch(sx[:, t, :]), column(k, mix, t),
                                             xc[:, t, :, 1:PREV], ALU.mult, ALU.add).then_inc(mixed, 1)
            copy("fWr")
            copy("fWv")
            for b in range(B):
                tiles.wait_filled(dve, "out", b)
                tiles.wait_out(dve, "rr", [b])
                dve.tensor_tensor(rr[:, b, :], rr[:, b, :], tiles.bank("out", b)[0:L, :], ALU.mult
                                  ).then_inc(tiles.emptied["d"], 1)


def layer1(nc, k, ins, ctx):
    with ExitStack() as own:
        def sb(name, shape):
            return own.enter_context(nc.sbuf_tensor(name, shape, F32))

        k.same_head = sb("same_head", [P, P])
        T = {f: sb(f"T_{f}", [P, KT, B * L]) for f in "rkvg"}
        T["w"] = sb("T_w", [P, KT, B, PREV])
        with ExitStack() as inner:
            xa = inner.enter_context(nc.sbuf_tensor("xa", [P, KT, B, PREV], F32))
            norm_features(nc, k, ctx, "ln1", lambda t, half: prev_tokens(xa, t, half, 1),
                          "L1_xattn_ln1_w", "L1_xattn_ln1_b", 1e-5,
                          loads=[(xa[:, t, :, 0:1], k.ctxT[:, :, t, 1:2].rearrange("b p s -> p b s")) for t in range(KT)])
            layer1_mixing(nc, k, ins, ctx, xa, T)
        yT = sb("yT", [P, KT, B * L])
        layer1_scan(nc, k, ins, ctx, T, yT)
        layer1_output(nc, k, ins, ctx, T, yT)
    with ExitStack() as own:
        xc = own.enter_context(nc.sbuf_tensor("xc", [P, KT, B, PREV], F32))
        norm_features(nc, k, ctx, "ln2", lambda t, half: prev_tokens(xc, t, half, 1),
                      "L1_xattn_ln2_w", "L1_xattn_ln2_b", 1e-5,
                      loads=[(xc[:, t, :, 0:1], k.ctxT[:, :, t, 0:1].rearrange("b p s -> p b s")) for t in range(KT)])
        layer1_channel_mix(nc, k, ins, ctx, xc)



H2, DH2 = 16, 128
G2 = 8
N_GROUPS = H2 // G2
T2 = 121
NT2 = 3
N2 = T2 * NT2
WINDOW = 115
WINDOWS = [(first, min(WINDOW, G2 * L - first)) for first in range(0, G2 * L, WINDOW)]
NW = len(WINDOWS)


def layer2_attention(nc, k, ins, ctx, layer, hT):
    w = {n: ins[f"L2_xattn_{n}{layer}"] for n in ("wq", "wk", "wv", "wo")}
    context = ins["ctx_2048"]
    W = G2 * DH2
    scale = DH2 ** -0.5
    with ExitStack() as own:
        own.callback(k.sems.end_phase)
        def sb(name, shape):
            return own.enter_context(nc.sbuf_tensor(f"{name}_layer{layer}", shape, F32))

        def sem(name):
            return k.sems.take(f"{name}_layer{layer}")

        wq = sb("wq", [P, KT, W])
        wk = sb("wk", [P, KT, W])
        wkT = sb("wkT", [P, G2, D])
        wv = sb("wv", [P, KT, W])
        wo = sb("wo", [P, G2, D])
        key_bias = sb("key_bias", [P, H2])
        group_key_bias = sb("group_key_bias", [P, G2])
        value_bias = sb("value_bias", [1, H2 * DH2])
        value_b = sb("value_b", [1, H2 * DH2])
        group_value_bias = sb("group_value_bias", [1, W])
        cT = [sb(f"cT{s}", [P, KT, S]) for s in range(2)]
        c = [sb(f"c{s}", [T2, NT2, D]) for s in range(2)]
        qT = sb("qT", [P, G2 * L])
        G = sb("G", [P, KT, G2 * L])
        learned = sb("learned", [1, G2 * L])
        probs = [sb(f"p{i}", [WINDOW, N2]) for i in range(4)]
        probsT = sb("pT", [T2, NT2, G2 * L])
        Z = sb("Z", [P, KT, G2 * L])
        oT = sb("oT", [P, G2 * L])
        neg_max = [sb(f"neg_max2_{s}", [WINDOW, NW]) for s in range(2)]
        sums = [sb(f"sums2_{s}", [WINDOW, NW]) for s in range(2)]
        inverse = sb("inverse2", [WINDOW, NW])

        work = psum_banks(nc, own, f"work2_{layer}_", 3)
        ps_scores = psum_banks(nc, own, f"scores2_{layer}_", 2)
        ps_turned = psum_banks(nc, own, f"turned2_{layer}_", 2)
        spare = psum_banks(nc, own, f"spare2_{layer}_", 1)[0]

        TILES = 21
        G_AT, Z_AT, O_AT, OUT_AT = 2, 10, 18, 20
        ACT_TILES = [*range(G_AT, G_AT + 8), *range(Z_AT, Z_AT + 8, 2)]
        DVE_TILES = [j for j in range(TILES) if j not in ACT_TILES]

        bias_loaded = sem("bias_loaded2")
        zeroed = sem("zeroed2")
        W_loaded = {n: sem(f"{n}_loaded2") for n in w}
        cT_loaded = [sem(f"cT_loaded{s}") for s in range(2)]
        c_loaded = [sem(f"c_loaded{s}") for s in range(2)]
        biased = sem("biased2")
        grouped = sem("grouped2")
        wk_turned = sem("wk_turned")
        wkT_copied = sem("wkT_copied")
        tile_done = sem("tile_done2")
        act_copied = sem("act_copied2")
        dve_copied = sem("dve_copied2")
        learned_done = sem("learned_done")
        learned_copied = sem("learned_copied")
        scored = sem("scored2")
        maxed = sem("maxed2")
        exped = sem("exped2")
        inverted = sem("inverted2")
        scaled = sem("scaled2")
        turned = sem("turned2")
        turned_copied = sem("turned_copied2")

        def wait_copied(eng, g, tile):
            if tile < 0:
                g, tile = g - 1, tile + TILES
            if tile in ACT_TILES:
                eng.wait_ge(act_copied, at(g, len(ACT_TILES), ACT_TILES.index(tile)))
            else:
                eng.wait_ge(dve_copied, at(g, len(DVE_TILES), DVE_TILES.index(tile)))

        def bank(tile):
            return work[tile % 3]

        def half_cols(ap, half):
            return ap[..., half * HALF:(half + 1) * HALF]

        block = own.enter_context(nc.Block())

        @block.sync
        def _(sp):
            sp.dma_start(value_bias[:], ins[f"L2_xattn_bias_v{layer}"].rearrange("a b h d -> (a b) (h d)")
                         ).then_inc(bias_loaded, 16)
            sp.dma_start(value_b[:], ins[f"L2_xattn_bv{layer}"].rearrange("(a n) -> a n", a=1)
                         ).then_inc(bias_loaded, 16)
            sp.wait_ge(zeroed, 1)
            with sp.Fori(0, N_GROUPS) as group:
                cols = bass.ds(group * W, W)
                sp.wait_ge(wk_turned, at(group, G2, G2 - 1, back=1))
                sp.dma_start(wk[:], w["wk"].rearrange("(k p) n -> p k n", p=P)[:, :, cols]).then_inc(W_loaded["wk"], 16)
                sp.wait_ge(tile_done, at(B * group - 1, TILES, G_AT - 1))
                sp.dma_start(wq[:], w["wq"].rearrange("(k p) n -> p k n", p=P)[:, :, cols]).then_inc(W_loaded["wq"], 16)
                with sp.Fori(0, B // 2) as i:
                    for s in range(2):
                        b = 2 * i + s
                        g = B * group + b
                        sp.wait_ge(scored, at(g, NW, NW - 1, back=2))
                        sp.dma_start(cT[s][:], k.ctxT[b]).then_inc(cT_loaded[s], 16)
                        sp.wait_ge(tile_done, at(g, TILES, O_AT - 1, back=2))
                        sp.dma_start(c[s][1:T2, 0, :], context[b, 0:T2 - 1, :]).then_inc(c_loaded[s], 16)
                        sp.dma_start(c[s][:, 1, :], context[b, T2 - 1:2 * T2 - 1, :]).then_inc(c_loaded[s], 16)
                        sp.dma_start(c[s][0:T2 - 1, 2, :], context[b, 2 * T2 - 1:S, :]).then_inc(c_loaded[s], 16)

        @block.gpsimd
        def _(pool):
            k.sems.clear_ended(pool)
            for s in range(2):
                pool.memset(c[s][:], 0.0)
            for i in range(4):
                last = pool.memset(probs[i][:, N2 - 1:N2], 0.0)
            last.then_inc(zeroed, 1)
            with pool.Fori(0, N_GROUPS) as group:
                pool.wait_ge(tile_done, at(B * group - 1, TILES, OUT_AT - 1))
                pool.dma_start(wv[:], w["wv"].rearrange("(k p) n -> p k n", p=P)[:, :, bass.ds(group * W, W)]
                               ).then_inc(W_loaded["wv"], 16)
                pool.wait_ge(tile_done, at(B * group - 1, TILES, OUT_AT))
                pool.dma_start(wo[:], w["wo"].rearrange("(h p) n -> p h n", p=P)[:, bass.ds(group * G2, G2), :]
                               ).then_inc(W_loaded["wo"], 16)

        @block.tensor
        def _(pe):
            pe.sem_inc(wk_turned, 2 * G2)
            pe.sem_inc(tile_done, 2 * TILES)
            pe.sem_inc(learned_done, 4)
            pe.sem_inc(scored, 2 * NW)
            pe.sem_inc(turned, 2 * NW)
            with pe.Fori(0, N_GROUPS) as group:
                pe.wait_ge(W_loaded["wk"], 16 * (group + 1))
                for h in range(G2):
                    if h == 0:
                        pe.wait_ge(learned_copied, at(B * group, 2, -1))
                    else:
                        pe.wait_ge(wkT_copied, at(group, G2, h - 1))
                    for t in range(KT):
                        mm = pe.transpose(spare[:, t * P:(t + 1) * P], wk[:, t, h * P:(h + 1) * P], k.ident[:])
                    mm.then_inc(wk_turned, 1)
                with pe.Fori(0, B // 2) as i:
                    for s in range(2):
                        b = 2 * i + s
                        g = B * group + b
                        pe.wait_ge(W_loaded["wq"], 16 * (group + 1))
                        for half in range(2):
                            wait_copied(pe, g, half - 3)
                            for h in range(4 * half, 4 * half + 4):
                                out = bank(half)[:, h % 4 * L:(h % 4 + 1) * L]
                                for t in range(KT):
                                    mm = pe.matmul(out, wq[:, t, h * P:(h + 1) * P], hT[:, t, bass.ds(b * L, L)],
                                                   start=(t == 0), stop=(t == KT - 1))
                            mm.then_inc(tile_done, 1)
                        pe.wait_ge(grouped, group + 1)
                        pe.wait_ge(wkT_copied, at(group, G2, G2 - 1))
                        for half in range(2):
                            wait_copied(pe, g, half)
                            pe.wait_ge(learned_copied, at(g, 2, half - 1))
                            for h in range(4 * half, 4 * half + 4):
                                mm = pe.matmul(spare[0:1, h % 4 * L:(h % 4 + 1) * L], group_key_bias[:, h:h + 1],
                                               qT[:, h * L:(h + 1) * L], start=True, stop=True)
                            mm.then_inc(learned_done, 1)
                        for half in range(2):
                            for t in range(KT):
                                tile = G_AT + 4 * half + t
                                wait_copied(pe, g, tile - 3)
                                for h in range(4 * half, 4 * half + 4):
                                    mm = pe.matmul(bank(tile)[:, h % 4 * L:(h % 4 + 1) * L],
                                                   wkT[:, h, t * P:(t + 1) * P], qT[:, h * L:(h + 1) * L],
                                                   start=True, stop=True)
                                mm.then_inc(tile_done, 1)

                        def scores(v):
                            first, n = WINDOWS[v]
                            out = ps_scores[(NW * s + v) % 2]
                            if v == 0:
                                pe.wait_ge(cT_loaded[s], 16 * ((B // 2) * group + i + 1))
                            half = (first + n - 1) // HALF
                            wait_copied(pe, g, G_AT + 4 * half + 3)
                            pe.wait_ge(learned_copied, at(g, 2, half))
                            pe.wait_ge(exped, at(g, NW, v - 2))
                            pe.matmul(out[0:n, 0:1], learned[0:1, first:first + n], k.ident[0:1, 0:1],
                                      start=True, stop=True)
                            for t in range(KT):
                                mm = pe.matmul(out[0:n, 1:1 + S], G[:, t, first:first + n], cT[s][:, t, :],
                                               start=(t == 0), stop=(t == KT - 1))
                            mm.then_inc(scored, 1)

                        def turn(v):
                            first, n = WINDOWS[v]
                            u = NW * s + v
                            pe.wait_ge(scaled, at(g, NW, v))
                            pe.wait_ge(turned_copied, at(g, NW, v - 2))
                            for j in range(NT2):
                                mm = pe.transpose(ps_turned[u % 2][0:T2, j * WINDOW:j * WINDOW + n],
                                                  probs[u % 4][0:n, j * T2:(j + 1) * T2], k.ident[0:n, 0:n])
                            mm.then_inc(turned, 1)

                        for v in range(NW + 2):
                            if v < NW:
                                scores(v)
                            if v >= 2:
                                turn(v - 2)
                        pe.wait_ge(c_loaded[s], 48 * ((B // 2) * group + i + 1))
                        for half in range(2):
                            last = max(v for v in range(NW) if WINDOWS[v][0] < (half + 1) * HALF)
                            pe.wait_ge(turned_copied, at(g, NW, last))
                            for t in range(KT):
                                tile = Z_AT + 4 * half + t
                                wait_copied(pe, g, tile - 3)
                                for j in range(NT2):
                                    mm = pe.matmul(bank(tile)[:, 0:HALF], c[s][:, j, t * P:(t + 1) * P],
                                                   half_cols(probsT[:, j, :], half), start=(j == 0), stop=(j == NT2 - 1))
                                mm.then_inc(tile_done, 1)
                        pe.wait_ge(W_loaded["wv"], 16 * (group + 1))
                        for half in range(2):
                            tile = O_AT + half
                            for z in range(4):
                                wait_copied(pe, g, Z_AT + 4 * half + z)
                            wait_copied(pe, g, tile - 3)
                            for h in range(4 * half, 4 * half + 4):
                                out = bank(tile)[:, h % 4 * L:(h % 4 + 1) * L]
                                pe.matmul(out, group_value_bias[0:1, h * P:(h + 1) * P],
                                          probsT[0:1, 0, h * L:(h + 1) * L], start=True, stop=False)
                                for t in range(KT):
                                    mm = pe.matmul(out, wv[:, t, h * P:(h + 1) * P], Z[:, t, h * L:(h + 1) * L],
                                                   start=False, stop=(t == KT - 1))
                            mm.then_inc(tile_done, 1)
                        pe.wait_ge(W_loaded["wo"], 16 * (group + 1))
                        wait_copied(pe, g, OUT_AT - 3)
                        wait_copied(pe, g, OUT_AT - 1)
                        for h in range(G2):
                            mm = pe.matmul(bank(OUT_AT)[0:L, :], oT[:, h * L:(h + 1) * L], wo[:, h, :],
                                           start=(h == 0), stop=(h == G2 - 1))
                        mm.then_inc(tile_done, 1)

        @block.scalar
        def _(act):
            act.sem_inc(wkT_copied, 2 * G2)
            act.sem_inc(act_copied, 2 * len(ACT_TILES))
            act.sem_inc(learned_copied, 4)
            act.sem_inc(exped, 2 * NW)
            act.sem_inc(turned_copied, 2 * NW)
            act.wait_ge(biased, 3)
            with act.Fori(0, N_GROUPS) as group:
                act.wait_ge(tile_done, at(B * group - 1, TILES, OUT_AT))
                act.activation(group_key_bias[:], key_bias[:, bass.ds(group * G2, G2)], ACT.Copy)
                act.activation(group_value_bias[:], value_bias[:, bass.ds(group * W, W)], ACT.Copy
                               ).then_inc(grouped, 1)
                for h in range(G2):
                    act.wait_ge(wk_turned, at(group, G2, h))
                    act.activation(wkT[:, h, :], spare[:], ACT.Copy, scale=scale).then_inc(wkT_copied, 1)
                with act.Fori(0, B // 2) as i:
                    for s in range(2):
                        g = B * group + 2 * i + s
                        for half in range(2):
                            act.wait_ge(learned_done, at(g, 2, half))
                            act.activation(half_cols(learned[:], half), spare[0:1, 0:HALF], ACT.Copy
                                           ).then_inc(learned_copied, 1)
                        for tile in range(G_AT, G_AT + 8):
                            half, t = divmod(tile - G_AT, KT)
                            act.wait_ge(tile_done, at(g, TILES, tile))
                            act.activation(half_cols(G[:, t, :], half), bank(tile)[:, 0:HALF], ACT.Copy
                                           ).then_inc(act_copied, 1)

                        def copy_turned(v):
                            first, n = WINDOWS[v]
                            u = NW * s + v
                            act.wait_ge(turned, at(g, NW, v))
                            src = ps_turned[u % 2][0:T2, 0:NT2 * WINDOW].rearrange("p (j n) -> p j n", j=NT2)
                            act.activation(probsT[:, :, first:first + n], src[:, :, 0:n], ACT.Copy
                                           ).then_inc(turned_copied, 1)

                        for v in range(NW + 2):
                            if v < NW:
                                _, n = WINDOWS[v]
                                u = NW * s + v
                                act.wait_ge(maxed, at(g, NW, v))
                                act.wait_ge(turned, at(g, NW, v - 4))
                                act.activation(probs[u % 4][0:n, 0:1 + S], ps_scores[u % 2][0:n, 0:1 + S], ACT.Exp,
                                               bias=neg_max[s][0:n, v:v + 1], accum_out=sums[s][0:n, v:v + 1]
                                               ).then_inc(exped, 1)
                            if v >= 2:
                                copy_turned(v - 2)
                        for tile in ACT_TILES[8:]:
                            half, t = divmod(tile - Z_AT, KT)
                            act.wait_ge(tile_done, at(g, TILES, tile))
                            act.activation(half_cols(Z[:, t, :], half), bank(tile)[:, 0:HALF], ACT.Copy
                                           ).then_inc(act_copied, 1)

        @block.vector
        def _(dve):
            dve.sem_inc(dve_copied, 2 * len(DVE_TILES))
            dve.sem_inc(maxed, 2 * NW)
            dve.sem_inc(inverted, 2 * NW)
            dve.sem_inc(scaled, 2 * NW)
            dve.tensor_tensor(key_bias[:], column(k, f"L2_xattn_bias_k{layer}", 0, H2),
                              column(k, f"L2_xattn_bk{layer}", 0, H2), ALU.subtract).then_inc(biased, 1)
            dve.wait_ge(biased, 1)
            dve.tensor_scalar(key_bias[:], key_bias[:], scale, None, ALU.mult).then_inc(biased, 1)
            dve.wait_ge(bias_loaded, 32)
            dve.tensor_tensor(value_bias[:], value_bias[:], value_b[:], ALU.subtract).then_inc(biased, 1)
            with dve.Fori(0, N_GROUPS) as group:
                with dve.Fori(0, B // 2) as i:
                    for s in range(2):
                        b = 2 * i + s
                        g = B * group + b

                        def biases(name, half):
                            tile, first, _ = PARAM_AT[name]
                            return k.params[:, tile, bass.ds(group * G2 + (first + 4 * half), 4)
                                            ].unsqueeze(2).broadcast_to([P, 4, L])

                        for half in range(2):
                            dve.wait_ge(tile_done, at(g, TILES, half))
                            dve.tensor_tensor(by_batch(half_cols(qT[:], half)), by_batch(bank(half)[:, 0:HALF]),
                                              biases(f"L2_xattn_bq{layer}", half), ALU.add).then_inc(dve_copied, 1)
                        for v in range(NW + 1):
                            if v < NW:
                                _, n = WINDOWS[v]
                                dve.wait_ge(scored, at(g, NW, v))
                                dve.tensor_reduce(neg_max[s][0:n, v:v + 1],
                                                  ps_scores[(NW * s + v) % 2][0:n, 0:1 + S], AX.X, ALU.max,
                                                  negate=True).then_inc(maxed, 1)
                            if v >= 1:
                                x = v - 1
                                _, n = WINDOWS[x]
                                p = probs[(NW * s + x) % 4][0:n, 0:1 + S]
                                dve.wait_ge(exped, at(g, NW, x))
                                dve.reciprocal(inverse[0:n, x:x + 1], sums[s][0:n, x:x + 1]).then_inc(inverted, 1)
                                dve.wait_ge(inverted, at(g, NW, x))
                                dve.tensor_scalar(p, p, inverse[0:n, x:x + 1], None, ALU.mult).then_inc(scaled, 1)
                        for tile in DVE_TILES[2:]:
                            dve.wait_ge(tile_done, at(g, TILES, tile))
                            if tile < O_AT:
                                half, t = divmod(tile - Z_AT, KT)
                                dve.tensor_copy(half_cols(Z[:, t, :], half), bank(tile)[:, 0:HALF]
                                                ).then_inc(dve_copied, 1)
                            elif tile < OUT_AT:
                                half = tile - O_AT
                                dve.tensor_tensor(by_batch(half_cols(oT[:], half)), by_batch(bank(tile)[:, 0:HALF]),
                                                  biases(f"L2_xattn_bv{layer}", half), ALU.add).then_inc(dve_copied, 1)
                            else:
                                x = k.X[:, bass.ds(b, 1), :].squeeze(1)
                                dve.tensor_tensor(x, x, bank(tile)[0:L, :], ALU.add).then_inc(dve_copied, 1)


def layer2(nc, k, ins, ctx):
    for layer in (1, 2):
        with ExitStack() as own:
            hT = own.enter_context(nc.sbuf_tensor(f"l2_hT{layer}", [P, KT, B * L], F32))
            norm_features(nc, k, ctx, f"l2ln{layer}", lambda t, half: by_batch(half_tokens(hT, t, half)),
                          f"L2_xattn_ln{layer}_scale", f"L2_xattn_ln{layer}_offset", 1e-5,
                          add_row=ins[f"L2_xattn_bo{layer}"])
            layer2_attention(nc, k, ins, ctx, layer, hT)
    with ExitStack() as own:
        hT = own.enter_context(nc.sbuf_tensor("l2_hTm", [P, KT, B * L], F32))
        norm_features(nc, k, ctx, "l2lnm", lambda t, half: by_batch(half_tokens(hT, t, half)),
                      "L2_xattn_ln_mlp_scale", "L2_xattn_ln_mlp_offset", 1e-5, add_row=ins["L2_xattn_b_fc2"])
        mlp(nc, k, ctx, "l2mlp", hT, ins["L2_xattn_w_fc1"], ins["L2_xattn_w_fc2"], "L2_xattn_b_fc1", ACT.Gelu)


H3, KV3, Q3, DH3 = 32, 8, 4, 16
T3, NT3 = 121, 3
N3 = T3 * NT3


def layer3_queries(nc, k, ins, ctx, queries):
    with ExitStack() as own:
        own.callback(k.sems.end_phase)
        Wq = own.enter_context(nc.sbuf_tensor("Wq3", [P, KT, D], F32))
        Wq_grouped = own.enter_context(nc.sbuf_tensor("Wq3_grouped", [P, KT, Q3, P], F32))
        xT = own.enter_context(nc.sbuf_tensor("xT3", [P, KT, B * L], F32))
        tiles = Tiles(k, "l3q", psum_banks(nc, own, "l3q_ps", 8),
                      [("xT", 2 * KT, "ad"), ("q", HALVES * Q3, "da")])
        loaded = k.sems.take("l3q_loaded")
        grouped = k.sems.take("l3q_grouped")
        block = own.enter_context(nc.Block())

        @block.sync
        def _(sp):
            load_features(sp, Wq, ins["L3_xattn_Wq"], loaded)

        @block.gpsimd
        def _(pool):
            k.sems.clear_ended(pool)

        @block.tensor
        def _(pe):
            turn_tokens(pe, k, tiles, "xT", k.X, lambda b: None)
            pe.wait_ge(grouped, KT)
            for half in range(HALVES):
                tiles.wait_out(pe, "xT", range(half * KT, (half + 1) * KT))
                for g in range(Q3):
                    j = half * Q3 + g
                    tiles.wait_free(pe, "q", j)
                    for t in range(KT):
                        mm = pe.matmul(tiles.bank("q", j)[:, 0:HALF], Wq_grouped[:, t, g, :], half_tokens(xT, t, half),
                                       start=(t == 0), stop=(t == KT - 1))
                    mm.then_inc(tiles.filled, 1)

        @block.scalar
        def _(act):
            for j in tiles.mine("a", "xT"):
                tiles.wait_filled(act, "xT", j)
                act.activation(half_tokens(xT, j % KT, j // KT), tiles.bank("xT", j)[:, 0:HALF], ACT.Copy
                               ).then_inc(tiles.emptied["a"], 1)
            for j in tiles.mine("a", "q"):
                tiles.wait_filled(act, "q", j)
                act.activation(half_tokens(queries, j % Q3, j // Q3), tiles.bank("q", j)[:, 0:HALF], ACT.Identity,
                               bias=column(k, "L3_xattn_bq", j % Q3)).then_inc(tiles.emptied["a"], 1)

        @block.vector
        def _(dve):
            for j in tiles.mine("d", "xT"):
                tiles.wait_filled(dve, "xT", j)
                dve.tensor_copy(half_tokens(xT, j % KT, j // KT), tiles.bank("xT", j)[:, 0:HALF]
                                ).then_inc(tiles.emptied["d"], 1)
            dve.wait_ge(loaded, 16)
            for t in range(KT):
                dve.tensor_copy(Wq_grouped[:, t].rearrange("p g (v d) -> p g v d", v=KV3),
                                Wq[:, t, :].rearrange("p (v g d) -> p g v d", v=KV3, g=Q3)).then_inc(grouped, 1)
            for j in tiles.mine("d", "q"):
                tiles.wait_filled(dve, "q", j)
                dve.tensor_scalar(half_tokens(queries, j % Q3, j // Q3), tiles.bank("q", j)[:, 0:HALF],
                                  column(k, "L3_xattn_bq", j % Q3), None, ALU.add).then_inc(tiles.emptied["d"], 1)


def layer3_attention(nc, k, ins, ctx, queries):
    with ExitStack() as own:
        own.callback(k.sems.end_phase)
        def sb(name, shape):
            return own.enter_context(nc.sbuf_tensor(name, shape, F32))

        def sem(name):
            return k.sems.take(name)

        Wk = sb("Wk3", [P, KT, P])
        Wv = sb("Wv3", [P, KT, P])
        v_bias = sb("v_bias3", [P, P])
        head_rows = sb("head_rows", [P, KV3])
        cT = [sb(f"cT3_{s}", [P, KT, N3]) for s in range(2)]
        mask_add = [sb(f"mask3_{s}", [L, N3]) for s in range(2)]
        q_heads = [sb(f"q_heads3_{s}", [P, Q3, KV3, L]) for s in range(2)]
        keysT = sb("keysT3", [P, N3])
        values = sb("values3", [T3, NT3, P])
        probs = [sb(f"probs3_{i}", [L, N3]) for i in range(4)]
        probsT = [sb(f"probsT3_{i}", [T3, NT3, L]) for i in range(2)]
        neg_max = sb("neg_max3", [L, H3])
        sums = [sb(f"sums3_{s}", [L, H3]) for s in range(2)]
        rsum = sb("rsum3", [L, H3])
        work = psum_banks(nc, own, "work3_", 2)
        ps_scores = psum_banks(nc, own, "scores3_", 2)
        ps_turned = psum_banks(nc, own, "turned3_", 2)
        ps_att = own.enter_context(nc.psum_tensor("ps_att3", [P, H3, DH3], F32))

        loaded = sem("loaded3")
        padded = sem("padded3")
        rows_ready = sem("head_rows_ready")
        cT_loaded = [sem(f"cT3_loaded{s}") for s in range(2)]
        mask_loaded = [sem(f"mask3_loaded{s}") for s in range(2)]
        projected = sem("projected3")
        keys_copied = sem("keys_copied3")
        values_copied = sem("values_copied3")
        headed = sem("headed3")
        scored = sem("scored3")
        shifted = sem("shifted3")
        maxed = sem("maxed3")
        exped = sem("exped3")
        turned = sem("turned3")
        turned_copied = {"a": sem("turned_act3"), "d": sem("turned_dve3")}
        attended = sem("attended3")
        inverted = sem("inverted3")
        att_copied = sem("att_copied3")

        def wait_turned(eng, b, h):
            eng.wait_ge(turned_copied["ad"[h % 2]], at(b, H3 // 2, h // 2))

        def copy_turned(eng, engine, b, h):
            eng.wait_ge(turned, at(b, H3, h))
            eng.wait_ge(attended, at(b, H3, h - 2))
            dst = probsT[h % 2][:].rearrange("p j l -> p (j l)")
            src = ps_turned[h % 2][0:T3, 0:NT3 * L]
            ins_ = eng.activation(dst, src, ACT.Copy) if engine == "a" else eng.tensor_copy(dst, src)
            ins_.then_inc(turned_copied[engine], 1)

        block = own.enter_context(nc.Block())

        @block.sync
        def _(sp):
            load_features(sp, Wk, ins["L3_xattn_Wk"], loaded)
            load_features(sp, Wv, ins["L3_xattn_Wv"], loaded)
            sp.dma_start(v_bias[:], ins["L3_xattn_bv"].partition_broadcast(P)).then_inc(loaded, 16)
            sp.wait_ge(padded, 1)
            with sp.Fori(0, B // 2) as i:
                for s in range(2):
                    b = 2 * i + s
                    sp.wait_ge(projected, at(b, 2, 1, back=2))
                    sp.dma_start(cT[s][:, :, 0:S], k.ctxT[b]).then_inc(cT_loaded[s], 16)
                    sp.wait_ge(shifted, at(b, H3, H3 - 1, back=2))
                    sp.dma_start(mask_add[s][:, 0:S], ins["mask_Bx1xSxS2_ff0"][b, 0]).then_inc(mask_loaded[s], 16)

        @block.gpsimd
        def _(pool):
            k.sems.clear_ended(pool)
            for s in range(2):
                pool.memset(cT[s][:, :, S:N3], 0.0)
                last = pool.memset(mask_add[s][:, S:N3], MASKED)
            last.then_inc(padded, 1)
            pool.sem_inc(headed, 2 * Q3)
            pool.wait_ge(rows_ready, 1)
            with pool.Fori(0, B // 2) as i:
                for s in range(2):
                    b = 2 * i + s
                    pool.wait_ge(scored, at(b, H3, H3 - 1, back=2))
                    for g in range(Q3):
                        pool.tensor_tensor(
                            q_heads[s][:, g], queries[:, g, bass.ds(b * L, L)].unsqueeze(1).broadcast_to([P, KV3, L]),
                            head_rows[:].unsqueeze(2).broadcast_to([P, KV3, L]), ALU.mult).then_inc(headed, 1)

        @block.tensor
        def _(pe):
            pe.sem_inc(projected, 4)
            for done in (scored, turned, attended):
                pe.sem_inc(done, 2 * H3)
            pe.wait_ge(loaded, 48)
            with pe.Fori(0, B // 2) as i:
                for s in range(2):
                    b = 2 * i + s
                    pe.wait_ge(cT_loaded[s], 16 * (i + 1))
                    pe.wait_ge(keys_copied, at(b, 1, 0, back=1))
                    for t in range(KT):
                        mm = pe.matmul(work[0][:, 0:N3], Wk[:, t, :], cT[s][:, t, :], start=(t == 0), stop=(t == KT - 1))
                    mm.then_inc(projected, 1)
                    pe.wait_ge(values_copied, at(b, 1, 0, back=1))
                    for j in range(NT3):
                        for t in range(KT):
                            mm = pe.matmul(work[1][0:T3, j * P:(j + 1) * P], cT[s][:, t, j * T3:(j + 1) * T3], Wv[:, t, :],
                                           start=(t == 0), stop=(t == KT - 1))
                    mm.then_inc(projected, 1)

                    def scores(h):
                        v, g = divmod(h, Q3)
                        if h == 0:
                            pe.wait_ge(keys_copied, at(b, 1, 0))
                            pe.wait_ge(headed, at(b, Q3, Q3 - 1))
                        pe.wait_ge(shifted, at(b, H3, h - 2))
                        pe.matmul(ps_scores[h % 2][0:L, 0:N3], q_heads[s][:, g, v, :], keysT[:], start=True, stop=True
                                  ).then_inc(scored, 1)

                    def turn(h):
                        pe.wait_ge(exped, at(b, H3, h))
                        wait_turned(pe, b, h - 2)
                        for j in range(NT3):
                            mm = pe.transpose(ps_turned[h % 2][0:T3, j * L:(j + 1) * L],
                                              probs[h % 4][:, j * T3:(j + 1) * T3], k.ident[0:L, 0:L])
                        mm.then_inc(turned, 1)

                    def attend(h):
                        v = h // Q3
                        if h == 0:
                            pe.wait_ge(values_copied, at(b, 1, 0))
                            pe.wait_ge(att_copied, at(b, 1, 0, back=1))
                        wait_turned(pe, b, h)
                        for j in range(NT3):
                            mm = pe.matmul(ps_att[0:L, h, :], probsT[h % 2][:, j, :],
                                           values[:, j, v * DH3:(v + 1) * DH3], start=(j == 0), stop=(j == NT3 - 1))
                        mm.then_inc(attended, 1)

                    for step in range(H3 + 3):
                        if step < H3:
                            scores(step)
                        if 0 <= step - 2 < H3:
                            turn(step - 2)
                        if 0 <= step - 3 < H3:
                            attend(step - 3)

        @block.scalar
        def _(act):
            act.sem_inc(keys_copied, 2)
            act.sem_inc(exped, 2 * H3)
            act.sem_inc(turned_copied["a"], H3)
            with act.Fori(0, B // 2) as i:
                for s in range(2):
                    b = 2 * i + s
                    act.wait_ge(projected, at(b, 2, 0))
                    act.activation(keysT[:], work[0][:, 0:N3], ACT.Identity, bias=column(k, "L3_xattn_bk")
                                   ).then_inc(keys_copied, 1)
                    for h in range(H3 + 1):
                        if h < H3:
                            act.wait_ge(maxed, at(b, H3, h))
                            act.activation(probs[h % 4][:], probs[h % 4][:], ACT.Exp, bias=neg_max[:, h:h + 1],
                                           accum_out=sums[s][:, h:h + 1]).then_inc(exped, 1)
                        if h >= 1 and h % 2 == 1:
                            copy_turned(act, "a", b, h - 1)

        @block.vector
        def _(dve):
            dve.tensor_scalar(head_rows[:], k.head_of[:], DH3 ** -0.5, None, ALU.mult).then_inc(rows_ready, 1)
            dve.sem_inc(values_copied, 2)
            dve.sem_inc(shifted, 2 * H3)
            dve.sem_inc(maxed, 2 * H3)
            dve.sem_inc(turned_copied["d"], H3)
            dve.sem_inc(inverted, 2)
            dve.sem_inc(att_copied, 2)
            dve.wait_ge(loaded, 48)
            with dve.Fori(0, B // 2) as i:
                for s in range(2):
                    b = 2 * i + s
                    dve.wait_ge(projected, at(b, 2, 1))
                    dve.tensor_tensor(values[:], work[1][0:T3, 0:NT3 * P].rearrange("p (j d) -> p j d", j=NT3),
                                      v_bias[0:T3, :].unsqueeze(1).broadcast_to([T3, NT3, P]), ALU.add
                                      ).then_inc(values_copied, 1)
                    dve.wait_ge(mask_loaded[s], 16 * (i + 1))
                    for h in range(H3 + 2):
                        if h < H3:
                            dve.wait_ge(scored, at(b, H3, h))
                            dve.wait_ge(turned, at(b, H3, h - 4))
                            dve.tensor_tensor(probs[h % 4][:], ps_scores[h % 2][0:L, 0:N3], mask_add[s][:], ALU.add
                                              ).then_inc(shifted, 1)
                            dve.wait_ge(shifted, at(b, H3, h))
                            dve.tensor_reduce(neg_max[:, h:h + 1], probs[h % 4][:], AX.X, ALU.max, negate=True
                                              ).then_inc(maxed, 1)
                        if h >= 2 and (h - 1) % 2 == 1:
                            copy_turned(dve, "d", b, h - 1) if h - 1 < H3 else None
                    dve.wait_ge(exped, at(b, H3, H3 - 1))
                    dve.reciprocal(rsum[:], sums[s][:]).then_inc(inverted, 1)
                    dve.wait_ge(inverted, at(b, 1, 0))
                    dve.wait_ge(attended, at(b, H3, H3 - 1))
                    dve.tensor_tensor(
                        k.ATT[:, bass.ds(b, 1), :].squeeze(1).rearrange("l (h d) -> l h d", h=H3), ps_att[0:L, :, :],
                        rsum[:].unsqueeze(2).broadcast_to([L, H3, DH3]), ALU.mult).then_inc(att_copied, 1)


def layer3_output(nc, k, ins, ctx, out):
    with ExitStack() as own:
        own.callback(k.sems.end_phase)
        def sb(name, shape):
            return own.enter_context(nc.sbuf_tensor(name, shape, F32))

        def sem(name):
            return k.sems.take(name)

        Wo = sb("Wo3", [P, KT, D])
        rows = {n: sb(f"{n}_row3", [L, D]) for n in ("bo", "gamma", "beta")}
        attT = sb("attT3", [P, KT, B * L])
        Y = sb("Y3", [L, B, D])
        stats = norm_stats(nc, own, "l3n")
        n0 = k.norms
        k.norms += HALVES
        tiles = Tiles(k, "l3o", psum_banks(nc, own, "l3o_ps", 8), [("attT", 2 * KT, "ad"), ("out", B, "d")])
        loaded = sem("l3o_loaded")
        residual = sem("l3o_residual")
        scaled = sem("l3o_scaled")
        offset = sem("l3o_offset")
        stored = sem("l3o_stored")
        block = own.enter_context(nc.Block())

        @block.sync
        def _(sp):
            load_features(sp, Wo, ins["L3_xattn_Wo"], loaded)
            for n, row in rows.items():
                sp.dma_start(row[:], ins[f"L3_xattn_{n}"].partition_broadcast(L)).then_inc(loaded, 16)
            for b in range(B):
                sp.wait_ge(offset, b + 1)
                sp.dma_start(out[b], Y[:, b, :]).then_inc(stored, 16)
            sp.wait_ge(stored, 16 * B)

        @block.tensor
        def _(pe):
            turn_tokens(pe, k, tiles, "attT", k.ATT, lambda b: None)
            pe.wait_ge(loaded, 64)
            project_tokens(pe, tiles, "out", attT, Wo, KT,
                           lambda b: tiles.wait_out(pe, "attT", range((b // 4) * KT, (b // 4 + 1) * KT)))

        @block.scalar
        def _(act):
            for j in tiles.mine("a", "attT"):
                tiles.wait_filled(act, "attT", j)
                act.activation(half_tokens(attT, j % KT, j // KT), tiles.bank("attT", j)[:, 0:HALF], ACT.Copy
                               ).then_inc(tiles.emptied["a"], 1)

        @block.gpsimd
        def _(pool):
            k.sems.clear_ended(pool)
            pool.wait_ge(loaded, 64)
            for b in range(B):
                pool.tensor_tensor(Y[:, b, :], k.X[:, b, :], rows["bo"][:], ALU.add).then_inc(residual, 1)
            for half in range(HALVES):
                invert_half_pool(pool, k, stats, half, n0 + half)
                for c in range(4):
                    b = 4 * half + c
                    pool.wait_ge(scaled, b + 1)
                    pool.tensor_tensor(Y[:, b, :], Y[:, b, :], rows["beta"][:], ALU.add).then_inc(offset, 1)

        @block.vector
        def _(dve):
            for j in tiles.mine("d", "attT"):
                tiles.wait_filled(dve, "attT", j)
                dve.tensor_copy(half_tokens(attT, j % KT, j // KT), tiles.bank("attT", j)[:, 0:HALF]
                                ).then_inc(tiles.emptied["d"], 1)
            for half in range(HALVES):
                for c in range(4):
                    b = 4 * half + c
                    tiles.wait_filled(dve, "out", b)
                    dve.wait_ge(residual, b + 1)
                    dve.tensor_tensor(Y[:, b, :], Y[:, b, :], tiles.bank("out", b)[0:L, :], ALU.add
                                      ).then_inc(tiles.emptied["d"], 1)
                tiles.wait_out(dve, "out", [4 * half + 3])
                norm_half_dve(dve, k, Y, Y, stats, 1e-6, half, n0 + half)
                for c in range(4):
                    b = 4 * half + c
                    dve.wait_ge(k.stat_sem["normed"], 4 * n0 + b + 1)
                    dve.tensor_tensor(Y[:, b, :], Y[:, b, :], rows["gamma"][:], ALU.mult).then_inc(scaled, 1)


def layer3(nc, k, ins, ctx, out):
    with ExitStack() as own:
        k.ATT = own.enter_context(nc.sbuf_tensor("ATT3", [L, B, D], F32))
        with ExitStack() as inner:
            queries = inner.enter_context(nc.sbuf_tensor("queries3", [P, Q3, B * L], F32))
            layer3_queries(nc, k, ins, ctx, queries)
            layer3_attention(nc, k, ins, ctx, queries)
        layer3_output(nc, k, ins, ctx, out)


def program(nc, ins, out):
    k = Shared()
    k.sems = Semaphores(nc)
    with ExitStack() as ctx:
        setup(nc, k, ins, ctx)
        statistics_semaphores(nc, k, ctx)
        with ExitStack() as own:
            k.ATT = own.enter_context(nc.sbuf_tensor("ATT", [L, B, D], F32))
            layer0_attention(nc, k, ins, ctx)
            hT = own.enter_context(nc.sbuf_tensor("l0_hT", [P, KT, B * L], F32))
            layer0_output(nc, k, ins, ctx, hT)
            mlp(nc, k, ctx, "l0mlp", hT, ins["L0_xattn_mlp_w1"], ins["L0_xattn_mlp_w2"], "L0_xattn_mlp_b1",
                ACT.Gelu_apprx_tanh)
        layer1(nc, k, ins, ctx)
        layer2(nc, k, ins, ctx)
        layer3(nc, k, ins, ctx, out)


def kernel(**inputs):
    import numpy as _np
    import concourse.bacc as _bacc
    from concourse import mybir as _mybir
    from concourse.bass_utils import run_bass_kernel_spmd as _run

    nc = _bacc.Bacc("TRN2", target_bir_lowering=False, num_devices=1)
    arrays, ins = {}, {}
    for name, value in inputs.items():
        a = _np.ascontiguousarray(value)
        arrays[f"in_{name}_dram"] = a
        ins[name] = nc.dram_tensor(f"in_{name}_dram", a.shape, _mybir.dt.from_np(a.dtype), kind="ExternalInput").ap()
    out = nc.dram_tensor("out_0_dram", (B, L, D), F32, kind="ExternalOutput").ap()
    program(nc, ins, out)
    r = _run(nc, [arrays], core_ids=[0])
    return r.results[0]["out_0_dram"]
```

```python
from contextlib import ExitStack

import concourse.bass as bass
from concourse import mybir

F32 = mybir.dt.float32
F32R = mybir.dt.float32r
I32 = mybir.dt.int32
ALU = mybir.AluOpType
ACT = mybir.ActivationFunctionType
AX = mybir.AxisListType

P = 128
B, L, D = 8, 100, 512
S = 361
KT = D // P
HALF = 4 * L
HALVES = B * L // HALF
MASKED = -1e30

H0, DH0 = 16, 32
T0 = 116
NT0 = 4
N0 = T0 * NT0
F_MLP = 2048
FT = F_MLP // P


class Split:

    def __init__(self, ctx, nc, name, shape):
        self.hi = ctx.enter_context(nc.sbuf_tensor(f"{name}_hi", shape, F32R))
        self.lo = ctx.enter_context(nc.sbuf_tensor(f"{name}_lo", shape, F32R))

    def round(self, act, cut, value):
        return act.activation(cut(self.hi), value, ACT.Copy)

    def rest(self, dve, cut, value):
        return dve.tensor_tensor(cut(self.lo), value, cut(self.hi).bitcast(F32), ALU.subtract)


def product(pe, out, a, b, cut_a, cut_b, start, stop):
    pe.matmul(out, cut_a(a.hi), cut_b(b.hi), start=start, stop=False)
    pe.matmul(out, cut_a(a.hi), cut_b(b.lo), start=False, stop=False)
    return pe.matmul(out, cut_a(a.lo), cut_b(b.hi), start=False, stop=stop)


def at(batch, events, event, back=0):
    return events * (batch + 2 - back) + event + 1


class Semaphores:

    def __init__(self, nc):
        self.nc, self.taken, self.ended = nc, [], []

    def take(self, name):
        self.taken.append(self.nc.alloc_semaphore(name))
        return self.taken[-1]

    def clear_ended(self, pool):
        for s in self.ended:
            pool.sem_clear(s)

    def end_phase(self):
        for s in self.ended:
            self.nc.release_semaphore(s)
        self.ended, self.taken = self.taken, []


class Shared:
    pass


PARAM_TILES = [
    [("L0_xattn_q_b", 4), ("L0_xattn_postnorm_w", 4), ("L0_xattn_mlp_b1", 16), ("kv_b_keys", 4),
     ("L1_xattn_ln1_w", 4), ("L1_xattn_ln1_b", 4), ("L1_xattn_ln2_w", 4), ("L1_xattn_ln2_b", 4),
     ("L1_xattn_maa_x", 4), ("L1_xattn_maa_w", 4), ("L1_xattn_maa_k", 4), ("L1_xattn_maa_v", 4),
     ("L1_xattn_maa_r", 4), ("L1_xattn_maa_g", 4), ("L1_xattn_time_decay", 4), ("L1_xattn_faaaa", 4),
     ("L1_xattn_gn_w", 4), ("L1_xattn_gn_b", 4), ("L1_xattn_fmaa_k", 4), ("L1_xattn_fmaa_r", 4)],
    [("L2_xattn_ln1_scale", 4), ("L2_xattn_ln1_offset", 4), ("L2_xattn_ln2_scale", 4),
     ("L2_xattn_ln2_offset", 4), ("L2_xattn_ln_mlp_scale", 4), ("L2_xattn_ln_mlp_offset", 4),
     ("L2_xattn_bq1", 16), ("L2_xattn_bq2", 16), ("L2_xattn_bv1", 16), ("L2_xattn_bv2", 16),
     ("L2_xattn_b_fc1", 16)],
    [("L2_xattn_bk1", 16), ("L2_xattn_bk2", 16), ("L2_xattn_bias_k1", 16), ("L2_xattn_bias_k2", 16),
     ("L3_xattn_bq", 4), ("L3_xattn_bk", 1)],
]
PARAM_AT = {}
for _tile, _rows in enumerate(PARAM_TILES):
    _at = 0
    for _name, _n in _rows:
        PARAM_AT[_name] = (_tile, _at, _n)
        _at += _n


def column(k, name, j=0, n=1, rows=slice(0, P)):
    tile, first, _ = PARAM_AT[name]
    return k.params[rows, tile, first + j:first + j + n]


def setup(nc, k, ins, ctx):
    k.ident = ctx.enter_context(nc.sbuf_tensor("ident", [P, P], F32))
    k.params = ctx.enter_context(nc.sbuf_tensor("params", [P, len(PARAM_TILES), P], F32))
    k.minus_half = ctx.enter_context(nc.sbuf_tensor("minus_half", [P, 4], F32))
    k.eps5 = ctx.enter_context(nc.sbuf_tensor("eps5", [P, 1], F32))
    k.head_of = ctx.enter_context(nc.sbuf_tensor("head_of", [P, P // N1], F32))
    k.X = ctx.enter_context(nc.sbuf_tensor("X", [L, B, D], F32))
    k.states = ctx.enter_context(nc.sbuf_tensor("states", [P, KT, 2, B], F32))
    with ExitStack() as own:
        own.callback(k.sems.end_phase)
        rows = own.enter_context(nc.sbuf_tensor("param_rows", [P, len(PARAM_TILES), P], F32))
        ps = own.enter_context(nc.psum_tensor("ps_setup", [P, len(PARAM_TILES), P], F32))
        state_rows = own.enter_context(nc.sbuf_tensor("state_rows", [2 * B, D], F32))
        ps_states = own.enter_context(nc.psum_tensor("ps_states", [P, KT, 2 * B], F32))
        zeroed = k.sems.take("rows_zeroed")
        blank = k.sems.take("ident_blank")
        ready = k.sems.take("ident_ready")
        loaded = k.sems.take("params_loaded")
        k.x_loaded = k.sems.take("x_loaded")
        turned = k.sems.take("params_turned")
        copied = k.sems.take("params_copied")
        block = own.enter_context(nc.Block())

        n_loads = sum(len(t) for t in PARAM_TILES)

        @block.vector
        def _(dve):
            dve.memset(rows[:], 0.0).then_inc(zeroed, 1)
            dve.wait_ge(k.x_loaded, 16)
            dve.wait_ge(turned, 1)
            dve.tensor_copy(k.params[:], ps[:]).then_inc(copied, 1)
            dve.tensor_copy(k.states[:].rearrange("p k r b -> p k (r b)"), ps_states[:]).then_inc(copied, 1)

        @block.gpsimd
        def _(pool):
            k.sems.clear_ended(pool)
            pool.memset(k.minus_half[:], -0.5)
            pool.memset(k.eps5[:], 1e-5)
            pool.memset(k.ident[:], 0.0).then_inc(blank, 1)
            pool.wait_ge(blank, 1)
            pool.affine_select(out=k.ident[:], in_=k.ident[:], pattern=[[1, P]], compare_op=ALU.not_equal,
                               fill=1.0, base=0, channel_multiplier=-1).then_inc(ready, 1)

        @block.sync
        def _(sp):
            sp.dma_start(k.X[:], ins["x"].rearrange("b l d -> l b d")).then_inc(k.x_loaded, 16)
            for r in range(2):
                sp.dma_start(state_rows[r * B:(r + 1) * B, :], ins["ctx_2048"][:, r, :]).then_inc(loaded, 16)
            sp.wait_ge(zeroed, 1)
            for name, (tile, first, n) in PARAM_AT.items():
                dst = rows[first:first + n, tile, :]
                if name == "kv_b_keys":
                    src = ins["L0_xattn_kv_b"].rearrange("(m p two) -> m p two", m=n, two=2)[:, :, 0]
                    with nc.allow_non_contiguous_dma("512 biases"):
                        sp.dma_start(dst, src).then_inc(loaded, 16)
                    continue
                if name == "L3_xattn_bq":
                    src = ins[name].rearrange("(v g d) -> g v d", v=8, g=4)
                    dst = dst.rearrange("g (v d) -> g v d", v=8)
                    sp.dma_start(dst, src).then_inc(loaded, 16)
                    continue
                src = ins[name]
                if len(src.shape) == 3:
                    src = src.rearrange("a b c -> (a b c)")
                elif len(src.shape) == 4:
                    src = src.rearrange("a b c d -> (a b c d)")
                sp.dma_start(dst, src.rearrange("(n p) -> n p", p=P)).then_inc(loaded, 16)

        @block.tensor
        def _(pe):
            pe.wait_ge(ready, 1)
            pe.wait_ge(loaded, 16 * (n_loads + 2))
            for t in range(KT):
                pe.transpose(ps_states[:, t, :], state_rows[:, t * P:(t + 1) * P], k.ident[0:2 * B, 0:2 * B])
            for t in range(len(PARAM_TILES)):
                last = pe.transpose(ps[:, t, :], rows[:, t, :], k.ident[:])
            last.then_inc(turned, 1)


def layer0_attention(nc, k, ins, ctx):
    x, context, mask = ins["x"], ins["ctx_2048"], ins["mask_BxS2_ik0"]
    k.ctxT = {part: nc.dram_tensor(f"ctxT_{part}", [B, P, KT, S], F32R, kind="Internal").ap() for part in ("hi", "lo")}

    def sem(name):
        return k.sems.take(name)

    with ExitStack() as own:
        own.callback(k.sems.end_phase)
        def sb(name, shape, dt=F32):
            return own.enter_context(nc.sbuf_tensor(name, shape, dt))

        q_w = sb("q_w", [P, KT, D])
        kv_w = [sb(f"kv_w{i}", [P, 2 * D]) for i in range(2)]
        v_bias = sb("v_bias", [P, 2 * D])
        mask_i = [sb(f"mask_i{s}", [L, S], I32) for s in range(2)]
        mask_add = [sb(f"mask_add{s}", [L, N0]) for s in range(2)]
        hcat = [sb(f"hcat{s}", [T0, NT0, D]) for s in range(2)]
        hT = [Split(own, nc, f"hT{s}", [P, KT, N0]) for s in range(2)]
        own_T = [sb(f"own_T{s}", [P, KT, L]) for s in range(2)]
        keys_w = Split(own, nc, "keys_w", [P, KT, D])
        values_w = Split(own, nc, "values_w", [P, KT, D])
        keysT = sb("keysT", [P, KT, N0])
        keys_bias = sb("keys_bias", [P, KT])
        values = sb("values", [T0, NT0, D])
        q_heads = sb("q_heads", [P, H0, L])
        probs = [sb(f"probs{s}", [L, N0]) for s in range(4)]
        probsT = [sb(f"probsT{s}", [T0, NT0, L]) for s in range(2)]
        neg_max = sb("neg_max", [L, H0])
        sums = [sb(f"sums{s}", [L, H0]) for s in range(2)]
        rsum = sb("rsum", [L, H0])

        work = [own.enter_context(nc.psum_tensor(f"work{i}", [P, 512], F32)) for i in range(3)]
        ps_scores = [own.enter_context(nc.psum_tensor(f"scores{i}", [P, 512], F32)) for i in range(2)]
        ps_probsT = [own.enter_context(nc.psum_tensor(f"turned{i}", [P, 512], F32)) for i in range(2)]
        ps_att = own.enter_context(nc.psum_tensor("ps_att", [P, H0, DH0], F32))

        weights_loaded = sem("l0_weights_loaded")
        q_loaded = sem("l0_q_loaded")
        mask_loaded = [sem(f"l0_mask_loaded{s}") for s in range(2)]
        kv_loaded = [sem(f"l0_kv_loaded{t}") for t in range(KT)]
        consts_done = sem("l0_consts_done")
        tokens_loaded = [sem(f"l0_tokens_loaded{s}") for s in range(2)]
        ctxT_stored = [sem(f"l0_ctxT_stored{s}") for s in range(2)]
        tile_done = sem("l0_tile_done")
        rounded = sem("l0_rounded")
        act_copied = sem("l0_act_copied")
        dve_copied = sem("l0_dve_copied")
        w_rounded = sem("l0_w_rounded")
        w_split = sem("l0_w_split")
        scored = sem("l0_scored")
        shifted = sem("l0_shifted")
        maxed = sem("l0_maxed")
        exped = sem("l0_exped")
        turned = sem("l0_turned")
        probsT_copied = sem("l0_probsT_copied")
        attended = sem("l0_attended")
        masked = sem("l0_masked")
        inverted = sem("l0_inverted")
        att_copied = sem("l0_att_copied")

        TILES = 3 * KT + 1
        ACT_OF = {KT + 1 + m: m for m in range(KT)}
        DVE_OF = {j: n for n, j in enumerate([*range(KT + 1), *range(2 * KT + 1, TILES)])}

        def wait_copied(eng, b, tile):
            if tile < 0:
                b, tile = b - 1, {-3: TILES - 3, -2: TILES - 2, -1: TILES - 1}[tile]
            if tile in ACT_OF:
                eng.wait_ge(act_copied, at(b, len(ACT_OF), ACT_OF[tile]))
            else:
                eng.wait_ge(dve_copied, at(b, len(DVE_OF), DVE_OF[tile]))

        def bank_of(tile):
            return tile % 3

        def bank_before(tile):
            if tile >= 3:
                return tile - 3
            return {TILES - 1 - j: -1 - j for j in range(3)}[
                next(t for t in range(TILES - 1, TILES - 4, -1) if bank_of(t) == tile)]

        block = own.enter_context(nc.Block())

        @block.sync
        def _(sp):
            for t in range(KT):
                if t >= 2:
                    sp.wait_ge(w_split, 2 * (t - 1))
                sp.dma_start(kv_w[t % 2][:], ins["L0_xattn_kv_w"][t * P:(t + 1) * P, :]).then_inc(kv_loaded[t], 16)
            sp.dma_start(q_w[:], ins["L0_xattn_q_w"].rearrange("(k p) n -> p k n", p=P)).then_inc(q_loaded, 16)
            sp.dma_start(v_bias[:], ins["L0_xattn_kv_b"].partition_broadcast(P)).then_inc(weights_loaded, 16)
            sp.wait_ge(consts_done, 2)
            for s in range(2):
                sp.sem_inc(ctxT_stored[s], 32)
            whole = 3 * T0
            rest = S - whole
            with sp.Fori(0, B // 2) as i:
                for s in range(2):
                    b = 2 * i + s
                    sp.wait_ge(tile_done, at(b, TILES, KT - 1, back=2))
                    sp.dma_start(hcat[s][:, 0:3, :], context[b, 0:whole, :].rearrange("(t p) d -> p t d", p=T0)
                                 ).then_inc(tokens_loaded[s], 16)
                    sp.dma_start(hcat[s][0:rest, 3, :], context[b, whole:S, :]).then_inc(tokens_loaded[s], 16)
                    sp.dma_start(hcat[s][rest:rest + L, 3, :], x[b]).then_inc(tokens_loaded[s], 16)
                    sp.wait_ge(masked, at(b, 1, 0, back=2))
                    sp.dma_start(mask_i[s][:], mask[bass.ds(b, 1), :].squeeze(0).partition_broadcast(L)
                                 ).then_inc(mask_loaded[s], 16)
                    wait_copied(sp, b, KT - 1)
                    sp.dma_start(k.ctxT["hi"][b].bitcast(F32), hT[s].hi[:, :, 0:S].bitcast(F32)
                                 ).then_inc(ctxT_stored[s], 16)
                    sp.dma_start(k.ctxT["lo"][b].bitcast(F32), hT[s].lo[:, :, 0:S].bitcast(F32)
                                 ).then_inc(ctxT_stored[s], 16)
            for s in range(2):
                sp.wait_ge(ctxT_stored[s], 32 * (B // 2 + 1))

        @block.gpsimd
        def _(pool):
            k.sems.clear_ended(pool)
            for s in range(2):
                last = pool.memset(hcat[s][:, 3, :], 0.0)
            last.then_inc(consts_done, 1)
            pool.memset(q_heads[:], 0.0).then_inc(consts_done, 1)

        @block.tensor
        def _(pe):
            for done, per in ((tile_done, TILES), (scored, H0), (turned, H0), (attended, H0)):
                pe.sem_inc(done, 2 * per)
            pe.wait_ge(q_loaded, 16)
            with pe.Fori(0, B // 2) as i:
                for s in range(2):
                    b = 2 * i + s
                    pe.wait_ge(tokens_loaded[s], 48 * (i + 1))
                    for t in range(KT):
                        wait_copied(pe, b, bank_before(t))
                        for j in range(NT0):
                            mm = pe.transpose(work[bank_of(t)][:, j * T0:(j + 1) * T0],
                                              hcat[s][:, j, t * P:(t + 1) * P], k.ident[0:T0, 0:T0])
                        mm.then_inc(tile_done, 1)
                    wait_copied(pe, b, bank_before(KT))
                    wait_copied(pe, b, KT - 1)
                    for m in range(KT):
                        for t in range(KT):
                            mm = pe.matmul(work[bank_of(KT)][:, m * L:(m + 1) * L], q_w[:, t, m * P:(m + 1) * P],
                                           own_T[s][:, t, :], start=(t == 0), stop=(t == KT - 1))
                    mm.then_inc(tile_done, 1)
                    for m in range(KT):
                        tile = KT + 1 + m
                        wait_copied(pe, b, bank_before(tile))
                        for t in range(KT):
                            pe.wait_ge(w_split, 2 * t + 1)
                            mm = product(pe, work[bank_of(tile)][:, 0:N0], keys_w, hT[s],
                                         lambda x: x[:, t, m * P:(m + 1) * P], lambda x: x[:, t, :],
                                         start=(t == 0), stop=(t == KT - 1))
                        mm.then_inc(tile_done, 1)
                    for j in range(NT0):
                        tile = 2 * KT + 1 + j
                        wait_copied(pe, b, bank_before(tile))
                        for t in range(KT):
                            pe.wait_ge(w_split, 2 * t + 2)
                            mm = product(pe, work[bank_of(tile)][0:T0, :], hT[s], values_w,
                                         lambda x: x[:, t, j * T0:(j + 1) * T0], lambda x: x[:, t, :],
                                         start=(t == 0), stop=(t == KT - 1))
                        mm.then_inc(tile_done, 1)

                    def scores(h):
                        if h == 0:
                            wait_copied(pe, b, KT)
                        if h % 4 == 0:
                            wait_copied(pe, b, KT + 1 + h // 4)
                        pe.wait_ge(shifted, at(b, H0, h - 2))
                        pe.matmul(ps_scores[h % 2][0:L, 0:N0], q_heads[:, h, :], keysT[:, h // 4, :],
                                  start=True, stop=True).then_inc(scored, 1)

                    def turn(h):
                        pe.wait_ge(exped, at(b, H0, h))
                        pe.wait_ge(probsT_copied, at(b, H0, h - 2))
                        for j in range(NT0):
                            mm = pe.transpose(ps_probsT[h % 2][0:T0, j * L:(j + 1) * L],
                                              probs[h % 4][:, j * T0:(j + 1) * T0], k.ident[0:L, 0:L])
                        mm.then_inc(turned, 1)

                    def attend(h):
                        if h == 0:
                            wait_copied(pe, b, TILES - 1)
                            pe.wait_ge(att_copied, at(b, 1, 0, back=1))
                        pe.wait_ge(probsT_copied, at(b, H0, h))
                        for j in range(NT0):
                            mm = pe.matmul(ps_att[0:L, h, :], probsT[h % 2][:, j, :],
                                           values[:, j, h * DH0:(h + 1) * DH0], start=(j == 0), stop=(j == NT0 - 1))
                        mm.then_inc(attended, 1)

                    for step in range(H0 + 3):
                        if step < H0:
                            scores(step)
                        if 0 <= step - 2 < H0:
                            turn(step - 2)
                        if 0 <= step - 3 < H0:
                            attend(step - 3)

        @block.scalar
        def _(act):
            act.sem_inc(rounded, 2 * KT)
            act.sem_inc(act_copied, 2 * len(ACT_OF))
            act.sem_inc(exped, 2 * H0)
            act.sem_inc(probsT_copied, 2 * H0)
            for t in range(KT):
                act.wait_ge(kv_loaded[t], 16)
                for n, w in enumerate((keys_w, values_w)):
                    w.round(act, lambda x: x[:, t, :], kv_w[t % 2][:, n:2 * D:2]).then_inc(w_rounded, 1)
            act.wait_ge(consts_done, 3)
            with act.Fori(0, B // 2) as i:
                for s in range(2):
                    b = 2 * i + s
                    act.wait_ge(ctxT_stored[s], 32 * (i + 1))
                    for t in range(KT):
                        act.wait_ge(tile_done, at(b, TILES, t))
                        act.activation(own_T[s][:, t, :], work[bank_of(t)][:, S:S + L], ACT.Copy)
                        hT[s].round(act, lambda x: x[:, t, :], work[bank_of(t)][:, 0:N0]).then_inc(rounded, 1)
                    for m in range(KT):
                        tile = KT + 1 + m
                        act.wait_ge(tile_done, at(b, TILES, tile))
                        act.activation(keysT[:, m, :], work[bank_of(tile)][:, 0:N0], ACT.Identity,
                                       scale=1.0 / DH0, bias=keys_bias[:, m:m + 1]).then_inc(act_copied, 1)

                    def copy_probsT(h):
                        act.wait_ge(turned, at(b, H0, h))
                        act.wait_ge(attended, at(b, H0, h - 2))
                        act.activation(probsT[h % 2][:].rearrange("p j l -> p (j l)"),
                                       ps_probsT[h % 2][0:T0, 0:NT0 * L], ACT.Copy).then_inc(probsT_copied, 1)

                    for h in range(H0):
                        act.wait_ge(maxed, at(b, H0, h))
                        act.activation(probs[h % 4][:], probs[h % 4][:], ACT.Exp, bias=neg_max[:, h:h + 1],
                                       accum_out=sums[s][:, h:h + 1]).then_inc(exped, 1)
                        if h >= 1:
                            copy_probsT(h - 1)
                    copy_probsT(H0 - 1)

        @block.vector
        def _(dve):
            dve.sem_inc(dve_copied, 2 * len(DVE_OF))
            dve.sem_inc(shifted, 2 * H0)
            dve.sem_inc(maxed, 2 * H0)
            dve.sem_inc(inverted, 2)
            dve.sem_inc(att_copied, 2)
            for t in range(KT):
                for n, w in enumerate((keys_w, values_w)):
                    dve.wait_ge(w_rounded, 2 * t + n + 1)
                    w.rest(dve, lambda x: x[:, t, :], kv_w[t % 2][:, n:2 * D:2]).then_inc(w_split, 1)
            dve.wait_ge(weights_loaded, 16)
            dve.wait_ge(consts_done, 2)
            dve.sem_inc(masked, 2)
            dve.tensor_scalar(keys_bias[:], column(k, "kv_b_keys", 0, KT), 1.0 / DH0, None, ALU.mult)
            for s in range(2):
                dve.memset(mask_add[s][:, S:S + L], 0.0)
                last = dve.memset(mask_add[s][:, S + L:N0], MASKED)
            last.then_inc(consts_done, 1)
            with dve.Fori(0, B // 2) as i:
                for s in range(2):
                    b = 2 * i + s
                    for t in range(KT):
                        dve.wait_ge(rounded, at(b, KT, t))
                        hT[s].rest(dve, lambda x: x[:, t, :], work[bank_of(t)][:, 0:N0]).then_inc(dve_copied, 1)
                    dve.wait_ge(tile_done, at(b, TILES, KT))
                    for j in range(4):
                        r = slice(DH0 * j, DH0 * (j + 1))
                        last = dve.tensor_tensor(
                            q_heads[r, j:H0:4, :], work[bank_of(KT)][r, 0:HALF].rearrange("p (m l) -> p m l", m=KT),
                            column(k, "L0_xattn_q_b", 0, KT, rows=r).unsqueeze(2).broadcast_to([DH0, KT, L]), ALU.add)
                    last.then_inc(dve_copied, 1)
                    for j in range(NT0):
                        tile = 2 * KT + 1 + j
                        dve.wait_ge(tile_done, at(b, TILES, tile))
                        dve.tensor_tensor(values[:, j, :], work[bank_of(tile)][0:T0, :], v_bias[0:T0, 1:2 * D:2],
                                          ALU.add).then_inc(dve_copied, 1)
                    dve.wait_ge(mask_loaded[s], 16 * (i + 1))
                    dve.tensor_scalar(mask_add[s][:, 0:S], mask_i[s][:], 0, MASKED, ALU.is_equal, ALU.mult
                                      ).then_inc(masked, 1)
                    dve.wait_ge(masked, at(b, 1, 0))
                    for h in range(H0):
                        dve.wait_ge(scored, at(b, H0, h))
                        dve.wait_ge(turned, at(b, H0, h - 4))
                        dve.tensor_tensor(probs[h % 4][:], ps_scores[h % 2][0:L, 0:N0], mask_add[s][:], ALU.add
                                          ).then_inc(shifted, 1)
                        dve.wait_ge(shifted, at(b, H0, h))
                        dve.tensor_reduce(neg_max[:, h:h + 1], probs[h % 4][:], AX.X, ALU.max, negate=True
                                          ).then_inc(maxed, 1)
                    dve.wait_ge(exped, at(b, H0, H0 - 1))
                    dve.reciprocal(rsum[:], sums[s][:]).then_inc(inverted, 1)
                    dve.wait_ge(inverted, at(b, 1, 0))
                    dve.wait_ge(attended, at(b, H0, H0 - 1))
                    dve.tensor_tensor(
                        k.ATT[:, bass.ds(b, 1), :].squeeze(1).rearrange("l (h d) -> l h d", h=H0), ps_att[0:L, :, :],
                        rsum[:].unsqueeze(2).broadcast_to([L, H0, DH0]), ALU.mult).then_inc(att_copied, 1)



class Tiles:

    def __init__(self, k, name, banks, stages):
        self.filled = k.sems.take(f"{name}_filled")
        self.emptied = {"a": k.sems.take(f"{name}_act_emptied"),
                        "d": k.sems.take(f"{name}_dve_emptied")}
        self.banks = banks
        self.first, self.size, self.by = {}, {}, []
        counts = {"a": 0, "d": 0}
        for stage, n, engines in stages:
            self.first[stage], self.size[stage] = len(self.by), n
            for j in range(n):
                e = engines[j % len(engines)]
                counts[e] += 1
                self.by.append((e, counts[e]))

    def bank(self, stage, j):
        return self.banks[(self.first[stage] + j) % len(self.banks)]

    def wait_free(self, pe, stage, j):
        before = self.first[stage] + j - len(self.banks)
        if before >= 0:
            e, n = self.by[before]
            pe.wait_ge(self.emptied[e], n)

    def wait_filled(self, eng, stage, j):
        eng.wait_ge(self.filled, self.first[stage] + j + 1)

    def wait_out(self, eng, stage, tiles=None):
        last = {}
        for j in (range(self.size[stage]) if tiles is None else tiles):
            e, n = self.by[self.first[stage] + j]
            last[e] = max(last.get(e, 0), n)
        for e, n in last.items():
            eng.wait_ge(self.emptied[e], n)

    def mine(self, engine, stage):
        return [j for j in range(self.size[stage]) if self.by[self.first[stage] + j][0] == engine]


def psum_banks(nc, ctx, name, n):
    return [ctx.enter_context(nc.psum_tensor(f"{name}{i}", [P, 512], F32)) for i in range(n)]


def half_tokens(t, tile, half):
    return t[:, tile, half * HALF:(half + 1) * HALF]


def turn_tokens(pe, k, tiles, stage, src, ready):
    for half in range(HALVES):
        for t in range(KT):
            j = half * KT + t
            tiles.wait_free(pe, stage, j)
            for c in range(4):
                b = 4 * half + c
                if t == 0:
                    ready(b)
                mm = pe.transpose(tiles.bank(stage, j)[:, c * L:(c + 1) * L],
                                  src[:, b, t * P:(t + 1) * P], k.ident[0:L, 0:L])
            mm.then_inc(tiles.filled, 1)


def project_tokens(pe, tiles, stage, lhs, weights, n_k, ready=None):
    for b in range(B):
        tiles.wait_free(pe, stage, b)
        if ready is not None:
            ready(b)
        for t in range(n_k):
            mm = pe.matmul(tiles.bank(stage, b)[0:L, :], lhs[:, t, b * L:(b + 1) * L], weights[:, t, :],
                           start=(t == 0), stop=(t == n_k - 1))
        mm.then_inc(tiles.filled, 1)


def round_tiles(act, tiles, stage, split, whole, rounded):
    for j in range(2 * KT):
        half, t = divmod(j, KT)
        tiles.wait_out(act, stage, [j])
        split.round(act, lambda x: half_tokens(x, t, half), half_tokens(whole, t, half)).then_inc(rounded, 1)


def split_tiles(dve, split, whole, rounded):
    for j in range(2 * KT):
        half, t = divmod(j, KT)
        dve.wait_ge(rounded, j + 1)
        split.rest(dve, lambda x: half_tokens(x, t, half), half_tokens(whole, t, half))


def statistics_semaphores(nc, k, ctx):
    k.stat_sem = {n: ctx.enter_context(nc.semaphore(f"norm_{n}")) for n in
                  ("summed", "aggregated", "shifted", "inverted", "normed")}
    k.norms = 0


def norm_half_dve(dve, k, src, dst, stats, eps, half, n):
    sem = k.stat_sem
    for c in range(4):
        b = 4 * half + c
        last = dve.bn_stats(stats.six[:, b, :], src[:, b, :])
    last.then_inc(sem["summed"], 1)
    dve.wait_ge(sem["summed"], n + 1)
    for c in range(4):
        b = 4 * half + c
        last = dve.bn_aggr(stats.mean_var[:, b, :], stats.six[:, b, :])
    last.then_inc(sem["aggregated"], 1)
    dve.wait_ge(sem["aggregated"], n + 1)
    r = slice(4 * half, 4 * half + 4)
    dve.tensor_scalar(stats.shifted[:, r], stats.mean_var[:, r, 1], eps, None, ALU.add).then_inc(sem["shifted"], 1)
    dve.wait_ge(sem["inverted"], n + 1)
    for c in range(4):
        b = 4 * half + c
        dve.tensor_scalar(dst[:, b, :], src[:, b, :], stats.mean_var[:, b, 0:1], stats.inverse[:, b:b + 1],
                          ALU.subtract, ALU.mult).then_inc(sem["normed"], 1)


def invert_half_pool(pool, k, stats, half, n):
    r = slice(4 * half, 4 * half + 4)
    pool.wait_ge(k.stat_sem["shifted"], n + 1)
    pool.tensor_tensor(stats.inverse[:, r], stats.shifted[:, r], k.minus_half[0:L, 0:4], ALU.pow
                       ).then_inc(k.stat_sem["inverted"], 1)


def norm_stats(nc, ctx, name):
    def sb(what, shape):
        return ctx.enter_context(nc.sbuf_tensor(f"{name}_{what}", shape, F32))
    stats = Shared()
    stats.six = sb("six", [L, B, 6])
    stats.mean_var = sb("mean_var", [L, B, 2])
    stats.shifted = sb("shifted", [L, B])
    stats.inverse = sb("inverse", [L, B])
    return stats


def norm_features(nc, k, ctx, name, dst, scale, offset, eps, split=None, state=None, add_row=None):
    def tile_of(t, half):
        if state is None:
            return by_batch(half_tokens(dst, t, half))
        return prev_tokens(dst, t, half, 1)

    with ExitStack() as own:
        own.callback(k.sems.end_phase)
        stats = norm_stats(nc, own, name)
        N = own.enter_context(nc.sbuf_tensor(f"{name}_N", [L, B, D], F32))
        tiles = Tiles(k, name, psum_banks(nc, own, f"{name}_ps", 8), [("T", 2 * KT, "ad")])
        n0 = k.norms
        k.norms += HALVES
        loaded = k.sems.take(f"{name}_loaded")
        row = own.enter_context(nc.sbuf_tensor(f"{name}_row", [L, D], F32)) if add_row is not None else None
        rounded = k.sems.take(f"{name}_rounded")
        block = own.enter_context(nc.Block())

        @block.sync
        def _(sp):
            if row is not None:
                sp.dma_start(row[:], add_row.partition_broadcast(L)).then_inc(loaded, 16)

        @block.gpsimd
        def _(pool):
            k.sems.clear_ended(pool)
            for half in range(HALVES):
                invert_half_pool(pool, k, stats, half, n0 + half)
            if state is not None:
                pool.tensor_copy(dst[:, :, :, 0], k.states[:, :, state, :])
            if row is not None:
                pool.wait_ge(loaded, 16)
                for b in range(B):
                    pool.wait_ge(k.stat_sem["normed"], 4 * n0 + b + 1)
                    pool.tensor_tensor(k.X[:, b, :], k.X[:, b, :], row[:], ALU.add)

        @block.tensor
        def _(pe):
            turn_tokens(pe, k, tiles, "T", N, lambda b: pe.wait_ge(k.stat_sem["normed"], 4 * n0 + b + 1))

        @block.scalar
        def _(act):
            for j in tiles.mine("a", "T"):
                half, t = divmod(j, KT)
                tiles.wait_filled(act, "T", j)
                act.activation(tile_of(t, half), by_batch(tiles.bank("T", j)[:, 0:HALF]), ACT.Identity,
                               bias=column(k, offset, t), scale=column(k, scale, t)).then_inc(tiles.emptied["a"], 1)
            if split is not None:
                round_tiles(act, tiles, "T", split, dst, rounded)

        @block.vector
        def _(dve):
            for half in range(HALVES):
                norm_half_dve(dve, k, k.X, N, stats, eps, half, n0 + half)
            for j in tiles.mine("d", "T"):
                half, t = divmod(j, KT)
                tiles.wait_filled(dve, "T", j)
                dve.tensor_scalar(tile_of(t, half), by_batch(tiles.bank("T", j)[:, 0:HALF]), column(k, scale, t),
                                  column(k, offset, t), ALU.mult, ALU.add).then_inc(tiles.emptied["d"], 1)
            if split is not None:
                split_tiles(dve, split, dst, rounded)


def load_features(sp, dst, src, sem):
    sp.dma_start(dst[:], src.rearrange("(k p) n -> p k n", p=P)).then_inc(sem, 16)


def mlp(nc, k, ctx, name, hT, w1, w2, bias1, func):
    CHUNK = 2
    CHUNKS = FT // CHUNK
    STEPS = HALVES * CHUNKS
    STAGES = 4
    pieces = [("up", 0)]
    for c in range(CHUNKS):
        pieces += [("up", c + 1)] * (c + 1 < CHUNKS) + [("down", c)]
    with ExitStack() as own:
        own.callback(k.sems.end_phase)
        up_w = Split(own, nc, f"{name}_up", [P, KT, F_MLP])
        down_w = Split(own, nc, f"{name}_down", [P, FT, D])
        staged = [own.enter_context(nc.sbuf_tensor(f"{name}_staged{i}", [P, CHUNK * D], F32)) for i in range(STAGES)]
        g = [own.enter_context(nc.sbuf_tensor(f"{name}_g{i}", [P, HALF], F32)) for i in range(2)]
        gT = [Split(own, nc, f"{name}_gT{i}", [P, CHUNK, HALF]) for i in range(2)]
        banks = psum_banks(nc, own, f"{name}_ps", 4)
        sums = psum_banks(nc, own, f"{name}_sums", 4)
        loaded = [k.sems.take(f"{name}_loaded{i}") for i in range(STAGES)]
        w_rounded = k.sems.take(f"{name}_w_rounded")
        w_split = k.sems.take(f"{name}_w_split")
        filled = k.sems.take(f"{name}_filled")
        activated = k.sems.take(f"{name}_activated")
        g_rounded = k.sems.take(f"{name}_g_rounded")
        g_split = k.sems.take(f"{name}_g_split")
        used = k.sems.take(f"{name}_used")
        added = k.sems.take(f"{name}_added")
        block = own.enter_context(nc.Block())

        def piece_of(kind, c):
            if kind == "up":
                cols = slice(c * CHUNK * P, (c + 1) * CHUNK * P)
                return up_w, lambda x: x[:, :, cols], lambda x: x[:].rearrange("p (k n) -> p k n", k=KT)
            return down_w, lambda x: x[:, c * CHUNK:(c + 1) * CHUNK, :], lambda x: x[:].rearrange("p (f n) -> p f n", n=D)

        @block.sync
        def _(sp):
            up = w1.rearrange("(k p) n -> p k n", p=P)
            down = w2.rearrange("(f p) n -> p f n", p=P)
            for n, (kind, c) in enumerate(pieces):
                if n >= STAGES:
                    sp.wait_ge(w_split, n - STAGES + 1)
                _, cut, view = piece_of(kind, c)
                sp.dma_start(view(staged[n % STAGES]), cut(up if kind == "up" else down)
                             ).then_inc(loaded[n % STAGES], 16)

        @block.gpsimd
        def _(pool):
            k.sems.clear_ended(pool)

        @block.tensor
        def _(pe):
            def make(step):
                half, c = divmod(step, CHUNKS)
                if half == 0:
                    pe.wait_ge(w_split, pieces.index(("up", c)) + 1)
                for f in range(CHUNK * c, CHUNK * (c + 1)):
                    n = half * FT + f
                    if n >= 4:
                        pe.wait_ge(activated, n - 3)
                    for t in range(KT):
                        mm = product(pe, banks[n % 4][:, 0:HALF], up_w, hT, lambda x: x[:, t, f * P:(f + 1) * P],
                                     lambda x: half_tokens(x, t, half), start=(t == 0), stop=(t == KT - 1))
                    mm.then_inc(filled, 1)

            def use(step):
                half, c = divmod(step, CHUNKS)
                if half == 0:
                    pe.wait_ge(w_split, pieces.index(("down", c)) + 1)
                pe.wait_ge(g_split, CHUNK * (step + 1))
                for b in range(4):
                    if half > 0 and c == 0:
                        pe.wait_ge(added, 4 * (half - 1) + b + 1)
                    for f in range(CHUNK):
                        mm = product(pe, sums[b][0:L, :], gT[step % 2], down_w, lambda x: x[:, f, b * L:(b + 1) * L],
                                     lambda x: x[:, CHUNK * c + f, :],
                                     start=(c == 0 and f == 0), stop=(c == CHUNKS - 1 and f == CHUNK - 1))
                mm.then_inc(used, 1)

            for step in range(STEPS):
                make(step)
                if step > 0:
                    use(step - 1)
            use(STEPS - 1)

        @block.scalar
        def _(act):
            def round_piece(kind, c):
                n = pieces.index((kind, c))
                weight, cut, view = piece_of(kind, c)
                act.wait_ge(loaded[n % STAGES], 16 * (n // STAGES + 1))
                weight.round(act, cut, view(staged[n % STAGES])).then_inc(w_rounded, 1)

            round_piece("up", 0)
            for step in range(STEPS):
                half, c = divmod(step, CHUNKS)
                if half == 0:
                    if c + 1 < CHUNKS:
                        round_piece("up", c + 1)
                    round_piece("down", c)
                for f in range(CHUNK):
                    n = step * CHUNK + f
                    act.wait_ge(filled, n + 1)
                    if n >= 2:
                        act.wait_ge(g_split, n - 1)
                    act.activation(g[n % 2][:], banks[n % 4][:, 0:HALF], func, bias=column(k, bias1, CHUNK * c + f)
                                   ).then_inc(activated, 1)
                    act.wait_ge(activated, n + 1)
                    if step >= 2:
                        act.wait_ge(used, step - 1)
                    gT[step % 2].round(act, lambda x: x[:, f, :], g[n % 2][:]).then_inc(g_rounded, 1)

        @block.vector
        def _(dve):
            def split_piece(kind, c):
                n = pieces.index((kind, c))
                weight, cut, view = piece_of(kind, c)
                dve.wait_ge(w_rounded, n + 1)
                weight.rest(dve, cut, view(staged[n % STAGES])).then_inc(w_split, 1)

            split_piece("up", 0)
            for step in range(STEPS):
                half, c = divmod(step, CHUNKS)
                if half == 0:
                    if c + 1 < CHUNKS:
                        split_piece("up", c + 1)
                    split_piece("down", c)
                for f in range(CHUNK):
                    n = step * CHUNK + f
                    dve.wait_ge(g_rounded, n + 1)
                    gT[step % 2].rest(dve, lambda x: x[:, f, :], g[n % 2][:]).then_inc(g_split, 1)
                if c == CHUNKS - 1:
                    dve.wait_ge(used, step + 1)
                    for b in range(4):
                        x = k.X[:, 4 * half + b, :]
                        dve.tensor_tensor(x, x, sums[b][0:L, :], ALU.add).then_inc(added, 1)


def layer0_output(nc, k, ins, ctx, split):
    with ExitStack() as own:
        own.callback(k.sems.end_phase)
        def sb(name, shape):
            return own.enter_context(nc.sbuf_tensor(name, shape, F32))

        out_w = sb("out_w", [P, KT, D])
        out_b = sb("out_b", [L, D])
        mlp_b2 = sb("mlp_b2", [L, D])
        attT = sb("attT", [P, KT, B * L])
        Y = sb("Y", [L, B, D])
        hT = sb("l0_whole", [P, KT, B * L])
        square = sb("square", [L, D])
        sum_squares = sb("sum_squares", [L, B])
        mean_square = sb("mean_square", [L, B])
        inverse = sb("inverse", [L, B])
        tiles = Tiles(k, "l0o", psum_banks(nc, own, "l0o_ps", 8),
                      [("attT", 2 * KT, "ad"), ("out", B, "d"), ("hT", 2 * KT, "ad")])
        loaded = k.sems.take("l0o_loaded")
        residual = k.sems.take("l0o_residual")
        squared = k.sems.take("l0o_squared")
        meaned = k.sems.take("l0o_meaned")
        inverted = k.sems.take("l0o_inverted")
        normed = k.sems.take("l0o_normed")
        rounded = k.sems.take("l0o_rounded")
        block = own.enter_context(nc.Block())

        @block.sync
        def _(sp):
            load_features(sp, out_w, ins["L0_xattn_out_w"], loaded)
            sp.dma_start(out_b[:], ins["L0_xattn_out_b"].partition_broadcast(L)).then_inc(loaded, 16)
            sp.dma_start(mlp_b2[:], ins["L0_xattn_mlp_b2"].partition_broadcast(L)).then_inc(loaded, 16)

        @block.tensor
        def _(pe):
            turn_tokens(pe, k, tiles, "attT", k.ATT, lambda b: None)
            pe.wait_ge(loaded, 48)
            project_tokens(pe, tiles, "out", attT, out_w, KT,
                           lambda b: tiles.wait_out(pe, "attT", range((b // 4) * KT, (b // 4 + 1) * KT)))
            turn_tokens(pe, k, tiles, "hT", Y, lambda b: pe.wait_ge(normed, b + 1))

        @block.gpsimd
        def _(pool):
            k.sems.clear_ended(pool)
            pool.wait_ge(loaded, 48)
            for b in range(B):
                pool.tensor_tensor(Y[:, b, :], k.X[:, b, :], out_b[:], ALU.add).then_inc(residual, 1)
            for half in range(HALVES):
                r = slice(4 * half, 4 * half + 4)
                pool.wait_ge(meaned, half + 1)
                pool.tensor_tensor(inverse[:, r], mean_square[:, r], k.minus_half[0:L, 0:4], ALU.pow
                                   ).then_inc(inverted, 1)
            for b in range(B):
                pool.wait_ge(residual, b + 1)
                pool.tensor_tensor(k.X[:, b, :], k.X[:, b, :], mlp_b2[:], ALU.add)

        @block.scalar
        def _(act):
            for j in tiles.mine("a", "attT"):
                tiles.wait_filled(act, "attT", j)
                act.activation(half_tokens(attT, j % KT, j // KT), tiles.bank("attT", j)[:, 0:HALF], ACT.Copy
                               ).then_inc(tiles.emptied["a"], 1)
            for b in range(B):
                tiles.wait_out(act, "out", [b])
                if b:
                    act.wait_ge(squared, b)
                act.activation(square[:], Y[:, b, :], ACT.Square, accum_out=sum_squares[:, b:b + 1]
                               ).then_inc(squared, 1)
            for j in tiles.mine("a", "hT"):
                tiles.wait_filled(act, "hT", j)
                act.activation(half_tokens(hT, j % KT, j // KT), tiles.bank("hT", j)[:, 0:HALF], ACT.Copy,
                               scale=column(k, "L0_xattn_postnorm_w", j % KT)).then_inc(tiles.emptied["a"], 1)
            round_tiles(act, tiles, "hT", split, hT, rounded)

        @block.vector
        def _(dve):
            for j in tiles.mine("d", "attT"):
                tiles.wait_filled(dve, "attT", j)
                dve.tensor_copy(half_tokens(attT, j % KT, j // KT), tiles.bank("attT", j)[:, 0:HALF]
                                ).then_inc(tiles.emptied["d"], 1)
            for half in range(HALVES):
                for c in range(4):
                    b = 4 * half + c
                    tiles.wait_filled(dve, "out", b)
                    dve.wait_ge(residual, b + 1)
                    dve.tensor_tensor(Y[:, b, :], Y[:, b, :], tiles.bank("out", b)[0:L, :], ALU.add
                                      ).then_inc(tiles.emptied["d"], 1)
                r = slice(4 * half, 4 * half + 4)
                dve.wait_ge(squared, 4 * half + 4)
                dve.tensor_scalar(mean_square[:, r], sum_squares[:, r], 1.0 / D, 1e-6, ALU.mult, ALU.add
                                  ).then_inc(meaned, 1)
                dve.wait_ge(inverted, half + 1)
                for c in range(4):
                    b = 4 * half + c
                    dve.tensor_scalar(Y[:, b, :], Y[:, b, :], inverse[:, b:b + 1], None, ALU.mult
                                      ).then_inc(normed, 1)
            for j in tiles.mine("d", "hT"):
                tiles.wait_filled(dve, "hT", j)
                dve.tensor_scalar(half_tokens(hT, j % KT, j // KT), tiles.bank("hT", j)[:, 0:HALF],
                                  column(k, "L0_xattn_postnorm_w", j % KT), None, ALU.mult
                                  ).then_inc(tiles.emptied["d"], 1)
            split_tiles(dve, split, hT, rounded)


H1, N1 = 32, 16
F_MIX = 32
BRANCHES = ("w", "k", "v", "r", "g")
L_DECAY = 64
PREV = L + 1


def prev_tokens(t, tile, half, first):
    return t[:, tile, 4 * half:4 * half + 4, first:first + L]


def by_batch(ap):
    return ap.rearrange("p (b l) -> p b l", l=L)


def turn_weight(pe, k, tiles, stage, src, ready):
    for t in range(KT):
        tiles.wait_free(pe, stage, t)
        if t == 0:
            ready()
        for m in range(KT):
            mm = pe.transpose(tiles.bank(stage, t)[:, m * P:(m + 1) * P], src[:, m, t * P:(t + 1) * P], k.ident[:])
        mm.then_inc(tiles.filled, 1)


def copy_weight(tiles, engine, eng, stage, dst):
    for t in tiles.mine(engine, stage):
        tiles.wait_filled(eng, stage, t)
        if engine == "a":
            eng.activation(dst[:, t, :], tiles.bank(stage, t)[:], ACT.Copy).then_inc(tiles.emptied["a"], 1)
        else:
            eng.tensor_copy(dst[:, t, :], tiles.bank(stage, t)[:]).then_inc(tiles.emptied["d"], 1)


def project_features(pe, tiles, stage, weights, src, n_k, ready=None):
    for m in range(KT):
        for half in range(HALVES):
            j = m * HALVES + half
            tiles.wait_free(pe, stage, j)
            if ready is not None:
                ready(j)
            for t in range(n_k):
                mm = pe.matmul(tiles.bank(stage, j)[:, 0:HALF], weights(t, m), src(t, half),
                               start=(t == 0), stop=(t == n_k - 1))
            mm.then_inc(tiles.filled, 1)


def layer1_mixing(nc, k, ins, ctx, xa, T):
    with ExitStack() as own:
        own.callback(k.sems.end_phase)
        def sb(name, shape):
            return own.enter_context(nc.sbuf_tensor(name, shape, F32))

        def sem(name):
            return k.sems.take(name)

        sx = sb("sx", [P, KT, B * L])
        mixed = [sb(f"mixed{i}", [P, KT, B * L]) for i in range(2)]
        w1 = sb("maa_w1", [P, KT, 5 * F_MIX])
        w2 = sb("maa_w2", [P, 4, D])
        w2_last = sb("maa_w2_last", [F_MIX, D])
        t_four = sb("t_four", [P, B * L])
        t_last = sb("t_last", [F_MIX, B * L])
        dw1 = sb("decay_w1", [P, KT, L_DECAY])
        dw2 = sb("decay_w2", [L_DECAY, D])
        t_decay = sb("t_decay", [L_DECAY, B * L])
        natural = [sb(f"W_natural{i}", [P, KT, D]) for i in range(2)]
        turned = [sb(f"W_turned{i}", [P, KT, D]) for i in range(2)]
        stages = [("t", 4, "a")]
        for n, f in enumerate(BRANCHES):
            if f != "w":
                stages.append((f"W{f}", KT, "ad"))
            stages.append((f"mix_{f}", 2 * KT, "d"))
            if f == "w":
                stages += [("decay1", HALVES, "a"), ("decay2", 2 * KT, "a")]
            else:
                stages.append((f"out_{f}", 2 * KT, "a"))
        tiles = Tiles(k, "l1m", psum_banks(nc, own, "l1m_ps", 8), stages)
        zeroed = sem("l1m_zeroed")
        small = sem("l1m_small_loaded")
        W_loaded = {f: sem(f"l1m_W{f}_loaded") for f in BRANCHES[1:]}
        differed = sem("l1m_differed")
        first_mixed = sem("l1m_first_mixed")
        completed = sem("l1m_completed")
        exped = sem("l1m_exped")
        block = own.enter_context(nc.Block())

        @block.sync
        def _(sp):
            load_features(sp, w1, ins["L1_xattn_maa_w1"], small)
            sp.wait_ge(zeroed, 1)
            for f in range(4):
                sp.dma_start(w2[F_MIX * f:F_MIX * (f + 1), f, :], ins["L1_xattn_maa_w2"][f]).then_inc(small, 16)
            sp.dma_start(w2_last[:], ins["L1_xattn_maa_w2"][4]).then_inc(small, 16)
            load_features(sp, dw1, ins["L1_xattn_decay_w1"], small)
            sp.dma_start(dw2[:], ins["L1_xattn_decay_w2"]).then_inc(small, 16)
            for n, f in enumerate(BRANCHES[1:]):
                if n >= 2:
                    tiles.wait_out(sp, f"W{BRANCHES[n - 1]}")
                sp.dma_start(natural[n % 2][:], ins[f"L1_xattn_W{f}"].rearrange("(m p) i -> p m i", p=P)
                             ).then_inc(W_loaded[f], 16)

        @block.tensor
        def _(pe):
            pe.wait_ge(small, 16 * 8)
            for half in range(HALVES):
                for part in range(2):
                    j = 2 * half + part
                    tiles.wait_free(pe, "t", j)
                    for t in range(KT):
                        if j == 0:
                            pe.wait_ge(first_mixed, t + 1)
                        rows = slice(0, P) if part == 0 else slice(P, P + F_MIX)
                        n = rows.stop - rows.start
                        mm = pe.matmul(tiles.bank("t", j)[0:n, 0:HALF], w1[:, t, rows],
                                       half_tokens(mixed[0], t, half), start=(t == 0), stop=(t == KT - 1))
                    mm.then_inc(tiles.filled, 1)
            for n, f in enumerate(BRANCHES):
                W = n - 1
                if f != "w":
                    turn_weight(pe, k, tiles, f"W{f}", natural[W % 2], lambda: pe.wait_ge(W_loaded[f], 16))
                if n == 0:
                    tiles.wait_out(pe, "t")
                if n < 4:
                    project_features(pe, tiles, f"mix_{f}", lambda t, m: w2[:, n, m * P:(m + 1) * P],
                                     lambda t, half: t_four[:, half * HALF:(half + 1) * HALF], 1)
                else:
                    project_features(pe, tiles, f"mix_{f}", lambda t, m: w2_last[:, m * P:(m + 1) * P],
                                     lambda t, half: t_last[:, half * HALF:(half + 1) * HALF], 1)
                m_in = mixed[(n + 1) % 2]
                if f == "w":
                    for half in range(HALVES):
                        tiles.wait_free(pe, "decay1", half)
                        pe.wait_ge(completed, 2 * KT * (n + 1))
                        for t in range(KT):
                            mm = pe.matmul(tiles.bank("decay1", half)[0:L_DECAY, 0:HALF], dw1[:, t, :],
                                           half_tokens(m_in, t, half), start=(t == 0), stop=(t == KT - 1))
                        mm.then_inc(tiles.filled, 1)
                    tiles.wait_out(pe, "decay1")
                    project_features(pe, tiles, "decay2", lambda t, m: dw2[:, m * P:(m + 1) * P],
                                     lambda t, half: t_decay[:, half * HALF:(half + 1) * HALF], 1)
                else:
                    pe.wait_ge(completed, 2 * KT * (n + 1))
                    tiles.wait_out(pe, f"W{f}")
                    project_features(pe, tiles, f"out_{f}", lambda t, m: turned[W % 2][:, t, m * P:(m + 1) * P],
                                     lambda t, half: half_tokens(m_in, t, half), KT)

        @block.scalar
        def _(act):
            for half in range(HALVES):
                for part in range(2):
                    j = 2 * half + part
                    tiles.wait_filled(act, "t", j)
                    dst = t_four if part == 0 else t_last
                    n = P if part == 0 else F_MIX
                    act.activation(dst[:, half * HALF:(half + 1) * HALF], tiles.bank("t", j)[0:n, 0:HALF], ACT.Tanh
                                   ).then_inc(tiles.emptied["a"], 1)
            for n, f in enumerate(BRANCHES):
                if f == "w":
                    for half in range(HALVES):
                        tiles.wait_filled(act, "decay1", half)
                        act.activation(t_decay[:, half * HALF:(half + 1) * HALF],
                                       tiles.bank("decay1", half)[0:L_DECAY, 0:HALF], ACT.Tanh
                                       ).then_inc(tiles.emptied["a"], 1)
                    for j in range(2 * KT):
                        m, half = divmod(j, HALVES)
                        tiles.wait_filled(act, "decay2", j)
                        w = prev_tokens(T["w"], m, half, 1)
                        act.activation(w, by_batch(tiles.bank("decay2", j)[:, 0:HALF]), ACT.Exp,
                                       bias=column(k, "L1_xattn_time_decay", m)).then_inc(tiles.emptied["a"], 1)
                        tiles.wait_out(act, "decay2", [j])
                        act.activation(w, w, ACT.Exp, scale=-1.0)
                else:
                    copy_weight(tiles, "a", act, f"W{f}", turned[(n - 1) % 2])
                    for j in range(2 * KT):
                        m, half = divmod(j, HALVES)
                        tiles.wait_filled(act, f"out_{f}", j)
                        act.activation(half_tokens(T[f], m, half), tiles.bank(f"out_{f}", j)[:, 0:HALF],
                                       ACT.Silu if f == "g" else ACT.Copy).then_inc(tiles.emptied["a"], 1)

        @block.vector
        def _(dve):
            dve.memset(w2[:], 0.0).then_inc(zeroed, 1)
            dve.memset(T["w"][:, :, :, 0], 0.0)
            for t in range(KT):
                dve.tensor_tensor(by_batch(sx[:, t, :]), xa[:, t, :, 0:L], xa[:, t, :, 1:PREV], ALU.subtract
                                  ).then_inc(differed, 1)
            for t in range(KT):
                dve.wait_ge(differed, t + 1)
                dve.scalar_tensor_tensor(by_batch(mixed[0][:, t, :]), by_batch(sx[:, t, :]),
                                         column(k, "L1_xattn_maa_x", t), xa[:, t, :, 1:PREV], ALU.mult, ALU.add
                                         ).then_inc(first_mixed, 1)
            for n, f in enumerate(BRANCHES):
                if f != "w":
                    copy_weight(tiles, "d", dve, f"W{f}", turned[(n - 1) % 2])
                if n == 1:
                    tiles.wait_out(dve, "t")
                for j in range(2 * KT):
                    m, half = divmod(j, HALVES)
                    tiles.wait_filled(dve, f"mix_{f}", j)
                    if n >= 2 and j == 0:
                        back = BRANCHES[n - 2]
                        tiles.wait_filled(dve, "decay1" if back == "w" else f"out_{back}",
                                          (HALVES if back == "w" else 2 * KT) - 1)
                    dve.scalar_tensor_tensor(half_tokens(mixed[(n + 1) % 2], m, half),
                                             tiles.bank(f"mix_{f}", j)[:, 0:HALF], column(k, f"L1_xattn_maa_{f}", m),
                                             half_tokens(sx, m, half), ALU.add, ALU.mult
                                             ).then_inc(tiles.emptied["d"], 1)

        @block.gpsimd
        def _(pool):
            k.sems.clear_ended(pool)
            for n, f in enumerate(BRANCHES):
                for j in range(2 * KT):
                    m, half = divmod(j, HALVES)
                    tiles.wait_out(pool, f"mix_{f}", [j])
                    dst = by_batch(half_tokens(mixed[(n + 1) % 2], m, half))
                    pool.tensor_tensor(dst, dst, prev_tokens(xa, m, half, 1), ALU.add).then_inc(completed, 1)


def layer1_scan(nc, k, ins, ctx, T, yT):
    context = ins["ctx_2048"]
    with ExitStack() as own:
        own.callback(k.sems.end_phase)
        def sb(name, shape):
            return own.enter_context(nc.sbuf_tensor(name, shape, F32))

        def sem(name):
            return k.sems.take(name)

        start = sb("start_state", [P, KT, B, N1])
        spread = sb("spread", [P, N1, P])
        gather = sb("gather", [P, N1, P])
        rows = sb("row_in_head", [P, N1])
        kv = [sb(f"kv{i}", [P, B, PREV]) for i in range(2)]
        state = [sb(f"state{i}", [P, B, PREV]) for i in range(2)]
        rs = [sb(f"rs{i}", [P, B, L]) for i in range(2)]
        r_tile = sb("r_tile", [P, B * L])
        ps_v = [own.enter_context(nc.psum_tensor(f"ps_v{i}", [P, HALVES, 512], F32)) for i in range(2)]
        ps_y = [own.enter_context(nc.psum_tensor(f"ps_y{i}", [P, HALVES, 512], F32)) for i in range(2)]

        loaded = sem("l1s_loaded")
        built = sem("l1s_built")
        spreaded = sem("l1s_spread")
        started = sem("l1s_started")
        keyed = sem("l1s_keyed")
        scanned = sem("l1s_scanned")
        received = sem("l1s_received")
        gathered = sem("l1s_gathered")
        y_copied = sem("l1s_y_copied")
        r_copied = sem("l1s_r_copied")
        block = own.enter_context(nc.Block())

        @block.sync
        def _(sp):
            for b in range(B):
                src = context[b, 2:2 + N1, :].rearrange("r d -> (r d)").rearrange("(k p t) -> p k t", p=P, t=N1)
                with nc.allow_non_contiguous_dma("64-byte rows of the starting state"):
                    sp.dma_start(start[:, :, b, :], src).then_inc(loaded, 16)

        @block.gpsimd
        def _(pool):
            k.sems.clear_ended(pool)
            pool.sem_inc(received, 2 * N1)
            with pool.Fori(0, KT) as m:
                for t in range(N1):
                    if t == 0:
                        pool.wait_ge(r_copied, at(m, 1, 0))
                    pool.wait_ge(scanned, at(m, N1, t))
                    pool.wait_ge(gathered, at(m, N1, t - 2))
                    pool.tensor_tensor(rs[t % 2][:], by_batch(r_tile[:]),
                                       state[t % 2][:, :, 0:L], ALU.mult).then_inc(received, 1)

        @block.vector
        def _(dve):
            dve.sem_inc(keyed, 2 * N1)
            dve.sem_inc(scanned, 2 * N1)
            ident = k.ident[:].rearrange("p (h t) -> p h t", t=N1)
            dve.tensor_reduce(rows[:], k.ident[:].rearrange("p (h t) -> p t h", t=N1), AX.X, ALU.add)
            dve.tensor_reduce(k.head_of[:], ident, AX.X, ALU.add)
            dve.memset(gather[:], 0.0).then_inc(built, 1)
            dve.wait_ge(built, 1)
            dve.tensor_copy(k.same_head[:].rearrange("p (h t) -> p h t", t=N1),
                            k.head_of[:].unsqueeze(2).broadcast_to([P, P // N1, N1])).then_inc(built, 1)
            dve.wait_ge(built, 2)
            for t in range(N1):
                dve.tensor_scalar(spread[:, t, :], k.same_head[:], rows[:, t:t + 1], None, ALU.mult)
                last = dve.tensor_copy(gather[:, t, t:P:N1], k.same_head[:, t:P:N1])
            last.then_inc(built, 1)
            with dve.Fori(0, KT) as m:
                for t in range(N1 + 1):
                    if t < N1:
                        dve.wait_ge(spreaded, at(m, N1, t))
                        dve.wait_ge(scanned, at(m, N1, t - 2))
                        dve.tensor_tensor(
                            kv[t % 2][:, :, 1:PREV].rearrange("p (h b) l -> p h b l", h=HALVES),
                            ps_v[t % 2][:, :, 0:HALF].rearrange("p h (b l) -> p h b l", l=L),
                            T["k"][:, bass.ds(m, 1), :].squeeze(1).rearrange("p (h b l) -> p h b l", h=HALVES, l=L),
                            ALU.mult).then_inc(keyed, 1)
                    if t > 0:
                        u = t - 1
                        dve.wait_ge(keyed, at(m, N1, u))
                        dve.wait_ge(started, at(m, N1, u))
                        dve.wait_ge(received, at(m, N1, u - 2))
                        dve.tensor_tensor_scan(
                            state[u % 2][:].rearrange("p b l -> p (b l)"),
                            T["w"][:, bass.ds(m, 1), :, :].squeeze(1).rearrange("p b l -> p (b l)"),
                            kv[u % 2][:].rearrange("p b l -> p (b l)"), 0.0, ALU.mult, ALU.add).then_inc(scanned, 1)

        @block.scalar
        def _(act):
            act.sem_inc(started, 2 * N1)
            act.sem_inc(y_copied, 2)
            act.sem_inc(r_copied, 2)
            act.wait_ge(loaded, 16 * B)
            with act.Fori(0, KT) as m:
                act.wait_ge(received, at(m, N1, -1))
                act.activation(r_tile[:], T["r"][:, bass.ds(m, 1), :].squeeze(1), ACT.Copy).then_inc(r_copied, 1)
                for t in range(N1):
                    act.wait_ge(scanned, at(m, N1, t - 2))
                    act.activation(kv[t % 2][:, :, 0], start[:, bass.ds(m, 1), :, t].squeeze(1), ACT.Copy
                                   ).then_inc(started, 1)
                act.wait_ge(gathered, at(m, N1, N1 - 1))
                act.activation(yT[:, bass.ds(m, 1), :].squeeze(1).rearrange("p (h n) -> p h n", h=HALVES),
                               ps_y[0][:, :, 0:HALF], ACT.Copy).then_inc(y_copied, 1)

        @block.tensor
        def _(pe):
            pe.sem_inc(spreaded, 2 * N1)
            pe.sem_inc(gathered, 2 * N1)
            pe.wait_ge(built, 3)
            with pe.Fori(0, KT) as m:
                for t in range(N1 + 2):
                    if t < N1:
                        pe.wait_ge(keyed, at(m, N1, t - 2))
                        for half in range(HALVES):
                            mm = pe.matmul(ps_v[t % 2][:, half, 0:HALF], spread[:, t, :],
                                           T["v"][:, bass.ds(m, 1), half * HALF:(half + 1) * HALF].squeeze(1),
                                           start=True, stop=True)
                        mm.then_inc(spreaded, 1)
                    if t >= 2:
                        u = t - 2
                        pe.wait_ge(received, at(m, N1, u))
                        if u == 0:
                            pe.wait_ge(y_copied, at(m, 1, -1))
                        for half in range(HALVES):
                            mm = pe.matmul(ps_y[0][:, half, 0:HALF], gather[:, u, :],
                                           rs[u % 2][:].rearrange("p b l -> p (b l)")[:, half * HALF:(half + 1) * HALF],
                                           start=(u == 0), stop=(u == N1 - 1))
                        mm.then_inc(gathered, 1)


def layer1_output(nc, k, ins, ctx, T, yT):
    with ExitStack() as own:
        own.callback(k.sems.end_phase)
        def sb(name, shape):
            return own.enter_context(nc.sbuf_tensor(name, shape, F32))

        def sem(name):
            return k.sems.take(name)

        natural = sb("Wo_natural", [P, KT, D])
        turned = sb("Wo_turned", [P, KT, D])
        head_mean = sb("head_mean", [P, P])
        own_key = sb("own_key", [P, KT, B * L])
        square = sb("y_square", [P, KT, B * L])
        tiles = Tiles(k, "l1o", psum_banks(nc, own, "l1o_ps", 8),
                      [("Wo", KT, "a"), ("own", 2 * KT, "d"), ("mean", 2 * KT, "d"), ("var", 2 * KT, "a"),
                       ("out", B, "d")])
        loaded = sem("l1o_loaded")
        built = sem("l1o_built")
        keyed = sem("l1o_keyed")
        added = sem("l1o_added")
        squared = sem("l1o_squared")
        inverted = sem("l1o_inverted")
        scaled = sem("l1o_scaled")
        block = own.enter_context(nc.Block())

        def tile_of(t, j):
            return half_tokens(t, j // HALVES, j % HALVES)

        @block.sync
        def _(sp):
            sp.dma_start(natural[:], ins["L1_xattn_Wo"].rearrange("(m p) i -> p m i", p=P)).then_inc(loaded, 16)

        @block.tensor
        def _(pe):
            turn_weight(pe, k, tiles, "Wo", natural, lambda: pe.wait_ge(loaded, 16))
            for stage, weights, src, ready in (
                    ("own", k.same_head, own_key, lambda j: pe.wait_ge(keyed, KT + j // HALVES + 1)),
                    ("mean", head_mean, yT, lambda j: pe.wait_ge(added, j + 1)),
                    ("var", head_mean, square, lambda j: pe.wait_ge(squared, j + 1))):
                for j in range(2 * KT):
                    tiles.wait_free(pe, stage, j)
                    ready(j)
                    pe.matmul(tiles.bank(stage, j)[:, 0:HALF], weights[:], tile_of(src, j), start=True, stop=True
                              ).then_inc(tiles.filled, 1)
            pe.wait_ge(scaled, 3 * 2 * KT)
            tiles.wait_out(pe, "Wo")
            project_tokens(pe, tiles, "out", yT, turned, KT)

        @block.scalar
        def _(act):
            copy_weight(tiles, "a", act, "Wo", turned)
            for j in range(2 * KT):
                tiles.wait_out(act, "mean", [j])
                act.activation(tile_of(square, j), tile_of(yT, j), ACT.Square).then_inc(squared, 1)
            for j in range(2 * KT):
                tiles.wait_filled(act, "var", j)
                act.activation(tile_of(own_key, j), tiles.bank("var", j)[:, 0:HALF], ACT.Sqrt, bias=k.eps5[:]
                               ).then_inc(tiles.emptied["a"], 1)

        @block.gpsimd
        def _(pool):
            k.sems.clear_ended(pool)
            for j in range(2 * KT):
                tiles.wait_out(pool, "own", [j])
                pool.tensor_tensor(tile_of(yT, j), tile_of(yT, j), tile_of(square, j), ALU.add).then_inc(added, 1)

        @block.vector
        def _(dve):
            dve.tensor_scalar(head_mean[:], k.same_head[:], 1.0 / N1, None, ALU.mult).then_inc(built, 1)
            for t in range(KT):
                dve.scalar_tensor_tensor(own_key[:, t, :], T["r"][:, t, :], column(k, "L1_xattn_faaaa", t),
                                         T["k"][:, t, :], ALU.mult, ALU.mult).then_inc(keyed, 1)
            dve.wait_ge(keyed, KT)
            dve.wait_ge(built, 1)
            dve.sem_inc(keyed, KT)
            for j in range(2 * KT):
                tiles.wait_filled(dve, "own", j)
                dve.tensor_tensor(tile_of(square, j), tiles.bank("own", j)[:, 0:HALF], tile_of(T["v"], j), ALU.mult
                                  ).then_inc(tiles.emptied["d"], 1)
            for j in range(2 * KT):
                tiles.wait_filled(dve, "mean", j)
                dve.tensor_tensor(tile_of(yT, j), tile_of(yT, j), tiles.bank("mean", j)[:, 0:HALF], ALU.subtract
                                  ).then_inc(tiles.emptied["d"], 1)
            for j in range(2 * KT):
                tiles.wait_out(dve, "var", [j])
                dve.reciprocal(tile_of(square, j), tile_of(own_key, j)).then_inc(inverted, 1)
                dve.wait_ge(inverted, j + 1)
                dve.tensor_tensor(tile_of(yT, j), tile_of(yT, j), tile_of(square, j), ALU.mult).then_inc(scaled, 1)
                dve.wait_ge(scaled, 3 * j + 1)
                m = j // HALVES
                dve.tensor_scalar(tile_of(yT, j), tile_of(yT, j), column(k, "L1_xattn_gn_w", m),
                                  column(k, "L1_xattn_gn_b", m), ALU.mult, ALU.add).then_inc(scaled, 1)
                dve.wait_ge(scaled, 3 * j + 2)
                dve.tensor_tensor(tile_of(yT, j), tile_of(yT, j), tile_of(T["g"], j), ALU.mult).then_inc(scaled, 1)
            for b in range(B):
                tiles.wait_filled(dve, "out", b)
                dve.tensor_tensor(k.X[:, b, :], k.X[:, b, :], tiles.bank("out", b)[0:L, :], ALU.add
                                  ).then_inc(tiles.emptied["d"], 1)


def layer1_channel_mix(nc, k, ins, ctx, xc):
    with ExitStack() as own:
        own.callback(k.sems.end_phase)
        def sb(name, shape):
            return own.enter_context(nc.sbuf_tensor(name, shape, F32))

        def sem(name):
            return k.sems.take(name)

        names = ("fWk", "fWr", "fWv")
        natural = {n: sb(f"{n}_natural", [P, KT, D]) for n in names}
        turned = {n: sb(f"{n}_turned", [P, KT, D]) for n in names}
        sx = sb("sxc", [P, KT, B * L])
        xk = sb("xk", [P, KT, B * L])
        xr = sb("xr", [P, KT, B * L])
        kk = sb("kk", [P, KT, B * L])
        rr = sb("rr", [L, B, D])
        tiles = Tiles(k, "l1c", psum_banks(nc, own, "l1c_ps", 8),
                      [(n, KT, "ad") for n in names] + [("kk", 2 * KT, "a"), ("rr", B, "a"), ("out", B, "d")])
        loaded = {n: sem(f"l1c_{n}_loaded") for n in names}
        differed = sem("l1c_differed")
        mixed = sem("l1c_mixed")
        squared = sem("l1c_squared")
        block = own.enter_context(nc.Block())

        @block.sync
        def _(sp):
            for n in names:
                sp.dma_start(natural[n][:], ins[f"L1_xattn_{n}"].rearrange("(m p) i -> p m i", p=P)
                             ).then_inc(loaded[n], 16)

        @block.tensor
        def _(pe):
            for n in names:
                turn_weight(pe, k, tiles, n, natural[n], lambda: pe.wait_ge(loaded[n], 16))
            tiles.wait_out(pe, "fWk")
            pe.wait_ge(mixed, KT)
            project_features(pe, tiles, "kk", lambda t, m: turned["fWk"][:, t, m * P:(m + 1) * P],
                             lambda t, half: half_tokens(xk, t, half), KT)
            tiles.wait_out(pe, "fWr")
            tiles.wait_out(pe, "fWv")
            pe.wait_ge(mixed, 2 * KT)
            project_tokens(pe, tiles, "rr", xr, turned["fWr"], KT)
            pe.wait_ge(squared, 2 * KT)
            project_tokens(pe, tiles, "out", kk, turned["fWv"], KT)

        @block.scalar
        def _(act):
            for n in names:
                copy_weight(tiles, "a", act, n, turned[n])
            for j in range(2 * KT):
                tiles.wait_filled(act, "kk", j)
                act.activation(half_tokens(kk, j // HALVES, j % HALVES), tiles.bank("kk", j)[:, 0:HALF], ACT.Relu
                               ).then_inc(tiles.emptied["a"], 1)
            for b in range(B):
                tiles.wait_filled(act, "rr", b)
                act.activation(rr[:, b, :], tiles.bank("rr", b)[0:L, :], ACT.Sigmoid).then_inc(tiles.emptied["a"], 1)

        @block.gpsimd
        def _(pool):
            k.sems.clear_ended(pool)
            for j in range(2 * KT):
                tiles.wait_out(pool, "kk", [j])
                t = half_tokens(kk, j // HALVES, j % HALVES)
                pool.tensor_tensor(t, t, t, ALU.mult).then_inc(squared, 1)
            for b in range(B):
                tiles.wait_out(pool, "out", [b])
                pool.tensor_tensor(k.X[:, b, :], k.X[:, b, :], rr[:, b, :], ALU.add)

        @block.vector
        def _(dve):
            copy = lambda n: copy_weight(tiles, "d", dve, n, turned[n])
            for t in range(KT):
                dve.tensor_tensor(by_batch(sx[:, t, :]), xc[:, t, :, 0:L], xc[:, t, :, 1:PREV], ALU.subtract
                                  ).then_inc(differed, 1)
            copy("fWk")
            dve.wait_ge(differed, KT)
            for dst, mix in ((xk, "L1_xattn_fmaa_k"), (xr, "L1_xattn_fmaa_r")):
                for t in range(KT):
                    dve.scalar_tensor_tensor(by_batch(dst[:, t, :]), by_batch(sx[:, t, :]), column(k, mix, t),
                                             xc[:, t, :, 1:PREV], ALU.mult, ALU.add).then_inc(mixed, 1)
            copy("fWr")
            copy("fWv")
            for b in range(B):
                tiles.wait_filled(dve, "out", b)
                tiles.wait_out(dve, "rr", [b])
                dve.tensor_tensor(rr[:, b, :], rr[:, b, :], tiles.bank("out", b)[0:L, :], ALU.mult
                                  ).then_inc(tiles.emptied["d"], 1)


def layer1(nc, k, ins, ctx):
    with ExitStack() as own:
        def sb(name, shape):
            return own.enter_context(nc.sbuf_tensor(name, shape, F32))

        k.same_head = sb("same_head", [P, P])
        T = {f: sb(f"T_{f}", [P, KT, B * L]) for f in "rkvg"}
        T["w"] = sb("T_w", [P, KT, B, PREV])
        with ExitStack() as inner:
            xa = inner.enter_context(nc.sbuf_tensor("xa", [P, KT, B, PREV], F32))
            norm_features(nc, k, ctx, "ln1", xa, "L1_xattn_ln1_w", "L1_xattn_ln1_b", 1e-5, state=1)
            layer1_mixing(nc, k, ins, ctx, xa, T)
        yT = sb("yT", [P, KT, B * L])
        layer1_scan(nc, k, ins, ctx, T, yT)
        layer1_output(nc, k, ins, ctx, T, yT)
    with ExitStack() as own:
        xc = own.enter_context(nc.sbuf_tensor("xc", [P, KT, B, PREV], F32))
        norm_features(nc, k, ctx, "ln2", xc, "L1_xattn_ln2_w", "L1_xattn_ln2_b", 1e-5, state=0)
        layer1_channel_mix(nc, k, ins, ctx, xc)



H2, DH2 = 16, 128
G2 = 4
N_GROUPS = H2 // G2
QUAD = 4
UNITS = QUAD * G2
T2 = 121
NT2 = 3
N2 = T2 * NT2
KEYS2 = 1 + S
WEIGHTS2 = ("wq", "wk", "wv", "wo")


def unit_of(x):
    return divmod(x, G2)


ROUND_TILES = [("q", j) for j in range(G2)]
for _j in range(G2):
    ROUND_TILES += [("k", 0, _j)] + [("v", 0, _j)] * (_j < NT2)
for _x in range(UNITS - G2):
    _c, _j = unit_of(_x)
    ROUND_TILES += [("k", _c + 1, _j)] + [("v", _c + 1, _j)] * (_j < NT2)
ROUND_TILES += [("out", _c) for _c in range(QUAD)]
TILES2 = len(ROUND_TILES)
ACT_TILES2 = [n for n, tile in enumerate(ROUND_TILES) if tile[0] == "k"]
DVE_TILES2 = [n for n, tile in enumerate(ROUND_TILES) if tile[0] != "k"]


def layer2_attention(nc, k, ins, ctx, layer, hT):
    w = {n: ins[f"L2_xattn_{n}{layer}"] for n in WEIGHTS2}
    W = G2 * DH2
    with ExitStack() as own:
        own.callback(k.sems.end_phase)
        def sb(name, shape):
            return own.enter_context(nc.sbuf_tensor(f"{name}_layer{layer}", shape, F32))

        def split(name, shape):
            return Split(own, nc, f"{name}_layer{layer}", shape)

        def sem(name):
            return k.sems.take(f"{name}_layer{layer}")

        staged = [sb(f"staged{i}", [P, KT, W]) for i in range(2)]
        weights = {n: split(n, [P, KT, W]) for n in WEIGHTS2}
        key_bias = sb("key_bias", [P, H2])
        group_key_bias = sb("group_key_bias", [P, G2])
        group_q_bias = sb("group_q_bias", [P, G2])
        value_bias = sb("value_bias", [T2, 2, W])
        cT = [split(f"cT{s}", [P, KT, N2]) for s in range(2)]
        keysT = [sb(f"keysT2_{s}", [P, G2, KEYS2]) for s in range(2)]
        values = [sb(f"values2_{s}", [T2, NT2, W]) for s in range(2)]
        qT = sb("qT", [P, G2, HALF])
        probs = [sb(f"p{i}", [L, N2]) for i in range(4)]
        probsT = [sb(f"pT{i}", [T2, NT2, L]) for i in range(2)]
        oT = split("oT", [P, QUAD, G2 * L])
        neg_max = sb("neg_max2", [L, UNITS])
        sums = sb("sums2", [L, UNITS])
        inverse = sb("inverse2", [L, UNITS])

        work = psum_banks(nc, own, f"work2_{layer}_", 3)
        ps_scores = psum_banks(nc, own, f"scores2_{layer}_", 2)
        ps_turned = psum_banks(nc, own, f"turned2_{layer}_", 2)
        ps_o = psum_banks(nc, own, f"o2_{layer}_", 1)[0]

        zeroed = sem("zeroed2")
        w_loaded = {n: sem(f"{n}_loaded2") for n in WEIGHTS2}
        bias_loaded = sem("bias_loaded2")
        cT_loaded = [sem(f"cT_loaded{s}") for s in range(2)]
        biased = sem("biased2")
        grouped = sem("grouped2")
        w_rounded = sem("w_rounded2")
        w_split = sem("w_split2")
        tile_done = sem("tile_done2")
        act_copied = sem("act_copied2")
        dve_copied = sem("dve_copied2")
        key_placed = sem("key_placed2")
        scored = sem("scored2")
        maxed = sem("maxed2")
        exped = sem("exped2")
        inverted = sem("inverted2")
        scaled = sem("scaled2")
        turned = sem("turned2")
        turned_copied = sem("turned_copied2")
        attended = sem("attended2")
        o_rounded = sem("o_rounded2")
        o_split = sem("o_split2")

        def wait_done(eng, r, *tile):
            eng.wait_ge(tile_done, at(r, TILES2, ROUND_TILES.index(tile)))

        def wait_copied(eng, r, tile):
            if tile < 0:
                r, tile = r - 1, tile + TILES2
            if tile in ACT_TILES2:
                eng.wait_ge(act_copied, at(r, len(ACT_TILES2), ACT_TILES2.index(tile)))
            else:
                eng.wait_ge(dve_copied, at(r, len(DVE_TILES2), DVE_TILES2.index(tile)))

        def wait_tile(eng, r, *tile):
            wait_copied(eng, r, ROUND_TILES.index(tile))

        assert TILES2 % len(work) == 0

        def bank(*tile):
            return work[ROUND_TILES.index(tile) % len(work)]

        def wait_group_before(eng, group):
            wait_done(eng, HALVES * group - 1, "out", QUAD - 1)

        block = own.enter_context(nc.Block())

        @block.sync
        def _(sp):
            with sp.Fori(0, N_GROUPS) as group:
                cols = bass.ds(group * W, W)
                for m, n in enumerate(WEIGHTS2):
                    sp.wait_ge(w_split, 4 * KT * (group + 1) + KT * (m - 1))
                    src = w[n].rearrange("(k p) n -> p k n", p=P)
                    src = src[:, bass.ds(group * G2, G2), :] if n == "wo" else src[:, :, cols]
                    sp.dma_start(staged[m % 2][:], src).then_inc(w_loaded[n], 16)
                    if m == 1:
                        wait_tile(sp, HALVES * group - 1, "v", QUAD - 1, NT2 - 1)
                        bv = ins[f"L2_xattn_bv{layer}"][cols]
                        sp.dma_start(value_bias[:, 1, :], bv.partition_broadcast(T2)).then_inc(bias_loaded, 16)
                        sp.dma_start(value_bias[1:T2, 0, :], bv.partition_broadcast(T2 - 1)).then_inc(bias_loaded, 16)
                        bias_v = ins[f"L2_xattn_bias_v{layer}"].rearrange("a b h d -> (a b) (h d)")
                        sp.dma_start(value_bias[0:1, 0, :], bias_v[:, cols]).then_inc(bias_loaded, 16)

        @block.gpsimd
        def _(pool):
            k.sems.clear_ended(pool)
            for s in range(2):
                for part in (cT[s].hi, cT[s].lo):
                    pool.memset(part[:].bitcast(F32), 0.0)
            for i in range(4):
                last = pool.memset(probs[i][:, N2 - 1:N2], 0.0)
            last.then_inc(zeroed, 1)
            pool.wait_ge(zeroed, 1)
            with pool.Fori(0, N_GROUPS) as group:
                with pool.Fori(0, HALVES) as half:
                    r = HALVES * group + half
                    for c in range(QUAD):
                        if c >= 2:
                            wait_done(pool, r, "k", c - 2, G2 - 1)
                        else:
                            wait_done(pool, r - 1, "k", c + 2, G2 - 1)
                        for part in ("hi", "lo"):
                            dst = cT[c % 2].hi if part == "hi" else cT[c % 2].lo
                            src = k.ctxT[part][bass.ds(QUAD * half + c, 1)].rearrange("b p k s -> (b p) k s")
                            pool.dma_start(dst[:, :, 1:1 + S], src).then_inc(cT_loaded[c % 2], 16)

        @block.tensor
        def _(pe):
            pe.sem_inc(tile_done, 2 * TILES2)
            for done in (scored, turned, attended):
                pe.sem_inc(done, 2 * UNITS)
            with pe.Fori(0, N_GROUPS) as group:
                with pe.Fori(0, HALVES) as half:
                    r = HALVES * group + half

                    def start_tile(*tile):
                        wait_copied(pe, r, ROUND_TILES.index(tile) - len(work))
                        return bank(*tile)

                    def wait_weight(n, t):
                        pe.wait_ge(w_split, 4 * KT * (group + 1) + KT * WEIGHTS2.index(n) + t + 1)

                    def keys(c, j):
                        out = start_tile("k", c, j)
                        if j == 0:
                            pe.wait_ge(cT_loaded[c % 2], 64 * r + 32 * (c // 2 + 1))
                        for t in range(KT):
                            if c == 0 and j == 0:
                                wait_weight("wk", t)
                            mm = product(pe, out[:, 0:KEYS2], weights["wk"], cT[c % 2],
                                         lambda x: x[:, t, j * P:(j + 1) * P], lambda x: x[:, t, 0:KEYS2],
                                         start=(t == 0), stop=(t == KT - 1))
                        mm.then_inc(tile_done, 1)

                    def value_tile(c, j):
                        out = start_tile("v", c, j)
                        for t in range(KT):
                            if c == 0 and j == 0:
                                wait_weight("wv", t)
                            mm = product(pe, out[0:T2, :], cT[c % 2], weights["wv"],
                                         lambda x: x[:, t, j * T2:(j + 1) * T2], lambda x: x[:, t, :],
                                         start=(t == 0), stop=(t == KT - 1))
                        mm.then_inc(tile_done, 1)

                    def scores(x):
                        c, j = unit_of(x)
                        wait_tile(pe, r, "k", c, j)
                        if x < G2:
                            wait_tile(pe, r, "q", j)
                        if j == 0:
                            pe.wait_ge(key_placed, at(r, QUAD, c))
                        pe.wait_ge(exped, at(r, UNITS, x - 2))
                        pe.matmul(ps_scores[x % 2][0:L, 0:KEYS2], qT[:, j, c * L:(c + 1) * L], keysT[c % 2][:, j, :],
                                  start=True, stop=True).then_inc(scored, 1)

                    def turn(x):
                        pe.wait_ge(scaled, at(r, UNITS, x))
                        pe.wait_ge(turned_copied, at(r, UNITS, x - 2))
                        for n in range(NT2):
                            mm = pe.transpose(ps_turned[x % 2][0:T2, n * L:(n + 1) * L],
                                              probs[x % 4][:, n * T2:(n + 1) * T2], k.ident[0:L, 0:L])
                        mm.then_inc(turned, 1)

                    def attend(x):
                        c, j = unit_of(x)
                        if j == 0:
                            wait_tile(pe, r, "v", c, NT2 - 1)
                            pe.wait_ge(o_split, at(r, QUAD, c - 1))
                        pe.wait_ge(turned_copied, at(r, UNITS, x))
                        for n in range(NT2):
                            mm = pe.matmul(ps_o[:, j * L:(j + 1) * L], values[c % 2][:, n, j * P:(j + 1) * P],
                                           probsT[x % 2][:, n, :], start=(n == 0), stop=(n == NT2 - 1))
                        mm.then_inc(attended, 1)

                    def project(c):
                        out = start_tile("out", c)
                        pe.wait_ge(o_split, at(r, QUAD, c))
                        for j in range(G2):
                            if c == 0:
                                wait_weight("wo", j)
                            mm = product(pe, out[0:L, :], oT, weights["wo"],
                                         lambda x: x[:, c, j * L:(j + 1) * L], lambda x: x[:, j, :],
                                         start=(j == 0), stop=(j == G2 - 1))
                        mm.then_inc(tile_done, 1)

                    for j in range(G2):
                        out = start_tile("q", j)
                        for t in range(KT):
                            if j == 0:
                                wait_weight("wq", t)
                            mm = product(pe, out[:, 0:HALF], weights["wq"], hT,
                                         lambda x: x[:, t, j * P:(j + 1) * P],
                                         lambda x: x[:, t, bass.ds(half * HALF, HALF)],
                                         start=(t == 0), stop=(t == KT - 1))
                        mm.then_inc(tile_done, 1)
                    for j in range(G2):
                        keys(0, j)
                        if j < NT2:
                            value_tile(0, j)
                    for x in range(UNITS + 1):
                        c, j = unit_of(x)
                        if x < UNITS:
                            scores(x)
                        if c + 1 < QUAD:
                            keys(c + 1, j)
                        if x > 0:
                            turn(x - 1)
                        if c + 1 < QUAD and j < NT2:
                            value_tile(c + 1, j)
                        if c == QUAD - 1 and j > 0:
                            project(j - 1)
                        if x > 0:
                            attend(x - 1)
                    project(QUAD - 1)

        @block.scalar
        def _(act):
            act.sem_inc(w_rounded, 4 * KT)
            act.sem_inc(act_copied, 2 * len(ACT_TILES2))
            act.sem_inc(key_placed, 2 * QUAD)
            act.sem_inc(exped, 2 * UNITS)
            act.sem_inc(turned_copied, 2 * UNITS)
            act.sem_inc(o_rounded, 2 * QUAD)
            act.wait_ge(biased, 1)
            with act.Fori(0, N_GROUPS) as group:
                wait_group_before(act, group)
                tile, first, _ = PARAM_AT[f"L2_xattn_bq{layer}"]
                act.activation(group_key_bias[:], key_bias[:, bass.ds(group * G2, G2)], ACT.Copy)
                act.activation(group_q_bias[:], k.params[:, tile, bass.ds(group * G2 + first, G2)], ACT.Copy
                               ).then_inc(grouped, 1)
                for m, n in enumerate(WEIGHTS2):
                    act.wait_ge(w_loaded[n], 16 * (group + 1))
                    for t in range(KT):
                        weights[n].round(act, lambda x: x[:, t, :], staged[m % 2][:, t, :]).then_inc(w_rounded, 1)
                with act.Fori(0, HALVES) as half:
                    r = HALVES * group + half

                    def copy_key(c, j):
                        wait_done(act, r, "k", c, j)
                        act.activation(keysT[c % 2][:, j, 1:KEYS2], bank("k", c, j)[:, 1:KEYS2], ACT.Copy
                                       ).then_inc(act_copied, 1)
                        if j == 0:
                            act.wait_ge(grouped, group + 1)
                            act.activation(keysT[c % 2][:, :, 0], group_key_bias[:], ACT.Copy).then_inc(key_placed, 1)

                    def round_output(c):
                        act.wait_ge(attended, at(r, UNITS, c * G2 + G2 - 1))
                        oT.round(act, lambda x: x[:, c, :], ps_o[:, 0:G2 * L]).then_inc(o_rounded, 1)

                    for j in range(G2):
                        copy_key(0, j)
                    for x in range(UNITS + 1):
                        c, j = unit_of(x)
                        if x < UNITS:
                            act.wait_ge(maxed, at(r, UNITS, x))
                            act.wait_ge(turned, at(r, UNITS, x - 4))
                            act.activation(probs[x % 4][:, 0:KEYS2], ps_scores[x % 2][0:L, 0:KEYS2], ACT.Exp,
                                           bias=neg_max[:, x:x + 1], accum_out=sums[:, x:x + 1]).then_inc(exped, 1)
                        if c + 1 < QUAD:
                            copy_key(c + 1, j)
                        if x > 0:
                            act.wait_ge(turned, at(r, UNITS, x - 1))
                            act.activation(probsT[(x - 1) % 2][:].rearrange("p n l -> p (n l)"),
                                           ps_turned[(x - 1) % 2][0:T2, 0:NT2 * L], ACT.Copy).then_inc(turned_copied, 1)
                            if x % G2 == 0:
                                round_output(x // G2 - 1)

        @block.vector
        def _(dve):
            dve.sem_inc(w_split, 4 * KT)
            dve.sem_inc(dve_copied, 2 * len(DVE_TILES2))
            for done in (maxed, inverted, scaled):
                dve.sem_inc(done, 2 * UNITS)
            dve.sem_inc(o_split, 2 * QUAD)
            dve.tensor_tensor(key_bias[:], column(k, f"L2_xattn_bias_k{layer}", 0, H2),
                              column(k, f"L2_xattn_bk{layer}", 0, H2), ALU.subtract).then_inc(biased, 1)
            with dve.Fori(0, N_GROUPS) as group:
                wait_group_before(dve, group)
                for m, n in enumerate(WEIGHTS2):
                    for t in range(KT):
                        dve.wait_ge(w_rounded, 4 * KT * (group + 1) + KT * m + t + 1)
                        weights[n].rest(dve, lambda x: x[:, t, :], staged[m % 2][:, t, :]).then_inc(w_split, 1)
                with dve.Fori(0, HALVES) as half:
                    r = HALVES * group + half

                    def copy_values(c, j):
                        wait_done(dve, r, "v", c, j)
                        if c == 0 and j == 0:
                            dve.wait_ge(bias_loaded, 48 * (group + 1))
                        if j == 0:
                            dve.wait_ge(attended, at(r, UNITS, G2 * (c - 1) - 1))
                        dve.tensor_tensor(values[c % 2][:, j, :], bank("v", c, j)[0:T2, :],
                                          value_bias[:, min(j, 1), :], ALU.add).then_inc(dve_copied, 1)

                    def copy_output(c):
                        wait_done(dve, r, "out", c)
                        x = k.X[:, bass.ds(QUAD * half + c, 1), :].squeeze(1)
                        dve.tensor_tensor(x, x, bank("out", c)[0:L, :], ALU.add).then_inc(dve_copied, 1)

                    dve.wait_ge(grouped, group + 1)
                    for j in range(G2):
                        wait_done(dve, r, "q", j)
                        dve.tensor_scalar(qT[:, j, :], bank("q", j)[:, 0:HALF], group_q_bias[:, j:j + 1],
                                          DH2 ** -0.5, ALU.add, ALU.mult).then_inc(dve_copied, 1)
                    for j in range(NT2):
                        copy_values(0, j)
                    for x in range(UNITS + 1):
                        c, j = unit_of(x)
                        if x < UNITS:
                            dve.wait_ge(scored, at(r, UNITS, x))
                            dve.tensor_reduce(neg_max[:, x:x + 1], ps_scores[x % 2][0:L, 0:KEYS2], AX.X, ALU.max,
                                              negate=True).then_inc(maxed, 1)
                            dve.wait_ge(exped, at(r, UNITS, x))
                            dve.reciprocal(inverse[:, x:x + 1], sums[:, x:x + 1]).then_inc(inverted, 1)
                            dve.wait_ge(inverted, at(r, UNITS, x))
                            p = probs[x % 4][:, 0:KEYS2]
                            dve.tensor_scalar(p, p, inverse[:, x:x + 1], None, ALU.mult).then_inc(scaled, 1)
                        if x > 0 and x % G2 == 0:
                            dve.wait_ge(o_rounded, at(r, QUAD, x // G2 - 1))
                            oT.rest(dve, lambda y: y[:, x // G2 - 1, :], ps_o[:, 0:G2 * L]).then_inc(o_split, 1)
                        if c + 1 < QUAD and j < NT2:
                            copy_values(c + 1, j)
                        if c == QUAD - 1 and j > 0:
                            copy_output(j - 1)
                    copy_output(QUAD - 1)


def layer2(nc, k, ins, ctx):
    for layer in (1, 2):
        with ExitStack() as own:
            hT = Split(own, nc, f"l2_hT{layer}", [P, KT, B * L])
            with ExitStack() as inner:
                whole = inner.enter_context(nc.sbuf_tensor(f"l2_whole{layer}", [P, KT, B * L], F32))
                norm_features(nc, k, ctx, f"l2ln{layer}", whole,
                              f"L2_xattn_ln{layer}_scale", f"L2_xattn_ln{layer}_offset", 1e-5, split=hT,
                              add_row=ins[f"L2_xattn_bo{layer}"])
            layer2_attention(nc, k, ins, ctx, layer, hT)
    with ExitStack() as own:
        hT = Split(own, nc, "l2_hTm", [P, KT, B * L])
        with ExitStack() as inner:
            whole = inner.enter_context(nc.sbuf_tensor("l2_whole_m", [P, KT, B * L], F32))
            norm_features(nc, k, ctx, "l2lnm", whole, "L2_xattn_ln_mlp_scale", "L2_xattn_ln_mlp_offset", 1e-5,
                          split=hT, add_row=ins["L2_xattn_b_fc2"])
        mlp(nc, k, ctx, "l2mlp", hT, ins["L2_xattn_w_fc1"], ins["L2_xattn_w_fc2"], "L2_xattn_b_fc1", ACT.Gelu)


H3, KV3, Q3, DH3 = 32, 8, 4, 16
T3, NT3 = 121, 3
N3 = T3 * NT3


def layer3_queries(nc, k, ins, ctx, queries):
    with ExitStack() as own:
        own.callback(k.sems.end_phase)
        Wq = own.enter_context(nc.sbuf_tensor("Wq3", [P, KT, D], F32))
        Wq_grouped = own.enter_context(nc.sbuf_tensor("Wq3_grouped", [P, KT, Q3, P], F32))
        xT = own.enter_context(nc.sbuf_tensor("xT3", [P, KT, B * L], F32))
        tiles = Tiles(k, "l3q", psum_banks(nc, own, "l3q_ps", 8),
                      [("xT", 2 * KT, "ad"), ("q", HALVES * Q3, "da")])
        loaded = k.sems.take("l3q_loaded")
        grouped = k.sems.take("l3q_grouped")
        block = own.enter_context(nc.Block())

        @block.sync
        def _(sp):
            load_features(sp, Wq, ins["L3_xattn_Wq"], loaded)

        @block.gpsimd
        def _(pool):
            k.sems.clear_ended(pool)

        @block.tensor
        def _(pe):
            turn_tokens(pe, k, tiles, "xT", k.X, lambda b: None)
            pe.wait_ge(grouped, KT)
            for half in range(HALVES):
                tiles.wait_out(pe, "xT", range(half * KT, (half + 1) * KT))
                for g in range(Q3):
                    j = half * Q3 + g
                    tiles.wait_free(pe, "q", j)
                    for t in range(KT):
                        mm = pe.matmul(tiles.bank("q", j)[:, 0:HALF], Wq_grouped[:, t, g, :], half_tokens(xT, t, half),
                                       start=(t == 0), stop=(t == KT - 1))
                    mm.then_inc(tiles.filled, 1)

        @block.scalar
        def _(act):
            for j in tiles.mine("a", "xT"):
                tiles.wait_filled(act, "xT", j)
                act.activation(half_tokens(xT, j % KT, j // KT), tiles.bank("xT", j)[:, 0:HALF], ACT.Copy
                               ).then_inc(tiles.emptied["a"], 1)
            for j in tiles.mine("a", "q"):
                tiles.wait_filled(act, "q", j)
                act.activation(half_tokens(queries, j % Q3, j // Q3), tiles.bank("q", j)[:, 0:HALF], ACT.Identity,
                               bias=column(k, "L3_xattn_bq", j % Q3)).then_inc(tiles.emptied["a"], 1)

        @block.vector
        def _(dve):
            for j in tiles.mine("d", "xT"):
                tiles.wait_filled(dve, "xT", j)
                dve.tensor_copy(half_tokens(xT, j % KT, j // KT), tiles.bank("xT", j)[:, 0:HALF]
                                ).then_inc(tiles.emptied["d"], 1)
            dve.wait_ge(loaded, 16)
            for t in range(KT):
                dve.tensor_copy(Wq_grouped[:, t].rearrange("p g (v d) -> p g v d", v=KV3),
                                Wq[:, t, :].rearrange("p (v g d) -> p g v d", v=KV3, g=Q3)).then_inc(grouped, 1)
            for j in tiles.mine("d", "q"):
                tiles.wait_filled(dve, "q", j)
                dve.tensor_scalar(half_tokens(queries, j % Q3, j // Q3), tiles.bank("q", j)[:, 0:HALF],
                                  column(k, "L3_xattn_bq", j % Q3), None, ALU.add).then_inc(tiles.emptied["d"], 1)


def layer3_attention(nc, k, ins, ctx, queries):
    with ExitStack() as own:
        own.callback(k.sems.end_phase)
        def sb(name, shape):
            return own.enter_context(nc.sbuf_tensor(name, shape, F32))

        def sem(name):
            return k.sems.take(name)

        Wk = sb("Wk3", [P, KT, P])
        Wv = sb("Wv3", [P, KT, P])
        v_bias = sb("v_bias3", [P, P])
        head_rows = sb("head_rows", [P, KV3])
        cT = [sb(f"cT3_{s}", [P, KT, N3]) for s in range(2)]
        cT_parts = [sb(f"cT3_{part}", [P, KT, S]) for part in ("hi", "lo")]
        mask_add = [sb(f"mask3_{s}", [L, N3]) for s in range(2)]
        q_heads = [sb(f"q_heads3_{s}", [P, Q3, KV3, L]) for s in range(2)]
        keysT = sb("keysT3", [P, N3])
        values = sb("values3", [T3, NT3, P])
        probs = [sb(f"probs3_{i}", [L, N3]) for i in range(4)]
        probsT = [sb(f"probsT3_{i}", [T3, NT3, L]) for i in range(2)]
        neg_max = sb("neg_max3", [L, H3])
        sums = [sb(f"sums3_{s}", [L, H3]) for s in range(2)]
        rsum = sb("rsum3", [L, H3])
        work = psum_banks(nc, own, "work3_", 2)
        ps_scores = psum_banks(nc, own, "scores3_", 2)
        ps_turned = psum_banks(nc, own, "turned3_", 2)
        ps_att = own.enter_context(nc.psum_tensor("ps_att3", [P, H3, DH3], F32))

        loaded = sem("loaded3")
        padded = sem("padded3")
        rows_ready = sem("head_rows_ready")
        cT_loaded = sem("cT3_loaded")
        cT_summed = sem("cT3_summed")
        mask_loaded = [sem(f"mask3_loaded{s}") for s in range(2)]
        projected = sem("projected3")
        keys_copied = sem("keys_copied3")
        values_copied = sem("values_copied3")
        headed = sem("headed3")
        scored = sem("scored3")
        shifted = sem("shifted3")
        maxed = sem("maxed3")
        exped = sem("exped3")
        turned = sem("turned3")
        turned_copied = {"a": sem("turned_act3"), "d": sem("turned_dve3")}
        attended = sem("attended3")
        inverted = sem("inverted3")
        att_copied = sem("att_copied3")

        def wait_turned(eng, b, h):
            eng.wait_ge(turned_copied["ad"[h % 2]], at(b, H3 // 2, h // 2))

        def copy_turned(eng, engine, b, h):
            eng.wait_ge(turned, at(b, H3, h))
            eng.wait_ge(attended, at(b, H3, h - 2))
            dst = probsT[h % 2][:].rearrange("p j l -> p (j l)")
            src = ps_turned[h % 2][0:T3, 0:NT3 * L]
            ins_ = eng.activation(dst, src, ACT.Copy) if engine == "a" else eng.tensor_copy(dst, src)
            ins_.then_inc(turned_copied[engine], 1)

        block = own.enter_context(nc.Block())

        @block.sync
        def _(sp):
            load_features(sp, Wk, ins["L3_xattn_Wk"], loaded)
            load_features(sp, Wv, ins["L3_xattn_Wv"], loaded)
            sp.dma_start(v_bias[:], ins["L3_xattn_bv"].partition_broadcast(P)).then_inc(loaded, 16)
            sp.wait_ge(padded, 1)
            with sp.Fori(0, B // 2) as i:
                for s in range(2):
                    b = 2 * i + s
                    sp.wait_ge(cT_summed, at(b, 1, 0, back=1))
                    for dst, part in zip(cT_parts, ("hi", "lo")):
                        sp.dma_start(dst[:], k.ctxT[part][bass.ds(b, 1)].rearrange("b p k s -> (b p) k s").bitcast(F32)
                                     ).then_inc(cT_loaded, 16)
                    sp.wait_ge(shifted, at(b, H3, H3 - 1, back=2))
                    sp.dma_start(mask_add[s][:, 0:S], ins["mask_Bx1xSxS2_ff0"][b, 0]).then_inc(mask_loaded[s], 16)

        @block.gpsimd
        def _(pool):
            k.sems.clear_ended(pool)
            for s in range(2):
                pool.memset(cT[s][:, :, S:N3], 0.0)
                last = pool.memset(mask_add[s][:, S:N3], MASKED)
            last.then_inc(padded, 1)
            pool.sem_inc(headed, 2 * Q3)
            pool.sem_inc(cT_summed, 2)
            pool.wait_ge(rows_ready, 1)
            with pool.Fori(0, B // 2) as i:
                for s in range(2):
                    b = 2 * i + s
                    pool.wait_ge(cT_loaded, 32 * (b + 1))
                    pool.wait_ge(projected, at(b, 2, 1, back=2))
                    pool.tensor_tensor(cT[s][:, :, 0:S], cT_parts[0][:], cT_parts[1][:], ALU.add).then_inc(cT_summed, 1)
                    pool.wait_ge(scored, at(b, H3, H3 - 1, back=2))
                    for g in range(Q3):
                        pool.tensor_tensor(
                            q_heads[s][:, g], queries[:, g, bass.ds(b * L, L)].unsqueeze(1).broadcast_to([P, KV3, L]),
                            head_rows[:].unsqueeze(2).broadcast_to([P, KV3, L]), ALU.mult).then_inc(headed, 1)

        @block.tensor
        def _(pe):
            pe.sem_inc(projected, 4)
            for done in (scored, turned, attended):
                pe.sem_inc(done, 2 * H3)
            pe.wait_ge(loaded, 48)
            with pe.Fori(0, B // 2) as i:
                for s in range(2):
                    b = 2 * i + s
                    pe.wait_ge(cT_summed, at(b, 1, 0))
                    pe.wait_ge(keys_copied, at(b, 1, 0, back=1))
                    for t in range(KT):
                        mm = pe.matmul(work[0][:, 0:N3], Wk[:, t, :], cT[s][:, t, :], start=(t == 0), stop=(t == KT - 1))
                    mm.then_inc(projected, 1)
                    pe.wait_ge(values_copied, at(b, 1, 0, back=1))
                    for j in range(NT3):
                        for t in range(KT):
                            mm = pe.matmul(work[1][0:T3, j * P:(j + 1) * P], cT[s][:, t, j * T3:(j + 1) * T3], Wv[:, t, :],
                                           start=(t == 0), stop=(t == KT - 1))
                    mm.then_inc(projected, 1)

                    def scores(h):
                        v, g = divmod(h, Q3)
                        if h == 0:
                            pe.wait_ge(keys_copied, at(b, 1, 0))
                            pe.wait_ge(headed, at(b, Q3, Q3 - 1))
                        pe.wait_ge(shifted, at(b, H3, h - 2))
                        pe.matmul(ps_scores[h % 2][0:L, 0:N3], q_heads[s][:, g, v, :], keysT[:], start=True, stop=True
                                  ).then_inc(scored, 1)

                    def turn(h):
                        pe.wait_ge(exped, at(b, H3, h))
                        wait_turned(pe, b, h - 2)
                        for j in range(NT3):
                            mm = pe.transpose(ps_turned[h % 2][0:T3, j * L:(j + 1) * L],
                                              probs[h % 4][:, j * T3:(j + 1) * T3], k.ident[0:L, 0:L])
                        mm.then_inc(turned, 1)

                    def attend(h):
                        v = h // Q3
                        if h == 0:
                            pe.wait_ge(values_copied, at(b, 1, 0))
                            pe.wait_ge(att_copied, at(b, 1, 0, back=1))
                        wait_turned(pe, b, h)
                        for j in range(NT3):
                            mm = pe.matmul(ps_att[0:L, h, :], probsT[h % 2][:, j, :],
                                           values[:, j, v * DH3:(v + 1) * DH3], start=(j == 0), stop=(j == NT3 - 1))
                        mm.then_inc(attended, 1)

                    for step in range(H3 + 3):
                        if step < H3:
                            scores(step)
                        if 0 <= step - 2 < H3:
                            turn(step - 2)
                        if 0 <= step - 3 < H3:
                            attend(step - 3)

        @block.scalar
        def _(act):
            act.sem_inc(keys_copied, 2)
            act.sem_inc(exped, 2 * H3)
            act.sem_inc(turned_copied["a"], H3)
            with act.Fori(0, B // 2) as i:
                for s in range(2):
                    b = 2 * i + s
                    act.wait_ge(projected, at(b, 2, 0))
                    act.activation(keysT[:], work[0][:, 0:N3], ACT.Identity, bias=column(k, "L3_xattn_bk")
                                   ).then_inc(keys_copied, 1)
                    for h in range(H3 + 1):
                        if h < H3:
                            act.wait_ge(maxed, at(b, H3, h))
                            act.activation(probs[h % 4][:], probs[h % 4][:], ACT.Exp, bias=neg_max[:, h:h + 1],
                                           accum_out=sums[s][:, h:h + 1]).then_inc(exped, 1)
                        if h >= 1 and h % 2 == 1:
                            copy_turned(act, "a", b, h - 1)

        @block.vector
        def _(dve):
            dve.tensor_scalar(head_rows[:], k.head_of[:], DH3 ** -0.5, None, ALU.mult).then_inc(rows_ready, 1)
            dve.sem_inc(values_copied, 2)
            dve.sem_inc(shifted, 2 * H3)
            dve.sem_inc(maxed, 2 * H3)
            dve.sem_inc(turned_copied["d"], H3)
            dve.sem_inc(inverted, 2)
            dve.sem_inc(att_copied, 2)
            dve.wait_ge(loaded, 48)
            with dve.Fori(0, B // 2) as i:
                for s in range(2):
                    b = 2 * i + s
                    dve.wait_ge(projected, at(b, 2, 1))
                    dve.tensor_tensor(values[:], work[1][0:T3, 0:NT3 * P].rearrange("p (j d) -> p j d", j=NT3),
                                      v_bias[0:T3, :].unsqueeze(1).broadcast_to([T3, NT3, P]), ALU.add
                                      ).then_inc(values_copied, 1)
                    dve.wait_ge(mask_loaded[s], 16 * (i + 1))
                    for h in range(H3 + 2):
                        if h < H3:
                            dve.wait_ge(scored, at(b, H3, h))
                            dve.wait_ge(turned, at(b, H3, h - 4))
                            dve.tensor_tensor(probs[h % 4][:], ps_scores[h % 2][0:L, 0:N3], mask_add[s][:], ALU.add
                                              ).then_inc(shifted, 1)
                            dve.wait_ge(shifted, at(b, H3, h))
                            dve.tensor_reduce(neg_max[:, h:h + 1], probs[h % 4][:], AX.X, ALU.max, negate=True
                                              ).then_inc(maxed, 1)
                        if h >= 2 and (h - 1) % 2 == 1:
                            copy_turned(dve, "d", b, h - 1) if h - 1 < H3 else None
                    dve.wait_ge(exped, at(b, H3, H3 - 1))
                    dve.reciprocal(rsum[:], sums[s][:]).then_inc(inverted, 1)
                    dve.wait_ge(inverted, at(b, 1, 0))
                    dve.wait_ge(attended, at(b, H3, H3 - 1))
                    dve.tensor_tensor(
                        k.ATT[:, bass.ds(b, 1), :].squeeze(1).rearrange("l (h d) -> l h d", h=H3), ps_att[0:L, :, :],
                        rsum[:].unsqueeze(2).broadcast_to([L, H3, DH3]), ALU.mult).then_inc(att_copied, 1)


def layer3_output(nc, k, ins, ctx, out):
    with ExitStack() as own:
        own.callback(k.sems.end_phase)
        def sb(name, shape):
            return own.enter_context(nc.sbuf_tensor(name, shape, F32))

        def sem(name):
            return k.sems.take(name)

        Wo = sb("Wo3", [P, KT, D])
        rows = {n: sb(f"{n}_row3", [L, D]) for n in ("bo", "gamma", "beta")}
        attT = sb("attT3", [P, KT, B * L])
        Y = sb("Y3", [L, B, D])
        stats = norm_stats(nc, own, "l3n")
        n0 = k.norms
        k.norms += HALVES
        tiles = Tiles(k, "l3o", psum_banks(nc, own, "l3o_ps", 8), [("attT", 2 * KT, "ad"), ("out", B, "d")])
        loaded = sem("l3o_loaded")
        residual = sem("l3o_residual")
        scaled = sem("l3o_scaled")
        offset = sem("l3o_offset")
        stored = sem("l3o_stored")
        block = own.enter_context(nc.Block())

        @block.sync
        def _(sp):
            load_features(sp, Wo, ins["L3_xattn_Wo"], loaded)
            for n, row in rows.items():
                sp.dma_start(row[:], ins[f"L3_xattn_{n}"].partition_broadcast(L)).then_inc(loaded, 16)
            for b in range(B):
                sp.wait_ge(offset, b + 1)
                sp.dma_start(out[b], Y[:, b, :]).then_inc(stored, 16)
            sp.wait_ge(stored, 16 * B)

        @block.tensor
        def _(pe):
            turn_tokens(pe, k, tiles, "attT", k.ATT, lambda b: None)
            pe.wait_ge(loaded, 64)
            project_tokens(pe, tiles, "out", attT, Wo, KT,
                           lambda b: tiles.wait_out(pe, "attT", range((b // 4) * KT, (b // 4 + 1) * KT)))

        @block.scalar
        def _(act):
            for j in tiles.mine("a", "attT"):
                tiles.wait_filled(act, "attT", j)
                act.activation(half_tokens(attT, j % KT, j // KT), tiles.bank("attT", j)[:, 0:HALF], ACT.Copy
                               ).then_inc(tiles.emptied["a"], 1)

        @block.gpsimd
        def _(pool):
            k.sems.clear_ended(pool)
            pool.wait_ge(loaded, 64)
            for b in range(B):
                pool.tensor_tensor(Y[:, b, :], k.X[:, b, :], rows["bo"][:], ALU.add).then_inc(residual, 1)
            for half in range(HALVES):
                invert_half_pool(pool, k, stats, half, n0 + half)
                for c in range(4):
                    b = 4 * half + c
                    pool.wait_ge(scaled, b + 1)
                    pool.tensor_tensor(Y[:, b, :], Y[:, b, :], rows["beta"][:], ALU.add).then_inc(offset, 1)

        @block.vector
        def _(dve):
            for j in tiles.mine("d", "attT"):
                tiles.wait_filled(dve, "attT", j)
                dve.tensor_copy(half_tokens(attT, j % KT, j // KT), tiles.bank("attT", j)[:, 0:HALF]
                                ).then_inc(tiles.emptied["d"], 1)
            for half in range(HALVES):
                for c in range(4):
                    b = 4 * half + c
                    tiles.wait_filled(dve, "out", b)
                    dve.wait_ge(residual, b + 1)
                    dve.tensor_tensor(Y[:, b, :], Y[:, b, :], tiles.bank("out", b)[0:L, :], ALU.add
                                      ).then_inc(tiles.emptied["d"], 1)
                tiles.wait_out(dve, "out", [4 * half + 3])
                norm_half_dve(dve, k, Y, Y, stats, 1e-6, half, n0 + half)
                for c in range(4):
                    b = 4 * half + c
                    dve.wait_ge(k.stat_sem["normed"], 4 * n0 + b + 1)
                    dve.tensor_tensor(Y[:, b, :], Y[:, b, :], rows["gamma"][:], ALU.mult).then_inc(scaled, 1)


def layer3(nc, k, ins, ctx, out):
    with ExitStack() as own:
        k.ATT = own.enter_context(nc.sbuf_tensor("ATT3", [L, B, D], F32))
        with ExitStack() as inner:
            queries = inner.enter_context(nc.sbuf_tensor("queries3", [P, Q3, B * L], F32))
            layer3_queries(nc, k, ins, ctx, queries)
            layer3_attention(nc, k, ins, ctx, queries)
        layer3_output(nc, k, ins, ctx, out)


def program(nc, ins, out):
    k = Shared()
    k.sems = Semaphores(nc)
    with ExitStack() as ctx:
        setup(nc, k, ins, ctx)
        statistics_semaphores(nc, k, ctx)
        with ExitStack() as own:
            hT = Split(own, nc, "l0_hT", [P, KT, B * L])
            with ExitStack() as inner:
                k.ATT = inner.enter_context(nc.sbuf_tensor("ATT", [L, B, D], F32))
                layer0_attention(nc, k, ins, ctx)
                layer0_output(nc, k, ins, ctx, hT)
            mlp(nc, k, ctx, "l0mlp", hT, ins["L0_xattn_mlp_w1"], ins["L0_xattn_mlp_w2"], "L0_xattn_mlp_b1",
                ACT.Gelu_apprx_tanh)
        layer1(nc, k, ins, ctx)
        layer2(nc, k, ins, ctx)
        layer3(nc, k, ins, ctx, out)


def kernel(**inputs):
    import numpy as _np
    import concourse.bacc as _bacc
    from concourse import mybir as _mybir
    from concourse.bass_utils import run_bass_kernel_spmd as _run

    nc = _bacc.Bacc("TRN2", target_bir_lowering=False, num_devices=1)
    arrays, ins = {}, {}
    for name, value in inputs.items():
        a = _np.ascontiguousarray(value)
        arrays[f"in_{name}_dram"] = a
        ins[name] = nc.dram_tensor(f"in_{name}_dram", a.shape, _mybir.dt.from_np(a.dtype), kind="ExternalInput").ap()
    out = nc.dram_tensor("out_0_dram", (B, L, D), F32, kind="ExternalOutput").ap()
    program(nc, ins, out)
    r = _run(nc, [arrays], core_ids=[0])
    return r.results[0]["out_0_dram"]
```
